# Optimizing a Trainium2 kernel written in Bass

```python
import numpy as np
import jax
import jax.numpy as jnp

def _softmax(x, axis=-1):
    return jax.nn.softmax(x, axis=axis)

def _gelu(x):
    return jax.nn.gelu(x, approximate=True)

def _silu(x):
    return jax.nn.silu(x)

def _sigmoid(x):
    return jax.nn.sigmoid(x)

def _layernorm(x, axis=-1, eps=1e-05):
    m = jnp.mean(x, axis=axis, keepdims=True)
    v = jnp.var(x, axis=axis, keepdims=True)
    return (x - m) / jnp.sqrt(v + eps)

def _scatter_add(tgt, idx, src, axis=0):
    return tgt.at[idx].add(src)

def _segment_sum(src, seg, n):
    return jax.ops.segment_sum(src, seg, n)
kernel_name = 'mk_prb_d2_jaxref_r8_598f20'

def setup_inputs(seed: int=0):
    np.random.seed(seed)
    _w = jnp.asarray

    def _L0_attn_setup():
        import jax, jax.numpy as jnp
        import numpy as np
        HEADS = 16
        DIM_HEAD = 64
        SEG = 64
        P = 16

        def rmsnorm(x, g, eps=1e-06):
            var = jnp.mean(x * x, axis=-1, keepdims=True)
            return x * jax.lax.rsqrt(var + eps) * g
        key = jax.random.key(seed)
        ks = jax.random.split(key, 6)
        B, S, D = (2, 512, 128)
        inner = HEADS * DIM_HEAD
        return {'x': jax.random.normal(ks[0], (B, S, D), jnp.float32), 'gamma': jnp.ones((D,), jnp.float32), 'w_qkv': jax.random.normal(ks[1], (D, inner * 3), jnp.float32) * D ** (-0.5), 'w_out': jax.random.normal(ks[2], (inner, D), jnp.float32) * inner ** (-0.5), 'pm_k': jax.random.normal(ks[3], (HEADS, P, DIM_HEAD), jnp.float32) * 0.02, 'pm_v': jax.random.normal(ks[4], (HEADS, P, DIM_HEAD), jnp.float32) * 0.02}
    _L0_attn_in = _L0_attn_setup()

    def _L0_ffn_setup():
        import jax, jax.numpy as jnp
        import numpy as np
        import math
        GOLDEN_CENTER = 1.0 / math.e
        GOLDEN_LOWER = 0.5 - math.log(4.0 / 3.0)
        GOLDEN_UPPER = 0.5
        B, T, D = (4, 256, 128)
        E = 8
        I = 512 // (E // 2)

        def _routing_weights(x, Wr, temperature):
            inh = jax.nn.sigmoid(x @ Wr / temperature)
            in_zone = (inh >= GOLDEN_LOWER) & (inh <= GOLDEN_UPPER)
            dist = jnp.abs(inh - GOLDEN_CENTER)
            w = jnp.exp(-dist / 0.1) * in_zone.astype(x.dtype)
            wsum = w.sum(axis=-1, keepdims=True)
            no_expert = wsum < 1e-08
            fb = jnp.exp(-dist / 0.3)
            _, top2 = jax.lax.top_k(fb, 2)
            fb_mask = jax.nn.one_hot(top2, E, dtype=x.dtype).sum(axis=-2)
            fb_w = fb * fb_mask
            fb_w = fb_w / jnp.clip(fb_w.sum(axis=-1, keepdims=True), 1e-08)
            w = jnp.where(no_expert, fb_w, w)
            wsum = w.sum(axis=-1, keepdims=True)
            return w / jnp.clip(wsum, 1e-08)
        key = jax.random.key(seed)
        k = jax.random.split(key, 6)
        s_d = 1.0 / math.sqrt(D)
        s_i = 1.0 / math.sqrt(I)
        return {'x': jax.random.normal(k[0], (B, T, D), jnp.float32), 'Wg': jax.random.normal(k[1], (E, D, I), jnp.float32) * s_d, 'Wu': jax.random.normal(k[2], (E, D, I), jnp.float32) * s_d, 'Wd': jax.random.normal(k[3], (E, I, D), jnp.float32) * s_i, 'Wr': jax.random.normal(k[4], (D, E), jnp.float32) * s_d, 'temperature': jnp.ones((1,), jnp.float32)}
    _L0_ffn_in = _L0_ffn_setup()

    def _L1_attn_setup():
        import jax, jax.numpy as jnp
        import numpy as np
        N_HEADS = 16
        ROPE_THETA = 10000.0

        def _rope_tables(T, d, dtype=jnp.float32):
            inv = 1.0 / ROPE_THETA ** (jnp.arange(0, d, 2, dtype=dtype) / d)
            t = jnp.arange(T, dtype=dtype)
            freqs = jnp.outer(t, inv)
            return (jnp.cos(freqs), jnp.sin(freqs))

        def _apply_rope(x, cos, sin):
            x_even = x[..., ::2]
            x_odd = x[..., 1::2]
            cos = cos[None, None]
            sin = sin[None, None]
            rot_even = x_even * cos - x_odd * sin
            rot_odd = x_odd * cos + x_even * sin
            out = jnp.stack([rot_even, rot_odd], axis=-1)
            return out.reshape(x.shape)
        key = jax.random.key(seed)
        k1, k2, k3 = jax.random.split(key, 3)
        B, T, C = (1, 512, 128)
        x = jax.random.normal(k1, (B, T, C), dtype=jnp.float32)
        w_qkv = jax.random.normal(k2, (C, 3 * C), dtype=jnp.float32) * (1.0 / np.sqrt(C))
        w_out = jax.random.normal(k3, (C, C), dtype=jnp.float32) * (1.0 / np.sqrt(C))
        return {'x': x, 'w_qkv': w_qkv, 'w_out': w_out}
    _L1_attn_in = _L1_attn_setup()

    def _L1_ffn_setup():
        import jax, jax.numpy as jnp
        import numpy as np
        H = 128
        I = 128
        E = 8
        key = jax.random.key(seed)
        ks = jax.random.split(key, 8)
        s = 0.02
        x = jax.random.normal(ks[0], (4, 256, H), dtype=jnp.float32)
        Wg = jax.random.normal(ks[1], (H, E), dtype=jnp.float32) * s
        bg = jnp.zeros((E,), dtype=jnp.float32)
        W1 = jax.random.normal(ks[2], (E, H, I), dtype=jnp.float32) * s
        b1 = jnp.zeros((E, I), dtype=jnp.float32)
        W2 = jax.random.normal(ks[3], (E, I, H), dtype=jnp.float32) * s
        b2 = jnp.zeros((E, H), dtype=jnp.float32)
        return {'x': x, 'Wg': Wg, 'bg': bg, 'W1': W1, 'b1': b1, 'W2': W2, 'b2': b2}
    _L1_ffn_in = _L1_ffn_setup()
    _d = {'L0_attn_x': _L0_attn_in['x'], 'L0_attn_gamma': _L0_attn_in['gamma'], 'L0_attn_w_qkv': _L0_attn_in['w_qkv'], 'L0_attn_w_out': _L0_attn_in['w_out'], 'L0_attn_pm_k': _L0_attn_in['pm_k'], 'L0_attn_pm_v': _L0_attn_in['pm_v'], 'L0_ffn_Wg': _L0_ffn_in['Wg'], 'L0_ffn_Wu': _L0_ffn_in['Wu'], 'L0_ffn_Wd': _L0_ffn_in['Wd'], 'L0_ffn_Wr': _L0_ffn_in['Wr'], 'L0_ffn_temperature': _L0_ffn_in['temperature'], 'L1_attn_w_qkv': _L1_attn_in['w_qkv'], 'L1_attn_w_out': _L1_attn_in['w_out'], 'L1_ffn_Wg': _L1_ffn_in['Wg'], 'L1_ffn_bg': _L1_ffn_in['bg'], 'L1_ffn_W1': _L1_ffn_in['W1'], 'L1_ffn_b1': _L1_ffn_in['b1'], 'L1_ffn_W2': _L1_ffn_in['W2'], 'L1_ffn_b2': _L1_ffn_in['b2']}
    _x0 = _d['L0_attn_x']
    _d['L0_attn_x'] = jax.random.normal(jax.random.fold_in(jax.random.key(seed), 1), (8, 512, 128), dtype=_x0.dtype)
    del _x0
    return _d

def reference(L0_attn_x, L0_attn_gamma, L0_attn_w_qkv, L0_attn_w_out, L0_attn_pm_k, L0_attn_pm_v, L0_ffn_Wg, L0_ffn_Wu, L0_ffn_Wd, L0_ffn_Wr, L0_ffn_temperature, L1_attn_w_qkv, L1_attn_w_out, L1_ffn_Wg, L1_ffn_bg, L1_ffn_W1, L1_ffn_b1, L1_ffn_W2, L1_ffn_b2):

    def _L0_attn_ref(x, gamma, w_qkv, w_out, pm_k, pm_v):
        import jax, jax.numpy as jnp
        import numpy as np
        HEADS = 16
        DIM_HEAD = 64
        SEG = 64
        P = 16

        def rmsnorm(x, g, eps=1e-06):
            var = jnp.mean(x * x, axis=-1, keepdims=True)
            return x * jax.lax.rsqrt(var + eps) * g
        B, S, D = x.shape
        pad = -S % SEG
        Sp = S + pad
        nw = Sp // SEG
        h = rmsnorm(x, gamma)
        qkv = h @ w_qkv
        q, k, v = jnp.split(qkv, 3, axis=-1)

        def fold(t):
            t = jnp.pad(t, ((0, 0), (0, pad), (0, 0)))
            t = t.reshape(B, nw, SEG, HEADS, DIM_HEAD)
            return t.transpose(0, 1, 3, 2, 4)
        q, k, v = (fold(q), fold(k), fold(v))
        pmk = jnp.broadcast_to(pm_k, (B, nw, HEADS, P, DIM_HEAD))
        pmv = jnp.broadcast_to(pm_v, (B, nw, HEADS, P, DIM_HEAD))
        k = jnp.concatenate([pmk, k], axis=3)
        v = jnp.concatenate([pmv, v], axis=3)
        scale = DIM_HEAD ** (-0.5)
        sim = jnp.einsum('bwhid,bwhjd->bwhij', q, k) * scale
        qi = jnp.arange(SEG)[:, None]
        kj = jnp.arange(SEG + P)[None, :] - P
        mask = (kj < 0) | (qi >= kj)
        sim = jnp.where(mask, sim, -jnp.inf)
        attn = jax.nn.softmax(sim, axis=-1)
        out = jnp.einsum('bwhij,bwhjd->bwhid', attn, v)
        out = out.transpose(0, 1, 3, 2, 4).reshape(B, Sp, HEADS * DIM_HEAD)
        out = out[:, :S]
        return out @ w_out

    def _L0_ffn_ref(x, Wg, Wu, Wd, Wr, temperature):
        import jax, jax.numpy as jnp
        import numpy as np
        import math
        GOLDEN_CENTER = 1.0 / math.e
        GOLDEN_LOWER = 0.5 - math.log(4.0 / 3.0)
        GOLDEN_UPPER = 0.5
        B, T, D = (4, 256, 128)
        E = 8
        I = 512 // (E // 2)

        def _routing_weights(x, Wr, temperature):
            inh = jax.nn.sigmoid(x @ Wr / temperature)
            in_zone = (inh >= GOLDEN_LOWER) & (inh <= GOLDEN_UPPER)
            dist = jnp.abs(inh - GOLDEN_CENTER)
            w = jnp.exp(-dist / 0.1) * in_zone.astype(x.dtype)
            wsum = w.sum(axis=-1, keepdims=True)
            no_expert = wsum < 1e-08
            fb = jnp.exp(-dist / 0.3)
            _, top2 = jax.lax.top_k(fb, 2)
            fb_mask = jax.nn.one_hot(top2, E, dtype=x.dtype).sum(axis=-2)
            fb_w = fb * fb_mask
            fb_w = fb_w / jnp.clip(fb_w.sum(axis=-1, keepdims=True), 1e-08)
            w = jnp.where(no_expert, fb_w, w)
            wsum = w.sum(axis=-1, keepdims=True)
            return w / jnp.clip(wsum, 1e-08)
        weights = _routing_weights(x, Wr, temperature)
        gate = jnp.einsum('btd,edi->beti', x, Wg)
        up = jnp.einsum('btd,edi->beti', x, Wu)
        h = jax.nn.silu(gate) * up
        e_out = jnp.einsum('beti,eid->betd', h, Wd)
        out = jnp.einsum('bte,betd->btd', weights, e_out)
        return out

    def _L1_attn_ref(x, w_qkv, w_out):
        import jax, jax.numpy as jnp
        import numpy as np
        N_HEADS = 16
        ROPE_THETA = 10000.0

        def _rope_tables(T, d, dtype=jnp.float32):
            inv = 1.0 / ROPE_THETA ** (jnp.arange(0, d, 2, dtype=dtype) / d)
            t = jnp.arange(T, dtype=dtype)
            freqs = jnp.outer(t, inv)
            return (jnp.cos(freqs), jnp.sin(freqs))

        def _apply_rope(x, cos, sin):
            x_even = x[..., ::2]
            x_odd = x[..., 1::2]
            cos = cos[None, None]
            sin = sin[None, None]
            rot_even = x_even * cos - x_odd * sin
            rot_odd = x_odd * cos + x_even * sin
            out = jnp.stack([rot_even, rot_odd], axis=-1)
            return out.reshape(x.shape)
        B, T, C = x.shape
        H = N_HEADS
        D = C // H
        qkv = x @ w_qkv
        q, k, v = jnp.split(qkv, 3, axis=-1)
        to_heads = lambda t_: t_.reshape(B, T, H, D).transpose(0, 2, 1, 3)
        q, k, v = (to_heads(q), to_heads(k), to_heads(v))
        cos, sin = _rope_tables(T, D, x.dtype)
        q = _apply_rope(q, cos, sin)
        k = _apply_rope(k, cos, sin)
        scale = 1.0 / np.sqrt(D)
        att = jnp.einsum('bhtd,bhsd->bhts', q, k) * scale
        causal_mask = jnp.triu(jnp.ones((T, T), dtype=bool), 1)
        att = jnp.where(causal_mask[None, None], -jnp.inf, att)
        att = jax.nn.softmax(att, axis=-1)
        o = jnp.einsum('bhts,bhsd->bhtd', att, v)
        o = o.transpose(0, 2, 1, 3).reshape(B, T, C)
        return o @ w_out

    def _L1_ffn_ref(x, Wg, bg, W1, b1, W2, b2):
        import jax, jax.numpy as jnp
        import numpy as np
        H = 128
        I = 128
        E = 8
        B, S, Hd = x.shape
        xf = x.reshape(-1, Hd)
        logits = xf @ Wg + bg
        gates = jax.nn.softmax(logits, axis=-1)
        idx = jnp.argmax(gates, axis=-1)
        h = jax.nn.gelu(jnp.einsum('th,ehi->tei', xf, W1) + b1, approximate=False)
        y = jnp.einsum('tei,eih->teh', h, W2) + b2
        out = jnp.take_along_axis(y, idx[:, None, None], axis=1)[:, 0, :]
        return out.reshape(B, S, Hd)
    x = L0_attn_x
    xn = _layernorm(x, axis=-1)
    x = x + _L0_attn_ref(xn, L0_attn_gamma, L0_attn_w_qkv, L0_attn_w_out, L0_attn_pm_k, L0_attn_pm_v) + _L0_ffn_ref(xn, L0_ffn_Wg, L0_ffn_Wu, L0_ffn_Wd, L0_ffn_Wr, L0_ffn_temperature)
    xn = _layernorm(x, axis=-1)
    x = x + _L1_attn_ref(xn, L1_attn_w_qkv, L1_attn_w_out) + _L1_ffn_ref(xn, L1_ffn_Wg, L1_ffn_bg, L1_ffn_W1, L1_ffn_b1, L1_ffn_W2, L1_ffn_b2)
    return x

_drawn_inputs = setup_inputs


def setup_inputs(seed=0):
    import zlib

    import numpy as np

    out = dict(_drawn_inputs(seed))
    spreads = {'L0_attn_gamma': (1.0, 0.2),
     'L1_ffn_bg': (0.0, 0.1),
     'L1_ffn_b1': (0.0, 0.709),
     'L1_ffn_b2': (0.0, 0.1)}
    factors = {'L0_attn_pm_k': 56.735, 'L0_attn_pm_v': 8.0}
    for name, (base, spread) in spreads.items():
        noise = np.random.default_rng([zlib.crc32(name.encode()), seed]).standard_normal(out[name].shape)
        drawn = base * np.exp(spread * noise) if base else spread * noise
        out[name] = jnp.asarray(drawn.astype(out[name].dtype))
    for name, factor in factors.items():
        out[name] = (out[name] * factor).astype(out[name].dtype)
    return out
```

```python
from contextlib import ExitStack
import math

import numpy as np

import concourse.bass as bass
from concourse import mybir

F32 = mybir.dt.float32
F32R = mybir.dt.float32r
BF16 = mybir.dt.bfloat16
F16 = mybir.dt.float16
ALU = mybir.AluOpType
ACT = mybir.ActivationFunctionType
AX = mybir.AxisListType.X

P = 128
BATCH = 8
S = 512
NT = S // P
H = 16
DH0 = 64
DH1 = P // H
SEG = 64
PM = 16
HH = H // 2
CH = HH // 2
NE = 8
GH = 4
NG = H // GH
VW = 32
NB = 7
MASKED = -1e30
CENTER = 1.0 / math.e
LOWER = 0.5 - math.log(4.0 / 3.0)
LOGIT_LOWER = math.log(LOWER / (1.0 - LOWER))
MROW = 96
TERMS_Q = [(0, 3, 0, 0), (3, 2, 1, 0), (5, 1, 2, 0)]
TERMS_K = [(0, 3, 0, 1), (3, 2, 0, 1), (5, 1, 0, 1)]


def key_widths():
    return [S - P * i for i in range(NT)]


def sized_jobs(widths, order):
    out = []
    for i in order:
        k = min(GH, 512 // widths[i]) if widths[i] <= 256 else 1
        out += [(i, h, k, widths[i]) for h in range(0, GH, k)]
    return out


MAX_JOBS = sized_jobs([P * (i + 1) for i in range(NT)], range(NT))
EXP_JOBS = sized_jobs(key_widths(), range(NT))
NMJ, NEJ = len(MAX_JOBS), len(EXP_JOBS)
PT_BASE = [GH * sum(key_widths()[:i]) for i in range(NT)]
PT_SIZE = GH * sum(key_widths())

PER = {
    "x_loaded": 16, "stats0": 4, "moments0": 4, "scales0": 6, "xn_ready": 4, "h_ready": 4,
    "xT_made": 1, "hT_made": 1, "xT_copied": 1, "hT_copied": 1, "splits0": 5,
    "z_made": 1, "route0": 37, "route_tanh": 1, "route_exp": 2, "wT_made": 1, "wT_copied": 1,
    "v_made": 8, "v_copied": 8, "q_made": 16, "q_copied": 16, "q16_made": 16,
    "rough_made": 8, "rough_pm_made": 2, "max0": 18, "maxT_made": 2, "maxT_copied": 2, "max_stored": 32, "max_rows": 32,
    "pm_scores": 2, "pm_probs": 2, "pt_zeroed": 2, "scores_made": 8, "probs_made": 16, "probs_masked": 16,
    "den_made": 2, "rden_made": 6, "spread_made": 8, "spread_copied": 8, "pv_made": 8, "oT_made": 8,
    "out0_added": 8, "wb_made": 8, "gate_made": 8, "up_made": 8, "tanh_made": 8,
    "glu_a": 8, "glu_b": 8, "glu_c": 8, "down0_added": 8,
    "y0_copied": 1, "y0_turned": 1, "x1_ready": 1,
    "stats1": 4, "moments1": 4, "scales1": 2, "xn1_ready": 4, "x1T_made": 1, "x1T_copied": 1, "splits1": 2,
    "z1_made": 1, "route1": 8, "pick_turned": 1, "rope_in": 4, "rope": 14, "parts_stored": 32,
    "parts_loaded0": 192 * NG // 2, "parts_loaded1": 192 * NG // 2, "v1_made": 1, "v1_copied": 1, "rough1_made": NMJ * NG, "max1": NMJ * NG,
    "max1_parts": 3 * NG, "maxT1_made": NG, "maxT1_copied": NG, "max1_stored0": 8 * NG, "max1_stored1": 8 * NG, "max1_rows0": 8 * NG, "max1_rows1": 8 * NG,
    "scores1_made": NEJ * NG, "probs1_made": NEJ * NG, "probs1_masked": NEJ * NG,
    "pv1_made": NG, "pv1_copied": NG, "o1_turned": NG, "o1_ready": 2 * NG, "ocT_made": 1, "ocT_copied": 1,
    "out1_added": 1, "hidden_made": 8, "gelu_made": 8, "down1_added": 8, "y1_copied": 1, "y1_turned": 1,
    "out_ready": 1, "stored": 16,
}


START = {"x1_ready": 1, "stored": 1}


def bank_plan():
    jobs = [("xT", "xT_copied", 1), ("hT", "hT_copied", 1), ("z", "route0", 1)]

    def expert(e):
        return [(("wb", e), "glu_c", e + 1), (("gate", e), "glu_a", e + 1), (("up", e), "glu_b", e + 1)]

    for a in range(2):
        jobs += [(("v", a, t), "v_copied", 4 * a + t + 1) for t in range(NT)]
        jobs += [(("q", a, h), "q_copied", HH * a + h + 1) for h in range(HH)]
        jobs += [("wT", "wT_copied", 1)] if a == 0 else []
        jobs += [(("rough_pm", a), "max0", 9 * a + 1)]
        jobs += [(("rough", a, t), "max0", 9 * a + 2 + t) for t in range(NT)]
        jobs += expert(4 * a)
        jobs += [(("maxT", a), "maxT_copied", a + 1)]
        jobs += expert(4 * a + 1)
        jobs += [(("pm_scores", a), "pm_probs", a + 1)]
        jobs += [(("scores", a, t), "probs_made", 8 * a + 2 * t + 2) for t in range(NT)]
        jobs += expert(4 * a + 2)
        jobs += [(("den", a), "rden_made", 3 * a + 1)]
        for c in range(CH):
            jobs += [(("spread", a, c), "spread_copied", 4 * a + c + 1), (("pv", a, c), "oT_made", 4 * a + c + 1)]
        jobs += expert(4 * a + 3)
    jobs += [("y0", "x1_ready", 1), ("x1T", "x1T_copied", 1)]
    jobs += [(("rope", j), "rope", (1, 2, 8, 9)[j]) for j in range(4)]
    jobs += [("z1", "route1", 1), ("v1", "v1_copied", 1), ("pick", "route1", 7)]
    jobs += [(("hidden", e), "gelu_made", e + 1) for e in range(NE)]

    def max_pass(g):
        return [(("rough1", g, n), "max1", NMJ * g + n + 1) for n in range(NMJ)] + [(("maxT1", g), "maxT1_copied", g + 1)]

    def exp_pass(g):
        return [(("scores1", g, n), "probs1_made", NEJ * g + n + 1) for n in range(NEJ)]

    def values(g):
        return [(("pv1", g), "pv1_copied", g + 1), (("o1", g), "o1_ready", 2 * g + 2)]

    jobs += max_pass(0)
    for g in range(NG):
        jobs += max_pass(g + 1) if g + 1 < NG else []
        jobs += exp_pass(g) + values(g)
    jobs += [("ocT", "ocT_copied", 1), ("y1", "out_ready", 1)]
    last, plan = {}, {}
    for n, (job, sem, count) in enumerate(jobs):
        bank = n % NB
        plan[job] = (bank, last.get(bank))
        last[bank] = (sem, count)
    return plan


def build(nc, ins, out):
    plan = bank_plan()
    with ExitStack() as ctx:
        def sb(name, shape, dt):
            return ctx.enter_context(nc.sbuf_tensor(name, shape, dt))

        sem = {name: ctx.enter_context(nc.semaphore(name)) for name in PER}
        s_load = ctx.enter_context(nc.semaphore("weights_loaded"))
        s_set = ctx.enter_context(nc.semaphore("weights_prepared"))
        s_setpe = ctx.enter_context(nc.semaphore("folded_weights_made"))
        s_clear = ctx.enter_context(nc.semaphore("buffers_cleared"))

        banks = ctx.enter_context(nc.psum_tensor("banks", [P, 8, 512], F32))
        ysum = banks[:, NB, :]

        def bank(job):
            return banks[:, plan[job][0], :]

        aq = [sb(f"aq{i}", [P, H, P], F32R) for i in range(2)]
        wv = [sb(f"wv{i}", [P, H * DH0], F32R) for i in range(2)]
        wg = [sb(f"wg{i}", [P, NE, P], F32R) for i in range(2)]
        wu = [sb(f"wu{i}", [P, NE, P], F32R) for i in range(2)]
        w1 = [sb(f"w1{i}", [P, NE, P], F32R) for i in range(2)]
        qk1 = [sb(f"qk1{i}", [P, 4, P], F32R) for i in range(2)]
        wo0 = sb("wo0", [P, H // 2, P], F32)
        wd = sb("wd", [P, NE, P], F32)
        w2 = sb("w2", [P, NE, P], F32)
        gpm = sb("gpm", [P, H * PM], F32)
        gpm16 = sb("gpm16", [P, H * PM], F16)
        pmv = sb("pmv", [P, H // 2, P], F32)
        small = sb("small", [P, 3 * P + 8 + 8 + 8 + 8 + 4], F32)
        wv1, wo1, ident = small[:, 0:P], small[:, P:2 * P], small[:, 2 * P:3 * P]
        wr = small[:, 3 * P:3 * P + 8]
        wgate = small[:, 3 * P + 8:3 * P + 16]
        bg = small[:, 3 * P + 16:3 * P + 24]
        b1T = small[:, 3 * P + 24:3 * P + 32]
        gam, gam8, temp, rtemp = (small[:, 3 * P + 32 + i:3 * P + 33 + i] for i in range(4))
        b2 = sb("b2", [NE, P], F32)
        rank = sb("rank", [P, NT, NE], F32)
        esel = sb("esel", [P, 2, 32], F32)
        epm = sb("epm", [P, 4, 32], F32)
        cos = sb("cos", [P, S], F32)
        sin = sb("sin", [P, S], F32)
        identb = sb("identb", [P, P], BF16)
        mask0 = sb("mask0", [P, SEG], BF16)
        mask1 = sb("mask1", [P, S], BF16)
        selr = sb("selr", [P, CH, P], F32R)
        selw = sb("selw", [24, NE, P], BF16)
        selpm = sb("selpm", [2 * HH, P], BF16)
        neg = sb("neg", [P, SEG], BF16)
        v1 = sb("v1", [P, NT, H, VW], F32)
        QS = sb("QS", [P, 2, GH, S], BF16)
        KS = sb("KS", [P, 2, GH, S], BF16)
        QS8 = QS[:, :, :, :].rearrange("p a h t -> p (a h) t")

        big = sb("big", [P, 12288], F32)
        q32 = big[:, 0:4096].rearrange("p (h t) -> p h t", h=HH)
        q16 = big[:, 4096:6144].bitcast(F16).rearrange("p (h t) -> p h t", h=HH)
        v = big[:, 6144:8192].rearrange("p (t n) -> p t n", t=NT)
        PT = big[:, 8192:12288].rearrange("p (t h q) -> p t h q", t=NT, h=HH)
        PT1 = [big[:, PT_SIZE * i:PT_SIZE * (i + 1)] for i in range(2)]
        tmp = big[:, PT_SIZE:PT_SIZE + 4 * S].rearrange("p (a t) -> p a t", a=4)
        pq = big[:, PT_SIZE + 4 * S:PT_SIZE + 7 * S].bitcast(BF16).rearrange("p (j a t) -> p j a t", j=2, a=3)
        ohT = big[0:NE, 2 * PT_SIZE:2 * PT_SIZE + S]
        gm = big[0:NE, 2 * PT_SIZE + S:2 * PT_SIZE + 3 * S // 2].bitcast(BF16)
        mT1 = big[0:2 * GH, 2 * PT_SIZE + 2 * S:2 * PT_SIZE + 3 * S].bitcast(BF16).rearrange("p (a t) -> p a t", a=2)

        x = sb("x", [P, NT, P], F32)
        x1 = sb("x1", [P, NT, P], F32)
        xn = sb("xn", [P, NT, P], F32)
        hn = sb("hn", [P, NT, P], F32)
        xT = sb("xT", [P, S], F32)
        hT = sb("hT", [P, S], F32)
        xTs = [sb(f"xTs{i}", [P, S], F32R) for i in range(2)]
        hTs = [sb(f"hTs{i}", [P, S], F32R) for i in range(2)]
        hT16 = sb("hT16", [P, S], F16)
        st = sb("st", [P, 2 * NT, 6], F32)
        mv = sb("mv", [P, 2 * NT, 2], F32)
        sc = sb("sc", [P, 6, NT], F32)
        half = sb("half", [P, NT], F32)
        rt = sb("rt", [P, 16, NT, NE], F32)
        rw = sb("rw", [P, 12, NT], F32)
        wp = sb("wp", [P, NT, 24], BF16)
        wT = sb("wT", [24, S], BF16)
        mx = sb("mx", [P, 4, NT, HH], F32)
        mp = sb("mp", [P, NT, 2, HH], BF16)
        mT = sb("mT", [2 * HH, S], BF16)
        ppm = sb("ppm", [P, S], F32)
        rds = [sb(f"rds{i}", [P, S], F32R) for i in range(2)]
        spread = sb("spread", [P, 2, S], F32)
        oT = sb("oT", [P, 2, S], F32)
        act = sb("act", [P, 2, S], F32)
        glu = sb("glu", [P, S], F32)
        rd = glu
        glc = sb("glc", [P, 2, S], F32)
        yT = sb("yT", [P, S], F32)
        yout = hn
        o1v = spread[:, 0, :].rearrange("p (t h d) -> p t h d", t=NT, h=H)
        rdn = sb("rdn", [P, NT, GH], F32)
        mx1 = sb("mx1", [P, 2, NT, GH], F32)
        mp1 = sb("mp1", [P, NT, 2, GH], BF16)
        ov = oT
        scratch = nc.dram_tensor("scratch", [2, 3, P, S], BF16, kind="Internal").ap()

        mrows0 = nc.dram_tensor("mrows0", [2, 2, HH, S], BF16, kind="Internal").ap()
        mrows1 = nc.dram_tensor("mrows1", [NG, 2, GH, S], BF16, kind="Internal").ap()

        x_d, out_d = ins["x"], out
        staged = ["wv", "wg", "wu", "w1", "qk1", "wqT", "wkT", "gbc", "pmkT", "mask0", "mask1", "selr", "selw", "selpm"]
        direct = {"wo0": wo0, "wd": wd, "w2": w2, "pmv": pmv, "small": small[:, 0:3 * P + 36], "b2": b2,
                  "rank": rank, "esel": esel, "epm": epm, "cos": cos, "sin": sin}
        at, place = 0, {}
        for name in staged:
            rows, cols = ins[name].shape
            place[name] = big[0:rows, at:at + cols]
            at += cols
        assert at <= 12288
        loads = len(staged) + len(direct)

        block = ctx.enter_context(nc.Block())

        @block.sync
        def _(sp):
            for name in staged:
                sp.dma_start(place[name], ins[name]).then_inc(s_load, 16)
            for name, t in direct.items():
                dst = t if name == "small" else t[tuple([slice(None)] * len(t.shape))]
                src = ins[name]
                if len(dst.shape) == 3:
                    src = src.rearrange("p (a b) -> p a b", a=dst.shape[1])
                sp.dma_start(dst, src).then_inc(s_load, 16)
            for name, n in START.items():
                sp.sem_inc(sem[name], n)
            with sp.Fori(0, BATCH) as b:
                def up(name, n):
                    return b * PER[name] + START.get(name, 0) + n

                sp.wait_ge(sem["x1_ready"], up("x1_ready", 0))
                sp.dma_start(x[:, :, :], x_d[bass.ds(b, 1), :, :].rearrange("a (t p) d -> p (a t) d", p=P)).then_inc(sem["x_loaded"], 16)
                for a in range(2):
                    sp.wait_ge(sem["maxT_copied"], up("maxT_copied", a + 1))
                    if a:
                        sp.wait_ge(sem["scores_made"], up("scores_made", NT * a))
                    sp.dma_start(mrows0[a].rearrange("j h t -> (j h) t"), mT[:, :]).then_inc(sem["max_stored"], 16)
                    sp.wait_ge(sem["max_stored"], up("max_stored", 16 * (a + 1)))
                    sp.dma_start(QS8[MROW:MROW + 2, :, :], mrows0[a]).then_inc(sem["max_rows"], 16)
                for j in range(2):
                    sp.wait_ge(sem["rope"], up("rope", 7 * (j + 1)))
                    sp.dma_start(scratch[j].rearrange("a p t -> p a t"), pq[:, j, :, :]).then_inc(sem["parts_stored"], 16)
                sp.wait_ge(sem["parts_stored"], up("parts_stored", 32))

                def load_group(g):
                    for j, (dst, terms) in enumerate(((QS, TERMS_Q), (KS, TERMS_K))):
                        for first, n, p0, step in terms:
                            for m in range(n):
                                src = scratch[j, p0 + step * m].rearrange("(h d) t -> d h t", d=DH1)
                                r = DH1 * (first + m)
                                sp.dma_start(dst[r:r + DH1, g % 2, :, :], src[:, GH * g:GH * (g + 1), :])\
                                    .then_inc(sem[f"parts_loaded{g % 2}"], 16)

                def rows_group(g):
                    sp.wait_ge(sem["maxT1_copied"], up("maxT1_copied", g + 1))
                    sp.dma_start(mrows1[g].rearrange("j h t -> (j h) t"), mT1[:, g % 2, :]).then_inc(sem[f"max1_stored{g % 2}"], 16)
                    sp.wait_ge(sem[f"max1_stored{g % 2}"], up(f"max1_stored{g % 2}", 16 * (g // 2 + 1)))
                    sp.dma_start(QS[MROW:MROW + 2, g % 2, :, :], mrows1[g]).then_inc(sem[f"max1_rows{g % 2}"], 16)

                load_group(0)
                load_group(1)
                for g in range(NG):
                    rows_group(g)
                    if g + 2 < NG:
                        sp.wait_ge(sem["scores1_made"], up("scores1_made", NEJ * (g + 1)))
                        load_group(g + 2)
                sp.wait_ge(sem["out_ready"], up("out_ready", 1))
                sp.dma_start(out_d[bass.ds(b, 1), :, :].rearrange("a (t p) d -> p (a t) d", p=P), yout[:, :, :]).then_inc(sem["stored"], 16)
            sp.wait_ge(sem["stored"], BATCH * PER["stored"] + START["stored"])


        @block.tensor
        def _(pe):
            pe.wait_ge(s_load, 16 * loads)
            pe.wait_ge(s_set, SETUP_KEYS)
            for h in range(H):
                r, c = DH0 * (h % 2), h // 2
                rows = slice(r, r + DH0)
                mm = pe.matmul(banks[:, 2 * (h % 2) + c // 4, P * (c % 4):P * (c % 4) + P], place["wqT"][rows, P * c:P * c + P],
                               place["wkT"][rows, P * c:P * c + P], start=True, stop=True)
            mm.then_inc(s_setpe, 1)
            for h in range(H):
                r, c = DH0 * (h % 2), h // 2
                rows = slice(r, r + DH0)
                mm = pe.matmul(banks[:, 4 + h % 2, PM * c:PM * (c + 1)], place["wqT"][rows, P * c:P * c + P],
                               place["pmkT"][rows, PM * h:PM * (h + 1)], start=True, stop=True)
            mm.then_inc(s_setpe, 1)
            pe.wait_ge(s_set, SETUP_ALL)
            pe.wait_ge(s_clear, CLEARED)

            with pe.Fori(0, BATCH) as b:
                def up(name, n):
                    return b * PER[name] + START.get(name, 0) + n

                def claim(job):
                    before = plan[job][1]
                    if before:
                        pe.wait_ge(sem[before[0]], up(*before))
                    return bank(job)

                def three(o, w, m, first=True, last=True):
                    pe.matmul(o, w[0], m[0], start=first, stop=False, skip_group_check=True)
                    pe.matmul(o, w[1], m[0], start=False, stop=False, skip_group_check=True)
                    return pe.matmul(o, w[0], m[1], start=False, stop=last, skip_group_check=True)

                def turn(job, src, ready, done, dt=F32, width=P, rows=P):
                    o = claim(job)
                    o = o if dt == F32 else o.bitcast(BF16)
                    for t in range(NT):
                        if ready:
                            pe.wait_ge(sem[ready[0]], up(ready[0], ready[1](t)))
                        mm = pe.transpose(o[0:rows, P * t:P * (t + 1)], src(t), (ident if dt == F32 else identb[:, :]))
                    mm.then_inc(sem[done], 1)

                turn("xT", lambda t: xn[:, t, :], ("xn_ready", lambda t: t + 1), "xT_made")
                turn("hT", lambda t: hn[:, t, :], ("h_ready", lambda t: t + 1), "hT_made")
                z = claim("z")
                pe.wait_ge(sem["xT_copied"], up("xT_copied", 1))
                for t in range(NT):
                    mm = pe.matmul(z[:, NE * t:NE * (t + 1)], xT[:, P * t:P * (t + 1)], wr, start=True, stop=True)
                mm.then_inc(sem["z_made"], 1)

                def expert0(e):
                    o = claim(("wb", e))
                    pe.wait_ge(sem["wT_copied"], up("wT_copied", 1))
                    pe.matmul(o, selw[:, e, :], wT[:, :], start=True, stop=True).then_inc(sem["wb_made"], 1)
                    o = claim(("gate", e))
                    three(o, [w[:, e, :] for w in wg], [m[:, :] for m in xTs]).then_inc(sem["gate_made"], 1)
                    o = claim(("up", e))
                    three(o, [w[:, e, :] for w in wu], [m[:, :] for m in xTs]).then_inc(sem["up_made"], 1)
                    if e:
                        down0(e - 1)

                def down0(e):
                    pe.wait_ge(sem["glu_c"], up("glu_c", e + 1))
                    pe.matmul(ysum, wd[:, e, :], glc[:, e % 2, :], start=(e == 0), stop=(e == NE - 1),
                              skip_group_check=True).then_inc(sem["down0_added"], 1)

                def down1(e):
                    pe.wait_ge(sem["gelu_made"], up("gelu_made", e + 1))
                    pe.matmul(ysum, w2[:, e, :], act[:, e % 2, :], start=False, stop=False, skip_group_check=True)\
                        .then_inc(sem["down1_added"], 1)

                def out0(a, c):
                    pe.wait_ge(sem["oT_made"], up("oT_made", CH * a + c + 1))
                    pe.matmul(ysum, wo0[:, CH * a + c, :], oT[:, c % 2, :], start=False, stop=False,
                              skip_group_check=True).then_inc(sem["out0_added"], 1)

                pe.wait_ge(sem["splits0"], up("splits0", 5))
                for a in range(2):
                    for t in range(NT):
                        o = claim(("v", a, t))
                        three(o, [m[:, P * t:P * (t + 1)] for m in hTs], [w[:, S * a:S * (a + 1)] for w in wv])\
                            .then_inc(sem["v_made"], 1)
                    for h in range(HH):
                        o = claim(("q", a, h))
                        three(o, [w[:, HH * a + h, :] for w in aq], [m[:, :] for m in hTs]).then_inc(sem["q_made"], 1)
                    if a == 0:
                        turn("wT", lambda t: wp[:, t, :], ("route0", lambda t: 37), "wT_made", BF16, rows=24)
                    o = claim(("rough_pm", a))
                    for t in range(NT):
                        mm = pe.matmul(o[:, P * t:P * (t + 1)], hT16[:, P * t:P * (t + 1)],
                                       gpm16[:, P * a:P * (a + 1)], start=True, stop=True)
                    mm.then_inc(sem["rough_pm_made"], 1)
                    for t in range(NT):
                        o = claim(("rough", a, t))
                        pe.matmul(o.rearrange("p (h k) -> p h k", h=HH), identb[:, :], mask0[:, :].rearrange("p (o k) -> p o k", o=1).broadcast_to([P, HH, SEG]), start=True, stop=False, skip_group_check=True)
                        for h in range(HH):
                            if t == 0:
                                pe.wait_ge(sem["q16_made"], up("q16_made", HH * a + h + 1))
                            for w in range(2):
                                k = P * t + SEG * w
                                mm = pe.matmul(o[SEG * w:SEG * (w + 1), SEG * h:SEG * (h + 1)], q16[:, h, k:k + SEG],
                                               hT16[:, k:k + SEG], start=False, stop=(h == HH - 1), skip_group_check=True)
                        mm.then_inc(sem["rough_made"], 1)
                    expert0(4 * a)
                    turn(("maxT", a), lambda t: mp[:, t, :, :].rearrange("p c h -> p (c h)"),
                         ("max0", lambda t: 9 * (a + 1)), "maxT_made", BF16, rows=2 * HH)
                    expert0(4 * a + 1)
                    o = claim(("pm_scores", a))
                    pe.wait_ge(sem["maxT_copied"], up("maxT_copied", a + 1))
                    pe.matmul(o, selpm[:, :], mT[:, :], start=True, stop=False, skip_group_check=True)
                    pe.matmul(o, gpm[:, P * a:P * (a + 1)], hT[:, :], start=False, stop=True, skip_group_check=True)\
                        .then_inc(sem["pm_scores"], 1)
                    pe.wait_ge(sem["max_rows"], up("max_rows", 16 * (a + 1)))
                    for t in range(NT):
                        o = claim(("scores", a, t))
                        for w in range(2):
                            k = P * t + SEG * w
                            pe.matmul(o[SEG * w:SEG * (w + 1), :].rearrange("p (h q) -> p h q", h=HH), neg[0:MROW + 2, :],
                                      QS8[0:MROW + 2, :, k:k + SEG], start=True, stop=False, skip_group_check=True)
                        for w in range(2):
                            k = P * t + SEG * w
                            mm = pe.matmul(o[SEG * w:SEG * (w + 1), :].rearrange("p (h q) -> p h q", h=HH), hT[:, k:k + SEG],
                                           q32[:, :, k:k + SEG], start=False, stop=True, skip_group_check=True)
                        mm.then_inc(sem["scores_made"], 1)
                    expert0(4 * a + 2)
                    o = claim(("den", a))
                    pe.wait_ge(sem["pm_probs"], up("pm_probs", a + 1))
                    for j in range(4):
                        pe.matmul(o[32 * j:32 * j + 32, :], epm[:, j, :], ppm[:, :], start=True, stop=False,
                                  skip_group_check=True)
                    for t in range(NT):
                        pe.wait_ge(sem["probs_masked"], up("probs_masked", 8 * a + 2 * t + 2))
                        for h in range(HH):
                            j = h % 4
                            mm = pe.matmul(o[32 * j:32 * j + 32, P * t:P * (t + 1)], esel[:, h // 4, :], PT[:, t, h, :],
                                           start=False, stop=(h >= 4), skip_group_check=True)
                    mm.then_inc(sem["den_made"], 1)
                    for c in range(CH):
                        o = claim(("spread", a, c))
                        if c == 0:
                            pe.wait_ge(sem["rden_made"], up("rden_made", 3 * (a + 1)))
                        pe.matmul(o, selr[:, c, :], rds[0][:, :], start=True, stop=False, skip_group_check=True)
                        pe.matmul(o, selr[:, c, :], rds[1][:, :], start=False, stop=True, skip_group_check=True)\
                            .then_inc(sem["spread_made"], 1)
                        o = claim(("pv", a, c))
                        pe.matmul(o, pmv[:, CH * a + c, :], ppm[:, :], start=True, stop=False, skip_group_check=True)
                        for t in range(NT):
                            for r in range(2):
                                h = 2 * c + r
                                mm = pe.matmul(o[DH0 * r:DH0 * (r + 1), P * t:P * (t + 1)], v[:, t, DH0 * h:DH0 * (h + 1)],
                                               PT[:, t, h, :], start=False, stop=True, skip_group_check=True)
                        mm.then_inc(sem["pv_made"], 1)
                        if c:
                            out0(a, c - 1)
                    expert0(4 * a + 3)
                    out0(a, CH - 1)
                down0(NE - 1)
                turn("y0", lambda t: yT[:, P * t:P * (t + 1)], ("y0_copied", lambda t: 1), "y0_turned")

                turn("x1T", lambda t: xn[:, t, :], ("xn1_ready", lambda t: t + 1), "x1T_made")
                pe.wait_ge(sem["splits1"], up("splits1", 2))
                for j in range(4):
                    o = claim(("rope", j))
                    three(o, [w[:, j, :] for w in qk1], [m[:, :] for m in xTs]).then_inc(sem["rope_in"], 1)
                o = claim("z1")
                for t in range(NT):
                    mm = pe.matmul(o[:, NE * t:NE * (t + 1)], xT[:, P * t:P * (t + 1)], wgate, start=True, stop=True)
                mm.then_inc(sem["z1_made"], 1)
                o = claim("v1")
                for t in range(NT):
                    mm = pe.matmul(o[:, P * t:P * (t + 1)], xT[:, P * t:P * (t + 1)], wv1, start=True, stop=True)
                mm.then_inc(sem["v1_made"], 1)
                turn("pick", lambda t: rt[:, 5, t, :], ("route1", lambda t: 6), "pick_turned", rows=NE)
                pe.wait_ge(sem["route1"], up("route1", 8))
                pe.wait_ge(sem["y0_copied"], up("y0_copied", 1))
                pe.matmul(ysum, b2[:, :], ohT, start=True, stop=False, skip_group_check=True)
                for e in range(NE):
                    o = claim(("hidden", e))
                    pe.matmul(o, selw[0:NE, e, :], gm, start=True, stop=False, skip_group_check=True)
                    three(o, [w[:, e, :] for w in w1], [m[:, :] for m in xTs], first=False).then_inc(sem["hidden_made"], 1)
                    if e:
                        down1(e - 1)
                down1(NE - 1)

                def max_pass(g):
                    for n, (t, h0, k, w) in enumerate(MAX_JOBS):
                        o = claim(("rough1", g, n))
                        if n == 0:
                            pe.wait_ge(sem[f"parts_loaded{g % 2}"], up(f"parts_loaded{g % 2}", 192 * (g // 2 + 1)))
                        if t == 0:
                            pe.matmul(o, identb[:, :], mask1[:, :], start=True, stop=False, skip_group_check=True)
                        else:
                            for j in range(k):
                                pe.matmul(o[:, w * j + w - P:w * (j + 1)], identb[:, :], mask1[:, 0:P], start=(j == 0),
                                          stop=False, skip_group_check=True)
                        for j in range(k):
                            mm = pe.matmul(o[:, w * j:w * (j + 1)], QS[0:MROW, g % 2, h0 + j, P * t:P * (t + 1)],
                                           KS[0:MROW, g % 2, h0 + j, 0:w], start=False, stop=(j == k - 1),
                                           skip_group_check=True)
                        mm.then_inc(sem["rough1_made"], 1)

                def exp_pass(g):
                    pe.wait_ge(sem[f"max1_rows{g % 2}"], up(f"max1_rows{g % 2}", 16 * (g // 2 + 1)))
                    for n, (i, h0, k, w) in enumerate(EXP_JOBS):
                        o = claim(("scores1", g, n))
                        for j in range(k):
                            mm = pe.matmul(o[:, w * j:w * (j + 1)], KS[0:MROW + 2, g % 2, h0 + j, P * i:P * (i + 1)],
                                           QS[0:MROW + 2, g % 2, h0 + j, P * i:S], start=(j == 0), stop=(j == k - 1),
                                           skip_group_check=True)
                        mm.then_inc(sem["scores1_made"], 1)

                def values(g):
                    o = claim(("pv1", g))
                    for n, (i, h0, k, w) in enumerate(EXP_JOBS):
                        pe.wait_ge(sem["probs1_masked"], up("probs1_masked", NEJ * g + n + 1))
                        for h in range(h0, h0 + k):
                            at = PT_BASE[i] + w * h
                            mm = pe.matmul(o[32 * h:32 * h + 32, P * i:S], v1[:, i, GH * g + h, :],
                                           PT1[g % 2][:, at:at + w], start=(i == 0), stop=(i == NT - 1),
                                           skip_group_check=True)
                    mm.then_inc(sem["pv1_made"], 1)
                    turn(("o1", g), lambda t: ov[:, g % 2, P * t:P * (t + 1)], ("pv1_copied", lambda t: g + 1), "o1_turned")

                def max_turn(g):
                    turn(("maxT1", g), lambda t: mp1[:, t, :, :].rearrange("p c h -> p (c h)"),
                         ("max1_parts", lambda t: 3 * (g + 1)), "maxT1_made", BF16, rows=2 * GH)

                max_pass(0)
                max_turn(0)
                for g in range(NG):
                    if g + 1 < NG:
                        max_pass(g + 1)
                        max_turn(g + 1)
                    exp_pass(g)
                    values(g)
                turn("ocT", lambda t: o1v[:, t, :, :].rearrange("p h d -> p (h d)"), ("o1_ready", lambda t: 2 * NG), "ocT_made")
                pe.wait_ge(sem["ocT_copied"], up("ocT_copied", 1))
                pe.matmul(ysum, wo1, hT[:, :], start=False, stop=True, skip_group_check=True).then_inc(sem["out1_added"], 1)
                turn("y1", lambda t: yT[:, P * t:P * (t + 1)], ("y1_copied", lambda t: 1), "y1_turned")

        @block.scalar
        def _(sc_):
            act_e = sc_
            with act_e.Fori(0, BATCH) as b:
                def up(name, n):
                    return b * PER[name] + START.get(name, 0) + n

                def copy(dst, job, made, n, done):
                    act_e.wait_ge(sem[made], up(made, n))
                    act_e.activation(dst, job, ACT.Copy).then_inc(sem[done], 1)

                def tanh0(e):
                    act_e.wait_ge(sem["gate_made"], up("gate_made", e + 1))
                    if e >= 2:
                        act_e.wait_ge(sem["glu_a"], up("glu_a", e - 1))
                    act_e.activation(act[:, e % 2, :], bank(("gate", e)), ACT.Tanh, scale=0.5).then_inc(sem["tanh_made"], 1)

                copy(xT[:, :], bank("xT"), "xT_made", 1, "xT_copied")
                copy(hT[:, :], bank("hT"), "hT_made", 1, "hT_copied")
                for a in range(2):
                    for t in range(NT):
                        if a and t == 0:
                            act_e.wait_ge(sem["pv_made"], up("pv_made", CH))
                        copy(v[:, t, :], bank(("v", a, t)), "v_made", NT * a + t + 1, "v_copied")
                    if a == 0:
                        act_e.wait_ge(sem["route0"], up("route0", 1))
                        act_e.activation(rt[:, 1, :, :], rt[:, 0, :, :], ACT.Tanh, scale=0.5).then_inc(sem["route_tanh"], 1)
                    for h in range(HH):
                        if a and h == 0:
                            act_e.wait_ge(sem["scores_made"], up("scores_made", NT))
                        copy(q32[:, h, :], bank(("q", a, h)), "q_made", HH * a + h + 1, "q_copied")
                        if a == 0 and h == 3:
                            act_e.wait_ge(sem["route0"], up("route0", 5))
                            act_e.activation(rt[:, 5, :, :], rt[:, 4, :, :], ACT.Exp, scale=10.0).then_inc(sem["route_exp"], 1)
                            act_e.activation(rt[:, 6, :, :], rt[:, 4, :, :], ACT.Exp, scale=1.0 / 0.3).then_inc(sem["route_exp"], 1)
                    tanh0(4 * a)
                    tanh0(4 * a + 1)
                    act_e.wait_ge(sem["pm_scores"], up("pm_scores", a + 1))
                    if a:
                        act_e.wait_ge(sem["pv_made"], up("pv_made", CH))
                    act_e.activation(ppm[:, :], bank(("pm_scores", a)), ACT.Exp).then_inc(sem["pm_probs"], 1)
                    act_e.wait_ge(sem["pt_zeroed"], up("pt_zeroed", 2))
                    for t in range(NT):
                        act_e.wait_ge(sem["scores_made"], up("scores_made", NT * a + t + 1))
                        for w in range(2):
                            rows = slice(SEG * w, SEG * (w + 1))
                            act_e.activation(PT[rows, t, :, SEG * w:SEG * (w + 1)],
                                             bank(("scores", a, t))[rows, :].rearrange("p (h q) -> p h q", h=HH),
                                             ACT.Exp).then_inc(sem["probs_made"], 1)
                    tanh0(4 * a + 2)
                    for c in range(CH):
                        n = CH * a + c
                        if n >= 2:
                            act_e.wait_ge(sem["oT_made"], up("oT_made", n - 1))
                        copy(spread[:, c % 2, :], bank(("spread", a, c)), "spread_made", n + 1, "spread_copied")
                    tanh0(4 * a + 3)
                copy(yT[:, :], ysum, "down0_added", NE, "y0_copied")
                copy(xT[:, :], bank("x1T"), "x1T_made", 1, "x1T_copied")
                copy(v1[:, :, :, 0:DH1].rearrange("p t h d -> p (t h) d"), bank("v1").rearrange("p (n d) -> p n d", d=DH1),
                     "v1_made", 1, "v1_copied")
                for e in range(NE):
                    act_e.wait_ge(sem["hidden_made"], up("hidden_made", e + 1))
                    if e >= 2:
                        act_e.wait_ge(sem["down1_added"], up("down1_added", e - 1))
                    act_e.activation(act[:, e % 2, :], bank(("hidden", e)), ACT.Gelu, bias=b1T[:, e:e + 1]).then_inc(sem["gelu_made"], 1)
                for g in range(NG):
                    for n, (i, h0, k, w) in enumerate(EXP_JOBS):
                        act_e.wait_ge(sem["scores1_made"], up("scores1_made", NEJ * g + n + 1))
                        if g >= 2 and n == 0:
                            act_e.wait_ge(sem["pv1_made"], up("pv1_made", g - 1))
                        at = PT_BASE[i] + w * h0
                        act_e.activation(PT1[g % 2][:, at:at + w * k], bank(("scores1", g, n))[:, 0:w * k], ACT.Exp)\
                            .then_inc(sem["probs1_made"], 1)
                    if g >= 2:
                        act_e.wait_ge(sem["o1_turned"], up("o1_turned", g - 1))
                    copy(ov[:, g % 2, :], bank(("pv1", g)), "pv1_made", g + 1, "pv1_copied")
                copy(hT[:, :], bank("ocT"), "ocT_made", 1, "ocT_copied")
                copy(yT[:, :], ysum, "out1_added", 1, "y1_copied")

        @block.gpsimd
        def _(pool):
            pool.memset(QS[:, :, :, :], 0.0).then_inc(s_clear, 1)
            pool.memset(KS[:, :, :, :], 0.0).then_inc(s_clear, 1)
            pool.memset(v1[:, :, :, :], 0.0).then_inc(s_clear, 1)
            pool.memset(neg[:, :], 0.0).then_inc(s_clear, 1)
            pool.memset(half[:, :], -0.5).then_inc(s_clear, 1)
            pool.wait_ge(s_clear, 5)
            pool.memset(KS[MROW:MROW + 2, :, :, :], -1.0).then_inc(s_clear, 1)
            pool.wait_ge(s_clear, 6)
            pool.memset(neg[MROW:MROW + 2, :], -1.0).then_inc(s_clear, 1)
            pool.wait_ge(s_clear, 7)
            pool.memset(v1[:, :, :, DH1:DH1 + 1], 1.0).then_inc(s_clear, 1)
            pool.wait_ge(s_clear, CLEARED)
            pool.wait_ge(s_set, SETUP_ALL)
            with pool.Fori(0, BATCH) as b:
                def up(name, n):
                    return b * PER[name] + START.get(name, 0) + n

                def scales(layer, rms):
                    s, var = f"scales{layer}", mv[:, NT * layer:NT * (layer + 1), 1]
                    pool.wait_ge(sem[f"moments{layer}"], up(f"moments{layer}", NT))
                    pool.nop(nofuse=True)
                    pool.tensor_scalar(sc[:, 0, :], var, 1e-5, None, ALU.add).then_inc(sem[s], 1)
                    pool.wait_ge(sem[s], up(s, 1))
                    pool.nop(nofuse=True)
                    pool.tensor_tensor(sc[:, 1, :], sc[:, 0, :], half[:, :], ALU.pow).then_inc(sem[s], 1)
                    if rms:
                        pool.wait_ge(sem[s], up(s, 2))
                        pool.nop(nofuse=True)
                        pool.tensor_tensor(sc[:, 2, :], sc[:, 1, :], sc[:, 1, :], ALU.mult).then_inc(sem[s], 1)
                        pool.wait_ge(sem[s], up(s, 3))
                        pool.nop(nofuse=True)
                        pool.tensor_tensor(sc[:, 3, :], sc[:, 2, :], var, ALU.mult).then_inc(sem[s], 1)
                        pool.wait_ge(sem[s], up(s, 4))
                        pool.nop(nofuse=True)
                        pool.tensor_scalar(sc[:, 4, :], sc[:, 3, :], 1e-6, None, ALU.add).then_inc(sem[s], 1)
                        pool.wait_ge(sem[s], up(s, 5))
                        pool.nop(nofuse=True)
                        pool.tensor_tensor(sc[:, 5, :], sc[:, 4, :], half[:, :], ALU.pow).then_inc(sem[s], 1)

                scales(0, True)
                for w in range(2):
                    if w:
                        pool.wait_ge(sem["pt_zeroed"], up("pt_zeroed", 1))
                        pool.nop(nofuse=True)
                    pool.memset(PT[SEG * w:SEG * (w + 1), :, :, SEG * (1 - w):SEG * (2 - w)].rearrange("p t h q -> p (t h) q"), 0.0)\
                        .then_inc(sem["pt_zeroed"], 1)
                pool.wait_ge(sem["pt_zeroed"], up("pt_zeroed", 2))
                pool.nop(nofuse=True)
                for a in range(2):
                    for t in range(NT):
                        for w in range(2):
                            n = 2 * (NT * a + t) + w + 1
                            pool.wait_ge(sem["probs_made"], up("probs_made", n))
                            pool.nop(nofuse=True)
                            if n > 1:
                                pool.wait_ge(sem["probs_masked"], up("probs_masked", n - 1))
                                pool.nop(nofuse=True)
                            block_ = PT[SEG * w:SEG * (w + 1), t, :, SEG * w:SEG * (w + 1)]
                            pool.affine_select(out=block_, in_=block_, compare_op=ALU.is_ge, fill=0.0, base=0,
                                               pattern=[[0, HH], [1, SEG]], channel_multiplier=-1).then_inc(sem["probs_masked"], 1)
                pool.wait_ge(sem["probs_masked"], up("probs_masked", 16))
                pool.nop(nofuse=True)
                scales(1, False)
                for g in range(NG):
                    for n, (i, h0, k, w) in enumerate(EXP_JOBS):
                        pool.wait_ge(sem["probs1_made"], up("probs1_made", NEJ * g + n + 1))
                        pool.nop(nofuse=True)
                        at = PT_BASE[i] + w * h0
                        block_ = PT1[g % 2][:, at:at + w * k].rearrange("p (h q) -> p h q", h=k)[:, :, 0:P]
                        pool.affine_select(out=block_, in_=block_, compare_op=ALU.is_ge, fill=0.0, base=0,
                                           pattern=[[0, k], [1, P]], channel_multiplier=-1).then_inc(sem["probs1_masked"], 1)

        @block.vector
        def _(dve):
            done = [0]

            def prepare(ins_):
                done[0] += 1
                ins_.then_inc(s_set, 1)
                dve.wait_ge(s_set, done[0])

            dve.wait_ge(s_load, 16 * loads)
            gbc = place["gbc"]
            for c in range(H // 2):
                part = place["wkT"][:, P * c:P * (c + 1)]
                prepare(dve.tensor_tensor(part, part, gbc, ALU.mult))
            assert done[0] == SETUP_KEYS
            prepare(dve.tensor_scalar(gam8, gam, DH0 ** -0.5, None, ALU.mult))
            prepare(dve.reciprocal(rtemp, temp))
            prepare(dve.tensor_copy(identb[:, :], ident))
            prepare(dve.tensor_copy(mask0[:, :], place["mask0"]))
            prepare(dve.tensor_copy(mask1[:, :], place["mask1"]))
            prepare(dve.tensor_copy(selr[:, :, :], place["selr"].rearrange("p (a b) -> p a b", a=CH)))
            prepare(dve.tensor_copy(selw[:, :, :], place["selw"].rearrange("p (a b) -> p a b", a=NE)))
            prepare(dve.tensor_copy(selpm[:, :], place["selpm"]))
            prepare(dve.tensor_scalar(place["wv"], place["wv"], gam, None, ALU.mult))
            prepare(dve.tensor_scalar(place["qk1"][:, 0:2 * P], place["qk1"][:, 0:2 * P], DH1 ** -0.5, None, ALU.mult))
            for name, t in (("wv", wv), ("wg", wg), ("wu", wu), ("w1", w1), ("qk1", qk1)):
                full = tuple([slice(None)] * len(t[0].shape))
                src = place[name]
                if len(t[0].shape) == 3:
                    src = src.rearrange("p (a b) -> p a b", a=t[0].shape[1])
                prepare(dve.tensor_copy(t[0][full], src))
                prepare(dve.tensor_tensor(t[1][full], src, t[0][full].bitcast(F32), ALU.subtract))
            dve.wait_ge(s_setpe, 2)
            for n in range(4):
                src = banks[:, n, :].rearrange("p (a b) -> p a b", a=4)
                first = HH * (n % 2) + n // 2
                hi, lo = (t[:, first:HH * (n % 2 + 1):2, :] for t in aq)
                prepare(dve.tensor_scalar(hi, src, gam8, None, ALU.mult))
                prepare(dve.scalar_tensor_tensor(lo, src, gam8, hi.bitcast(F32), ALU.mult, ALU.subtract))
            for r in range(2):
                dst = gpm[:, :].rearrange("p (c r k) -> p c r k", c=H // 2, r=2)[:, :, r, :]
                prepare(dve.tensor_scalar(dst, banks[:, 4 + r, 0:P].rearrange("p (c k) -> p c k", k=PM), gam8, None, ALU.mult))
            prepare(dve.tensor_copy(gpm16[:, :], gpm[:, :]))
            assert done[0] == SETUP_ALL

            with dve.Fori(0, BATCH) as b:
                def up(name, n):
                    return b * PER[name] + START.get(name, 0) + n

                def norm(layer, src, dst, ready):
                    s, m, k = f"stats{layer}", f"moments{layer}", NT * layer
                    for t in range(NT):
                        dve.bn_stats(st[:, k + t, :], src[:, t, :]).then_inc(sem[s], 1)
                    dve.wait_ge(sem[s], up(s, NT))
                    dve.nop(nofuse=True)
                    for t in range(NT):
                        dve.bn_aggr(mv[:, k + t, :], st[:, k + t, :]).then_inc(sem[m], 1)
                    dve.wait_ge(sem[f"scales{layer}"], up(f"scales{layer}", 2))
                    for t in range(NT):
                        dve.tensor_scalar(dst[:, t, :], src[:, t, :], mv[:, k + t, 0:1], sc[:, 1, t:t + 1],
                                          ALU.subtract, ALU.mult).then_inc(sem[ready], 1)

                dve.wait_ge(sem["x_loaded"], up("x_loaded", 16))
                norm(0, x, xn, "xn_ready")
                dve.wait_ge(sem["scales0"], up("scales0", 6))
                dve.wait_ge(sem["stored"], up("stored", 0))
                for t in range(NT):
                    dve.wait_ge(sem["xn_ready"], up("xn_ready", t + 1))
                    dve.tensor_scalar(hn[:, t, :], xn[:, t, :], sc[:, 5, t:t + 1], None, ALU.mult).then_inc(sem["h_ready"], 1)

                def normalize(g):
                    dve.wait_ge(sem["o1_turned"], up("o1_turned", g + 1))
                    o = bank(("o1", g)).rearrange("p (t h c) -> p t h c", t=NT, h=GH)
                    dve.reciprocal(rdn[:, :, :], o[:, :, :, DH1]).then_inc(sem["o1_ready"], 1)
                    dve.wait_ge(sem["o1_ready"], up("o1_ready", 2 * g + 1))
                    dve.tensor_tensor(o1v[:, :, GH * g:GH * (g + 1), :], o[:, :, :, 0:DH1],
                                      rdn[:, :, :].rearrange("p t (h o) -> p t h o", o=1).broadcast_to([P, NT, GH, DH1]), ALU.mult)\
                        .then_inc(sem["o1_ready"], 1)

                def split(dst, src, s, n):
                    dve.tensor_copy(dst[0][:, :], src[:, :]).then_inc(sem[s], 1)
                    dve.wait_ge(sem[s], up(s, n))
                    dve.tensor_tensor(dst[1][:, :], src[:, :], dst[0][:, :].bitcast(F32), ALU.subtract).then_inc(sem[s], 1)

                dve.wait_ge(sem["xT_copied"], up("xT_copied", 1))
                split(xTs, xT, "splits0", 1)
                dve.wait_ge(sem["hT_copied"], up("hT_copied", 1))
                split(hTs, hT, "splits0", 3)
                dve.tensor_copy(hT16[:, :], hT[:, :]).then_inc(sem["splits0"], 1)

                count = [0]

                def step(name, ins_):
                    count[0] += 1
                    ins_.then_inc(sem[name], 1)
                    dve.wait_ge(sem[name], up(name, count[0]))

                R = [rt[:, i, :, :] for i in range(16)]
                T = [rw[:, i, :] for i in range(12)]

                def wide(t):
                    return t.rearrange("p (t o) -> p t o", o=1).broadcast_to([P, NT, NE])

                def route(ins_):
                    step("route0", ins_)

                dve.wait_ge(sem["z_made"], up("z_made", 1))
                route(dve.tensor_scalar(R[0], bank("z")[:, 0:NT * NE].rearrange("p (t e) -> p t e", t=NT), rtemp, None, ALU.mult))
                route(dve.tensor_scalar(R[2], R[0], LOGIT_LOWER, None, ALU.is_ge))
                route(dve.scalar_tensor_tensor(R[3], R[0], 0.0, R[2], ALU.is_le, ALU.mult))
                dve.wait_ge(sem["route_tanh"], up("route_tanh", 1))
                route(dve.tensor_scalar(R[7], R[1], 0.5, 0.5 - CENTER, ALU.mult, ALU.add))
                route(dve.scalar_tensor_tensor(R[4], R[7], -1.0, R[7], ALU.mult, ALU.min))
                dve.wait_ge(sem["route_exp"], up("route_exp", 2))
                route(dve.tensor_tensor(R[8], R[5], R[3], ALU.mult))
                route(dve.reduce_sum(T[0], R[8], AX))
                route(dve.tensor_scalar(T[1], T[0], 1e-8, None, ALU.is_lt))
                for k, (key, pick) in enumerate(((R[4], R[11]), (R[12], R[13]))):
                    route(dve.reduce_max(T[2], key, AX))
                    route(dve.tensor_tensor(R[9], key, wide(T[2]), ALU.is_equal))
                    route(dve.tensor_tensor(R[10], R[9], rank[:, :, :], ALU.mult))
                    route(dve.reduce_max(T[3], R[10], AX))
                    route(dve.tensor_tensor(pick, R[10], wide(T[3]), ALU.is_equal))
                    if k == 0:
                        route(dve.scalar_tensor_tensor(R[12], R[11], -4.0, R[4], ALU.mult, ALU.add))
                route(dve.tensor_tensor(R[11], R[11], R[13], ALU.add))
                route(dve.tensor_tensor(R[12], R[6], R[11], ALU.mult))
                route(dve.reduce_sum(T[4], R[12], AX))
                route(dve.tensor_scalar(T[5], T[4], 1e-8, None, ALU.max))
                route(dve.reciprocal(T[6], T[5]))
                route(dve.tensor_tensor(R[13], R[12], wide(T[6]), ALU.mult))
                route(dve.tensor_tensor(R[14], R[13], R[8], ALU.subtract))
                route(dve.tensor_tensor(R[9], R[14], wide(T[1]), ALU.mult))
                route(dve.tensor_tensor(R[10], R[9], R[8], ALU.add))
                route(dve.reduce_sum(T[7], R[10], AX))
                route(dve.tensor_scalar(T[8], T[7], 1e-8, None, ALU.max))
                route(dve.reciprocal(T[9], T[8]))
                route(dve.tensor_tensor(R[11], R[10], wide(T[9]), ALU.mult))
                route(dve.tensor_scalar(R[12], R[11], 0.5, None, ALU.mult))
                route(dve.tensor_copy(wp[:, :, 0:NE], R[12]))
                route(dve.tensor_tensor(R[13], R[12], wp[:, :, 0:NE], ALU.subtract))
                route(dve.tensor_copy(wp[:, :, NE:2 * NE], R[13]))
                route(dve.tensor_tensor(wp[:, :, 2 * NE:3 * NE], R[13], wp[:, :, NE:2 * NE], ALU.subtract))
                assert count[0] == PER["route0"], count
                count[0] = 0

                def glu_fn(e):
                    dve.wait_ge(sem["tanh_made"], up("tanh_made", e + 1))
                    if e:
                        dve.wait_ge(sem["glu_c"], up("glu_c", e))
                    dve.scalar_tensor_tensor(glu_[0], act[:, e % 2, :], 1.0, bank(("gate", e)), ALU.add, ALU.mult).then_inc(sem["glu_a"], 1)
                    dve.wait_ge(sem["up_made"], up("up_made", e + 1))
                    dve.wait_ge(sem["glu_a"], up("glu_a", e + 1))
                    dve.tensor_tensor(glu_[1], glu_[0], bank(("up", e)), ALU.mult).then_inc(sem["glu_b"], 1)
                    dve.wait_ge(sem["glu_b"], up("glu_b", e + 1))
                    if e >= 2:
                        dve.wait_ge(sem["down0_added"], up("down0_added", e - 1))
                    dve.tensor_tensor(glc[:, e % 2, :], glu_[1], bank(("wb", e)), ALU.mult).then_inc(sem["glu_c"], 1)

                glu_ = [glu[:, :], glu[:, :]]
                for a in range(2):
                    for h in range(HH):
                        dve.wait_ge(sem["q_copied"], up("q_copied", HH * a + h + 1))
                        if a and h == 0:
                            dve.wait_ge(sem["rough_made"], up("rough_made", NT))
                        dve.tensor_copy(q16[:, h, :], q32[:, h, :]).then_inc(sem["q16_made"], 1)
                    if a == 0:
                        dve.wait_ge(sem["wT_made"], up("wT_made", 1))
                        dve.tensor_copy(wT[:, :], bank("wT").bitcast(BF16)[0:24, 0:S]).then_inc(sem["wT_copied"], 1)
                    dve.wait_ge(sem["rough_pm_made"], up("rough_pm_made", a + 1))
                    count[0] = 9 * a
                    step("max0", dve.reduce_max(mx[:, 0, :, :], bank(("rough_pm", a)).rearrange("p (t h k) -> p t h k", t=NT, h=HH), AX))
                    for t in range(NT):
                        dve.wait_ge(sem["rough_made"], up("rough_made", NT * a + t + 1))
                        count[0] += 1
                        dve.reduce_max(mx[:, 1, t, :], bank(("rough", a, t)).rearrange("p (h k) -> p h k", h=HH), AX).then_inc(sem["max0"], 1)
                    dve.wait_ge(sem["max0"], up("max0", count[0]))
                    step("max0", dve.tensor_tensor(mx[:, 2, :, :], mx[:, 0, :, :], mx[:, 1, :, :], ALU.max))
                    step("max0", dve.tensor_copy(mp[:, :, 0, :], mx[:, 2, :, :]))
                    step("max0", dve.tensor_tensor(mx[:, 3, :, :], mx[:, 2, :, :], mp[:, :, 0, :], ALU.subtract))
                    step("max0", dve.tensor_copy(mp[:, :, 1, :], mx[:, 3, :, :]))
                    assert count[0] == 9 * (a + 1)
                    dve.wait_ge(sem["maxT_made"], up("maxT_made", a + 1))
                    if a:
                        dve.wait_ge(sem["max_stored"], up("max_stored", 16))
                        dve.wait_ge(sem["pm_scores"], up("pm_scores", 1))
                    dve.tensor_copy(mT[:, :], bank(("maxT", a)).bitcast(BF16)[0:2 * HH, 0:S]).then_inc(sem["maxT_copied"], 1)
                    for e in (4 * a, 4 * a + 1, 4 * a + 2):
                        glu_fn(e)
                    dve.wait_ge(sem["den_made"], up("den_made", a + 1))
                    if a:
                        dve.wait_ge(sem["spread_made"], up("spread_made", CH))
                    dve.wait_ge(sem["glu_c"], up("glu_c", 4 * a + 3))
                    count[0] = 3 * a
                    step("rden_made", dve.reciprocal(rd[:, :], bank(("den", a))))
                    step("rden_made", dve.tensor_copy(rds[0][:, :], rd[:, :]))
                    step("rden_made", dve.tensor_tensor(rds[1][:, :], rd[:, :], rds[0][:, :].bitcast(F32), ALU.subtract))
                    for c in range(CH):
                        n = CH * a + c
                        dve.wait_ge(sem["pv_made"], up("pv_made", n + 1))
                        dve.wait_ge(sem["spread_copied"], up("spread_copied", n + 1))
                        if n >= 2:
                            dve.wait_ge(sem["out0_added"], up("out0_added", n - 1))
                        dve.tensor_tensor(oT[:, c % 2, :], bank(("pv", a, c)), spread[:, c % 2, :], ALU.mult).then_inc(sem["oT_made"], 1)
                    glu_fn(4 * a + 3)

                dve.wait_ge(sem["y0_turned"], up("y0_turned", 1))
                dve.tensor_tensor(x1[:, :, :], x[:, :, :], bank("y0").rearrange("p (t d) -> p t d", t=NT), ALU.add)\
                    .then_inc(sem["x1_ready"], 1)
                dve.wait_ge(sem["x1_ready"], up("x1_ready", 1))
                norm(1, x1, xn, "xn1_ready")
                dve.wait_ge(sem["x1T_copied"], up("x1T_copied", 1))
                split(xTs, xT, "splits1", 1)
                for j in range(2):
                    count[0] = 7 * j
                    dve.wait_ge(sem["rope_in"], up("rope_in", 2 * j + 1))
                    step("rope", dve.tensor_tensor(tmp[:, 0, :], bank(("rope", 2 * j)), cos[:, :], ALU.mult))
                    dve.wait_ge(sem["rope_in"], up("rope_in", 2 * j + 2))
                    step("rope", dve.tensor_tensor(tmp[:, 1, :], bank(("rope", 2 * j + 1)), sin[:, :], ALU.mult))
                    step("rope", dve.tensor_tensor(tmp[:, 2, :], tmp[:, 0, :], tmp[:, 1, :], ALU.add))
                    step("rope", dve.tensor_copy(pq[:, j, 0, :], tmp[:, 2, :]))
                    step("rope", dve.tensor_tensor(tmp[:, 3, :], tmp[:, 2, :], pq[:, j, 0, :], ALU.subtract))
                    step("rope", dve.tensor_copy(pq[:, j, 1, :], tmp[:, 3, :]))
                    step("rope", dve.tensor_tensor(pq[:, j, 2, :], tmp[:, 3, :], pq[:, j, 1, :], ALU.subtract))
                count[0] = 0
                dve.wait_ge(sem["z1_made"], up("z1_made", 1))
                bgw = bg.rearrange("p (o e) -> p o e", o=1).broadcast_to([P, NT, NE])
                step("route1", dve.tensor_tensor(R[1], bank("z1")[:, 0:NT * NE].rearrange("p (t e) -> p t e", t=NT), bgw, ALU.add))
                step("route1", dve.reduce_max(T[0], R[1], AX))
                step("route1", dve.tensor_tensor(R[2], R[1], wide(T[0]), ALU.is_equal))
                step("route1", dve.tensor_tensor(R[3], R[2], rank[:, :, :], ALU.mult))
                step("route1", dve.reduce_max(T[1], R[3], AX))
                step("route1", dve.tensor_tensor(R[5], R[3], wide(T[1]), ALU.is_equal))
                dve.wait_ge(sem["pick_turned"], up("pick_turned", 1))
                step("route1", dve.tensor_copy(ohT, bank("pick")[0:NE, :]))
                step("route1", dve.tensor_scalar(gm, ohT, 1.0, -MASKED, ALU.subtract, ALU.mult))
                for g in range(NG):
                    for n, (t, h0, k, w) in enumerate(MAX_JOBS):
                        dve.wait_ge(sem["rough1_made"], up("rough1_made", NMJ * g + n + 1))
                        dve.reduce_max(mx1[:, 0, t, h0:h0 + k], bank(("rough1", g, n))[:, 0:w * k].rearrange("p (h k) -> p h k", h=k), AX)\
                            .then_inc(sem["max1"], 1)
                    dve.wait_ge(sem["max1"], up("max1", NMJ * (g + 1)))
                    count[0] = 3 * g
                    step("max1_parts", dve.tensor_copy(mp1[:, :, 0, :], mx1[:, 0, :, :]))
                    step("max1_parts", dve.tensor_tensor(mx1[:, 1, :, :], mx1[:, 0, :, :], mp1[:, :, 0, :], ALU.subtract))
                    step("max1_parts", dve.tensor_copy(mp1[:, :, 1, :], mx1[:, 1, :, :]))
                    dve.wait_ge(sem["maxT1_made"], up("maxT1_made", g + 1))
                    if g >= 2:
                        dve.wait_ge(sem[f"max1_stored{g % 2}"], up(f"max1_stored{g % 2}", 16 * (g // 2)))
                    dve.tensor_copy(mT1[:, g % 2, :], bank(("maxT1", g)).bitcast(BF16)[0:2 * GH, 0:S]).then_inc(sem["maxT1_copied"], 1)
                    if g:
                        normalize(g - 1)
                normalize(NG - 1)
                dve.wait_ge(sem["y1_turned"], up("y1_turned", 1))
                dve.tensor_tensor(yout[:, :, :], x1[:, :, :], bank("y1").rearrange("p (t d) -> p t d", t=NT), ALU.add)\
                    .then_inc(sem["out_ready"], 1)


SETUP_KEYS = H // 2
SETUP_ALL = SETUP_KEYS + 10 + 2 * 5 + 8 + 3
CLEARED = 8


def kernel(**inputs):
    import numpy as _np
    import concourse.bacc as _bacc
    from concourse import mybir as _mybir
    from concourse.bass_utils import run_bass_kernel_spmd as _run

    arrays = layout(inputs)
    nc = _bacc.Bacc("TRN2", target_bir_lowering=False, num_devices=1)
    ins, feed = {}, {}
    for name, a in arrays.items():
        feed[f"in_{name}"] = a
        ins[name] = nc.dram_tensor(f"in_{name}", a.shape, _mybir.dt.from_np(a.dtype), kind="ExternalInput").ap()
    out = nc.dram_tensor("out", (BATCH, S, P), F32, kind="ExternalOutput").ap()
    build(nc, ins, out)
    r = _run(nc, [feed], core_ids=[0])
    return r.results[0]["out"]


def layout(inputs):
    g = {k: np.asarray(v) for k, v in inputs.items()}

    def rows(a):
        return np.ascontiguousarray(a.transpose(1, 0, 2).reshape(a.shape[1], -1))

    out = {"x": np.ascontiguousarray(g["L0_attn_x"])}
    wqkv = g["L0_attn_w_qkv"]
    inner = H * DH0
    out["wv"] = np.ascontiguousarray(wqkv[:, 2 * inner:])
    out["wqT"] = rows(np.ascontiguousarray(wqkv[:, 0:inner].T).reshape(H // 2, P, P))
    out["wkT"] = rows(np.ascontiguousarray(wqkv[:, inner:2 * inner].T).reshape(H // 2, P, P))
    out["gbc"] = np.ascontiguousarray(np.broadcast_to(g["L0_attn_gamma"][None, :], (P, P)))
    pmk = g["L0_attn_pm_k"].reshape(H * PM, DH0).T
    out["pmkT"] = np.ascontiguousarray(np.concatenate([pmk, pmk], 0))
    out["wo0"] = rows(g["L0_attn_w_out"].reshape(H // 2, P, P))
    pmv = np.zeros((H // 2, HH, PM, 2, DH0), np.float32)
    for h in range(H):
        pmv[h // 2, h % HH, :, h % 2, :] = g["L0_attn_pm_v"][h]
    out["pmv"] = rows(pmv.reshape(H // 2, P, P))
    for name, key in (("wg", "L0_ffn_Wg"), ("wu", "L0_ffn_Wu"), ("wd", "L0_ffn_Wd"), ("w1", "L1_ffn_W1"), ("w2", "L1_ffn_W2")):
        out[name] = rows(g[key])
    w = g["L1_attn_w_qkv"].reshape(P, 3, P // 2, 2)
    q, k = w[:, 0], w[:, 1]
    out["qk1"] = np.ascontiguousarray(np.concatenate([a.reshape(P, P) for a in (q, q[:, :, ::-1], k, k[:, :, ::-1])], 1))
    col = [g["L0_attn_gamma"][:, None], np.zeros((P, 1), np.float32),
           np.broadcast_to(g["L0_ffn_temperature"][None, :], (P, 1)), np.zeros((P, 1), np.float32)]
    out["small"] = np.ascontiguousarray(np.concatenate(
        [w[:, 2].reshape(P, P), g["L1_attn_w_out"], np.eye(P, dtype=np.float32), g["L0_ffn_Wr"], g["L1_ffn_Wg"],
         np.broadcast_to(g["L1_ffn_bg"][None, :], (P, NE)), g["L1_ffn_b1"].T] + col, 1))
    out["b2"] = np.ascontiguousarray(g["L1_ffn_b2"])
    out["rank"] = np.tile(np.arange(NE, 0, -1, dtype=np.float32), (P, NT))
    r = np.arange(P)
    out["mask0"] = np.tile(np.where(np.arange(SEG)[None, :] > r[:, None] % SEG, MASKED, 0.0), (1, 1)).astype(np.float32)
    out["mask1"] = np.tile(np.where(r[None, :] > r[:, None], MASKED, 0.0), (1, NT)).astype(np.float32)
    out["selpm"] = np.where(np.arange(2 * HH)[:, None] % HH == r[None, :] // PM, -1.0, 0.0).astype(np.float32)
    out["selw"] = np.repeat(np.tile(np.eye(NE, dtype=np.float32), (3, 1)), P, 1)
    m = np.arange(32)
    out["esel"] = np.tile(np.concatenate([(m % 2 == c) for c in range(2)]).astype(np.float32), (P, 1))
    h8 = r // PM
    out["epm"] = np.concatenate([((h8[:, None] % 4 == j) & (h8[:, None] // 4 == m[None, :] % 2)) for j in range(4)], 1).astype(np.float32)
    selr = np.zeros((P, CH, 2, DH0), np.float32)
    for h in range(HH):
        selr[32 * (h % 4) + h // 4, h // 2, h % 2, :] = 1.0
    out["selr"] = selr.reshape(P, CH * P)
    inv = np.float32(1.0) / np.float32(10000.0) ** (np.arange(0, DH1, 2, dtype=np.float32) / np.float32(DH1))
    freqs = np.outer(np.arange(S, dtype=np.float32), inv).astype(np.float32)
    pair = (r % DH1) // 2
    out["cos"] = np.ascontiguousarray(np.cos(freqs).T[pair]).astype(np.float32)
    out["sin"] = np.ascontiguousarray(np.sin(freqs).T[pair] * np.where(r % 2 == 0, -1.0, 1.0)[:, None]).astype(np.float32)
    return out
```

```python
from contextlib import ExitStack
import math

import numpy as np

import concourse.bass as bass
from concourse import mybir

F32 = mybir.dt.float32
F32R = mybir.dt.float32r
BF16 = mybir.dt.bfloat16
F16 = mybir.dt.float16
ALU = mybir.AluOpType
ACT = mybir.ActivationFunctionType
AX = mybir.AxisListType.X

P = 128
BATCH = 8
S = 512
NT = S // P
H = 16
DH0 = 64
DH1 = P // H
SEG = 64
PM = 16
HH = H // 2
CH = HH // 2
NE = 8
GH = 4
NG = H // GH
VW = 32
NB = 7
MASKED = -1e30
CENTER = 1.0 / math.e
LOWER = 0.5 - math.log(4.0 / 3.0)
LOGIT_LOWER = math.log(LOWER / (1.0 - LOWER))
MROW = 96
TERMS_Q = [(0, 3, 0, 0), (3, 2, 1, 0), (5, 1, 2, 0)]
TERMS_K = [(0, 3, 0, 1), (3, 2, 0, 1), (5, 1, 0, 1)]


def key_widths():
    return [S - P * i for i in range(NT)]


def sized_jobs(widths, order):
    out = []
    for i in order:
        k = min(GH, 512 // widths[i]) if widths[i] <= 256 else 1
        out += [(i, h, k, widths[i]) for h in range(0, GH, k)]
    return out


MAX_JOBS = sized_jobs([P * (i + 1) for i in range(NT)], range(NT))
EXP_JOBS = sized_jobs(key_widths(), range(NT))
NMJ, NEJ = len(MAX_JOBS), len(EXP_JOBS)
PT_BASE = [GH * sum(key_widths()[:i]) for i in range(NT)]
PT_SIZE = GH * sum(key_widths())

PER = {
    "x_loaded": 16, "residual_loaded": 16, "stats0": 4, "moments0": 4, "scales0": 6, "xn_ready": 4, "h_ready": 4,
    "xT_made": 1, "hT_made": 1, "xT_copied": 1, "hT_copied": 1, "h_splits": 3, "x_splits": 2,
    "z_made": 1, "route0": 37, "route_tanh": 1, "route_exp": 2, "wT_made": 1, "wT_copied": 1,
    "v_made": 8, "v_copied": 8, "q_made": 16, "q_copied": 16, "q16_made": 16,
    "rough_made": 8, "rough_pm_made": 2, "max0": 18, "maxT_made": 2, "maxT_copied": 2, "max_stored": 32, "max_rows": 32,
    "pm_scores": 2, "pm_probs": 2, "pt_zeroed": 2, "scores_made": 8, "probs_made": 16, "probs_masked": 16,
    "den_made": 2, "rden_made": 6, "spread_made": 8, "spread_copied": 8, "pv_made": 8, "oT_made": 8,
    "out0_added": 8, "wb_made": 8, "gate_made": 8, "up_made": 8, "tanh_made": 8,
    "glu_a": 8, "glu_b": 8, "glu_c": 8, "down0_added": 8,
    "y0_copied": 1, "y0_turned": 1, "x1_ready": 1,
    "stats1": 4, "moments1": 4, "scales1": 2, "xn1_ready": 4, "x1T_made": 1, "x1T_copied": 1, "splits1": 2,
    "z1_made": 1, "route1": 8, "pick_turned": 1, "rope_in": 4, "rope": 14, "parts_stored": 32,
    "parts_loaded0": 2 * 192, "parts_loaded1": 192, "parts_loaded2": 192, "v1_filled": 2, "v1_made": 1, "v1_copied": 1, "rough1_made": NMJ * NG, "max1": NMJ * NG,
    "max1_parts": 3 * NG, "maxT1_made": NG, "maxT1_copied": NG, "max1_stored0": 8 * NG, "max1_stored1": 8 * NG, "max1_rows0": 8 * NG, "max1_rows1": 8 * NG,
    "scores1_made": NEJ * NG, "probs1_made": NEJ * NG, "probs1_masked": NEJ * NG,
    "values1_made": NEJ * NG, "pv1_copied": NG, "o1_turned": NG, "o1_ready": 2 * NG, "ocT_made": 1, "ocT_copied": 1,
    "out1_added": 1, "hidden_made": 8, "gelu_made": 8, "down1_added": 8, "y1_copied": 1, "y1_turned": 1,
    "out_ready": 1, "stored": 16,
}


N1 = NMJ * NG
S_LAG = 18
V_LAG = S_LAG + 3
SLOTS = N1 + V_LAG + 3
RING = 8
LOADED = 3
TURN_X, TURN_Z = 12, 14


def maxima_slot(g):
    return NMJ * g + NMJ - 1


def values_slot(g):
    return NMJ * g + NMJ - 1 + V_LAG


def bank_plan():
    jobs = []

    def expert(e):
        return [(("wb", e), "glu_c", e + 1), (("gate", e), "glu_a", e + 1), (("up", e), "glu_b", e + 1)]

    def q_jobs(a, heads, ahead):
        return [(("q", a, h), "q_copied", HH * a + h + 1 + ahead * PER["q_copied"]) for h in heads]

    def v_jobs(a, tiles, ahead):
        return [(("v", a, t), "v_copied", NT * a + t + 1 + ahead * PER["v_copied"]) for t in tiles]

    for a in range(2):
        jobs += v_jobs(a, range(NT), 0) + q_jobs(a, range(HH), 0) if a else []
        jobs += [(("rough_pm", a), "max0", 9 * a + 1)]
        jobs += [(("rough", a, t), "max0", 9 * a + 2 + t) for t in range(NT)]
        jobs += expert(4 * a)
        jobs += [(("maxT", a), "maxT_copied", a + 1)]
        jobs += expert(4 * a + 1)
        jobs += [(("pm_scores", a), "pm_probs", a + 1)]
        jobs += [(("scores", a, t), "probs_made", 8 * a + 2 * t + 2) for t in range(NT)]
        jobs += [("hT", "hT_copied", 1 + PER["hT_copied"])] if a else []
        jobs += expert(4 * a + 2)
        jobs += [(("den", a), "rden_made", 3 * a + 1)]
        jobs += expert(4 * a + 3)
        for c in range(CH):
            jobs += [(("spread", a, c), "spread_copied", 4 * a + c + 1), (("pv", a, c), "oT_made", 4 * a + c + 1)]
    jobs += q_jobs(0, range(Q_FIRST), 1)
    jobs += [("y0", "x1_ready", 1)]
    jobs += q_jobs(0, range(Q_FIRST, HH), 1)
    jobs += [("x1T", "x1T_copied", 1), ("z1", "route1", 1), ("v1", "v1_copied", 1), ("pick", "route1", 7)]
    jobs += [(("rope", j), "rope", (1, 2, 8, 9)[j]) for j in range(4)]
    jobs += [(("hidden", e), "gelu_made", e + 1) for e in range(NE)]
    for slot in range(SLOTS):
        if slot < N1:
            jobs += [(("rough1", slot), "max1", slot + 1)]
        if 0 <= slot - S_LAG < N1:
            jobs += [(("scores1", slot - S_LAG), "probs1_made", slot - S_LAG + 1)]
        if 0 <= slot - V_LAG < N1 and (slot - V_LAG) % NEJ == 0:
            jobs += [(("pv1", (slot - V_LAG) // NEJ), "pv1_copied", (slot - V_LAG) // NEJ + 1)]
        jobs += [("xT", "xT_copied", 1 + PER["xT_copied"])] if slot == TURN_X else []
        jobs += [("z", "route0", 1 + PER["route0"])] if slot == TURN_Z else []
        for g in range(NG):
            jobs += [(("maxT1", g), "maxT1_copied", g + 1)] if slot == maxima_slot(g) + 2 else []
            jobs += [(("o1", g), "o1_ready", 2 * g + 2)] if slot == values_slot(g) + 1 else []
    jobs += v_jobs(0, range(2), 1) + [("ocT", "ocT_copied", 1)] + v_jobs(0, range(2, NT), 1)
    jobs += [("wT", "wT_copied", 1 + PER["wT_copied"]), ("y1", "out_ready", 1)]
    plan, age, last, held = {}, list(range(NB)), {}, set()
    for job, sem, count in jobs:
        bank = next(k for k in age if k not in held)
        if job[0] == "pv1":
            held.add(bank)
        if job[0] == "o1":
            held.discard(plan["pv1", job[1]][0])
        age.remove(bank)
        age.append(bank)
        plan[job] = (bank, last.get(bank))
        last[bank] = (sem, count)
    for job, (bank, before) in plan.items():
        if before is None:
            plan[job] = (bank, (last[bank][0], last[bank][1] - PER[last[bank][0]]))
    return plan


Q_FIRST = 3
PLAN = bank_plan()

START = {"x1_ready": 1, "stored": 1, "y1_turned": 1, "y1_copied": 1}
START.update({sem: PER[sem] for bank, (sem, count) in PLAN.values() if count <= 0})


def build(nc, ins, out):
    plan = PLAN
    with ExitStack() as ctx:
        def sb(name, shape, dt):
            return ctx.enter_context(nc.sbuf_tensor(name, shape, dt))

        sem = {name: ctx.enter_context(nc.semaphore(name)) for name in PER}
        s_load = ctx.enter_context(nc.semaphore("weights_loaded"))
        s_set = ctx.enter_context(nc.semaphore("weights_prepared"))
        s_setpe = ctx.enter_context(nc.semaphore("folded_weights_made"))
        s_clear = ctx.enter_context(nc.semaphore("buffers_cleared"))

        banks = ctx.enter_context(nc.psum_tensor("banks", [P, 8, 512], F32))
        ysum = banks[:, NB, :]

        def bank(job):
            return banks[:, plan[job][0], :]

        aq = [sb(f"aq{i}", [P, H, P], F32R) for i in range(2)]
        wv = [sb(f"wv{i}", [P, H * DH0], F32R) for i in range(2)]
        wg = [sb(f"wg{i}", [P, NE, P], F32R) for i in range(2)]
        wu = [sb(f"wu{i}", [P, NE, P], F32R) for i in range(2)]
        w1 = [sb(f"w1{i}", [P, NE, P], F32R) for i in range(2)]
        qk1 = [sb(f"qk1{i}", [P, 4, P], F32R) for i in range(2)]
        wo0 = sb("wo0", [P, H // 2, P], F32)
        wd = sb("wd", [P, NE, P], F32)
        w2 = sb("w2", [P, NE, P], F32)
        gpm = sb("gpm", [P, H * PM], F32)
        gpm16 = sb("gpm16", [P, H * PM], F16)
        pmv = sb("pmv", [P, H // 2, P], F32)
        small = sb("small", [P, 3 * P + 8 + 8 + 8 + 8 + 4], F32)
        wv1, wo1, ident = small[:, 0:P], small[:, P:2 * P], small[:, 2 * P:3 * P]
        wr = small[:, 3 * P:3 * P + 8]
        wgate = small[:, 3 * P + 8:3 * P + 16]
        bg = small[:, 3 * P + 16:3 * P + 24]
        b1T = small[:, 3 * P + 24:3 * P + 32]
        gam, gam8, temp, rtemp = (small[:, 3 * P + 32 + i:3 * P + 33 + i] for i in range(4))
        b2 = sb("b2", [NE, P], F32)
        rank = sb("rank", [P, NT, NE], F32)
        esel = sb("esel", [P, 2, 32], F32)
        epm = sb("epm", [P, 4, 32], F32)
        cos = sb("cos", [P, S], F32)
        sin = sb("sin", [P, S], F32)
        identb = sb("identb", [P, P], BF16)
        mask0 = sb("mask0", [P, SEG], BF16)
        mask1 = sb("mask1", [P, S], BF16)
        selr = sb("selr", [P, CH, P], F32R)
        selw = sb("selw", [24, NE, P], BF16)
        selpm = sb("selpm", [2 * HH, P], BF16)
        neg = sb("neg", [P, SEG], BF16)
        QS = sb("QS", [P, LOADED, GH, S], BF16)
        KS = sb("KS", [P, LOADED, GH, S], BF16)
        QS8 = QS[:, 0:2, :, :].rearrange("p a h t -> p (a h) t")

        big = sb("big", [P, 12288], F32)
        q32 = big[:, 0:4096].rearrange("p (h t) -> p h t", h=HH)
        q16 = big[:, 4096:6144].bitcast(F16).rearrange("p (h t) -> p h t", h=HH)
        v = big[:, 6144:8192].rearrange("p (t n) -> p t n", t=NT)
        PT = big[:, 8192:12288].rearrange("p (t h q) -> p t h q", t=NT, h=HH)
        v1 = big[:, 6144:8192].rearrange("p (t h c) -> p t h c", t=NT, h=H)
        ring = big[:, 8192:12288].rearrange("p (n q) -> p n q", n=RING)
        tmp = big[:, 8192:8192 + 4 * S].rearrange("p (a t) -> p a t", a=4)
        pq = big[:, 8192 + 4 * S:8192 + 7 * S].bitcast(BF16).rearrange("p (j a t) -> p j a t", j=2, a=3)

        xin = sb("xin", [P, NT, P], F32)
        x = sb("x", [P, NT, P], F32)
        x1 = sb("x1", [P, NT, P], F32)
        xn = sb("xn", [P, NT, P], F32)
        hn = sb("hn", [P, NT, P], F32)
        xT = sb("xT", [P, S], F32)
        hT = sb("hT", [P, S], F32)
        xTs = [sb(f"xTs{i}", [P, S], F32R) for i in range(2)]
        hTs = [sb(f"hTs{i}", [P, S], F32R) for i in range(2)]
        hT16 = sb("hT16", [P, S], F16)
        st = sb("st", [P, 2 * NT, 6], F32)
        mv = sb("mv", [P, 2 * NT, 2], F32)
        sc = sb("sc", [P, 6, NT], F32)
        half = sb("half", [P, NT], F32)
        rt = sb("rt", [P, 16, NT, NE], F32)
        rw = sb("rw", [P, 12, NT], F32)
        wp = sb("wp", [P, NT, 24], BF16)
        wT = sb("wT", [24, S], BF16)
        mx = sb("mx", [P, 4, NT, HH], F32)
        mp = sb("mp", [P, NT, 2, HH], BF16)
        mT = sb("mT", [2 * HH, S], BF16)
        ppm = sb("ppm", [P, S], F32)
        rds = [sb(f"rds{i}", [P, S], F32R) for i in range(2)]
        spread = sb("spread", [P, 2, S], F32)
        oT = sb("oT", [P, 2, S], F32)
        act = sb("act", [P, 2, S], F32)
        glu = sb("glu", [P, S], F32)
        rd = glu
        glc = sb("glc", [P, 2, S], F32)
        yT = act[:, 0, :]
        xn1 = yout = hn
        ocT = spread[:, 1, :]
        ohT = glu[0:NE, :]
        gm = ppm[0:NE, 0:S // 2].bitcast(BF16)
        mT1 = glc[0:2 * GH, 0, :].bitcast(BF16).rearrange("p (a t) -> p a t", a=2)
        o1v = spread[:, 0, :].rearrange("p (t h d) -> p t h d", t=NT, h=H)
        rdn = sb("rdn", [P, NT, GH], F32)
        mx1 = sb("mx1", [P, 2, NT, GH], F32)
        mp1 = sb("mp1", [P, NT, 2, GH], BF16)
        ov = oT
        scratch = nc.dram_tensor("scratch", [2, 3, P, S], BF16, kind="Internal").ap()

        mrows0 = nc.dram_tensor("mrows0", [2, 2, HH, S], BF16, kind="Internal").ap()
        mrows1 = nc.dram_tensor("mrows1", [NG, 2, GH, S], BF16, kind="Internal").ap()

        x_d, out_d = ins["x"], out
        staged = ["wv", "wg", "wu", "w1", "qk1", "wqT", "wkT", "gbc", "pmkT", "mask0", "mask1", "selr", "selw", "selpm"]
        direct = {"wo0": wo0, "wd": wd, "w2": w2, "pmv": pmv, "small": small[:, 0:3 * P + 36], "b2": b2,
                  "rank": rank, "esel": esel, "epm": epm, "cos": cos, "sin": sin}
        at, place = 0, {}
        for name in staged:
            rows, cols = ins[name].shape
            place[name] = big[0:rows, at:at + cols]
            at += cols
        assert at <= 12288
        loads = len(staged) + len(direct)

        block = ctx.enter_context(nc.Block())

        @block.sync
        def _(sp):
            for name in staged:
                sp.dma_start(place[name], ins[name]).then_inc(s_load, 16)
            for name, t in direct.items():
                dst = t if name == "small" else t[tuple([slice(None)] * len(t.shape))]
                src = ins[name]
                if len(dst.shape) == 3:
                    src = src.rearrange("p (a b) -> p a b", a=dst.shape[1])
                sp.dma_start(dst, src).then_inc(s_load, 16)
            for name, n in START.items():
                sp.sem_inc(sem[name], n)
            sp.dma_start(xin[:, :, :], x_d[0].rearrange("(t p) d -> p t d", p=P)).then_inc(sem["x_loaded"], 16)
            with sp.Fori(0, BATCH) as b:
                def up(name, n):
                    return b * PER[name] + START.get(name, 0) + n

                sp.wait_ge(sem["x1_ready"], up("x1_ready", 0))
                sp.dma_start(x[:, :, :], x_d[bass.ds(b, 1), :, :].rearrange("a (t p) d -> p (a t) d", p=P)).then_inc(sem["residual_loaded"], 16)
                sp.wait_ge(sem["xn_ready"], up("xn_ready", NT))
                sp.dma_start(xin[:, :, :], x_d[bass.ds(b + 1, 1), :, :].rearrange("a (t p) d -> p (a t) d", p=P)).then_inc(sem["x_loaded"], 16)
                for a in range(2):
                    sp.wait_ge(sem["maxT_copied"], up("maxT_copied", a + 1))
                    if a:
                        sp.wait_ge(sem["scores_made"], up("scores_made", NT * a))
                    sp.dma_start(mrows0[a].rearrange("j h t -> (j h) t"), mT[:, :]).then_inc(sem["max_stored"], 16)
                    sp.wait_ge(sem["max_stored"], up("max_stored", 16 * (a + 1)))
                    sp.dma_start(QS8[MROW:MROW + 2, :, :], mrows0[a]).then_inc(sem["max_rows"], 16)
                for j in range(2):
                    sp.wait_ge(sem["rope"], up("rope", 7 * (j + 1)))
                    sp.dma_start(scratch[j].rearrange("a p t -> p a t"), pq[:, j, :, :]).then_inc(sem["parts_stored"], 16)
                sp.wait_ge(sem["parts_stored"], up("parts_stored", 32))

                def load_group(g):
                    for j, (dst, terms) in enumerate(((QS, TERMS_Q), (KS, TERMS_K))):
                        for first, n, p0, step in terms:
                            for m in range(n):
                                src = scratch[j, p0 + step * m].rearrange("(h d) t -> d h t", d=DH1)
                                r = DH1 * (first + m)
                                sp.dma_start(dst[r:r + DH1, g % LOADED, :, :], src[:, GH * g:GH * (g + 1), :])\
                                    .then_inc(sem[f"parts_loaded{g % LOADED}"], 16)

                def rows_group(g):
                    sp.wait_ge(sem["maxT1_copied"], up("maxT1_copied", g + 1))
                    sp.dma_start(mrows1[g].rearrange("j h t -> (j h) t"), mT1[:, g % 2, :]).then_inc(sem[f"max1_stored{g % 2}"], 16)
                    sp.wait_ge(sem[f"max1_stored{g % 2}"], up(f"max1_stored{g % 2}", 16 * (g // 2 + 1)))
                    sp.dma_start(QS[MROW:MROW + 2, g % LOADED, :, :], mrows1[g]).then_inc(sem[f"max1_rows{g % 2}"], 16)

                for g in range(LOADED):
                    load_group(g)
                for g in range(NG):
                    rows_group(g)
                    if g + 2 >= LOADED and g + 2 < NG:
                        sp.wait_ge(sem["scores1_made"], up("scores1_made", NEJ * (g + 3 - LOADED)))
                        load_group(g + 2)
                sp.wait_ge(sem["out_ready"], up("out_ready", 1))
                sp.dma_start(out_d[bass.ds(b, 1), :, :].rearrange("a (t p) d -> p (a t) d", p=P), yout[:, :, :]).then_inc(sem["stored"], 16)
            sp.wait_ge(sem["stored"], BATCH * PER["stored"] + START["stored"])


        @block.tensor
        def _(pe):
            pe.wait_ge(s_load, 16 * loads)
            pe.wait_ge(s_set, SETUP_KEYS)
            for h in range(H):
                r, c = DH0 * (h % 2), h // 2
                rows = slice(r, r + DH0)
                mm = pe.matmul(banks[:, 2 * (h % 2) + c // 4, P * (c % 4):P * (c % 4) + P], place["wqT"][rows, P * c:P * c + P],
                               place["wkT"][rows, P * c:P * c + P], start=True, stop=True)
            mm.then_inc(s_setpe, 1)
            for h in range(H):
                r, c = DH0 * (h % 2), h // 2
                rows = slice(r, r + DH0)
                mm = pe.matmul(banks[:, 4 + h % 2, PM * c:PM * (c + 1)], place["wqT"][rows, P * c:P * c + P],
                               place["pmkT"][rows, PM * h:PM * (h + 1)], start=True, stop=True)
            mm.then_inc(s_setpe, 1)
            pe.wait_ge(s_set, SETUP_ALL)
            pe.wait_ge(s_clear, CLEARED)


            def three(o, w, m, first=True, last=True):
                pe.matmul(o, w[0], m[0], start=first, stop=False, skip_group_check=True)
                pe.matmul(o, w[1], m[0], start=False, stop=False, skip_group_check=True)
                return pe.matmul(o, w[0], m[1], start=False, stop=last, skip_group_check=True)

            def turn(o, src, wait, dt=F32, rows=P):
                o = o if dt == F32 else o.bitcast(BF16)
                for t in range(NT):
                    wait(t)
                    mm = pe.transpose(o[0:rows, P * t:P * (t + 1)], src(t), (ident if dt == F32 else identb[:, :]))
                return mm

            def turn_h(up, claim):
                turn(claim("hT"), lambda t: hn[:, t, :], lambda t: pe.wait_ge(sem["h_ready"], up("h_ready", t + 1)))\
                    .then_inc(sem["hT_made"], 1)

            def queries(up, claim, a, heads):
                pe.wait_ge(sem["h_splits"], up("h_splits", 2))
                for h in heads:
                    o = claim(("q", a, h))
                    three(o, [w[:, HH * a + h, :] for w in aq], [m[:, :] for m in hTs]).then_inc(sem["q_made"], 1)

            def values0(up, claim, a, tiles):
                for t in tiles:
                    o = claim(("v", a, t))
                    three(o, [m[:, P * t:P * (t + 1)] for m in hTs], [w[:, S * a:S * (a + 1)] for w in wv])\
                        .then_inc(sem["v_made"], 1)

            def turn_x(up, claim):
                turn(claim("xT"), lambda t: xn[:, t, :], lambda t: pe.wait_ge(sem["xn_ready"], up("xn_ready", t + 1)))\
                    .then_inc(sem["xT_made"], 1)

            def route_product(up, claim):
                z = claim("z")
                pe.wait_ge(sem["xT_copied"], up("xT_copied", 1))
                for t in range(NT):
                    mm = pe.matmul(z[:, NE * t:NE * (t + 1)], xT[:, P * t:P * (t + 1)], wr, start=True, stop=True)
                mm.then_inc(sem["z_made"], 1)

            def turn_weights(up, claim):
                turn(claim("wT"), lambda t: wp[:, t, :], lambda t: pe.wait_ge(sem["route0"], up("route0", PER["route0"])) if t == 0 else None,
                     BF16, rows=24).then_inc(sem["wT_made"], 1)

            def up_first(name, n):
                return START.get(name, 0) + n

            freed = {}

            def claim_first(job):
                before = freed.get(plan[job][0])
                if before:
                    pe.wait_ge(sem[before[0]], up_first(*before))
                name = job if isinstance(job, str) else job[0]
                freed[plan[job][0]] = {"hT": ("hT_copied", 1), "xT": ("xT_copied", 1), "z": ("route0", 1), "wT": ("wT_copied", 1),
                                       "q": ("q_copied", job[-1] + 1 if name == "q" else 0),
                                       "v": ("v_copied", job[-1] + 1 if name == "v" else 0)}[name]
                return bank(job)

            turn_h(up_first, claim_first)
            queries(up_first, claim_first, 0, range(HH))
            turn_x(up_first, claim_first)
            route_product(up_first, claim_first)
            values0(up_first, claim_first, 0, range(NT))
            turn_weights(up_first, claim_first)
            for name, n in (("q_copied", HH), ("v_copied", NT), ("xT_copied", 1), ("wT_copied", 1)):
                pe.wait_ge(sem[name], up_first(name, n))

            with pe.Fori(0, BATCH) as b:
                def up(name, n):
                    return b * PER[name] + START.get(name, 0) + n

                def up_next(name, n):
                    return up(name, n + PER[name])

                def claim(job):
                    before = plan[job][1]
                    pe.wait_ge(sem[before[0]], up(*before))
                    return bank(job)

                def expert0(e):
                    o = claim(("wb", e))
                    pe.wait_ge(sem["wT_copied"], up("wT_copied", 1))
                    pe.matmul(o, selw[:, e, :], wT[:, :], start=True, stop=True).then_inc(sem["wb_made"], 1)
                    o = claim(("gate", e))
                    pe.wait_ge(sem["x_splits"], up("x_splits", 2))
                    three(o, [w[:, e, :] for w in wg], [m[:, :] for m in xTs]).then_inc(sem["gate_made"], 1)
                    o = claim(("up", e))
                    three(o, [w[:, e, :] for w in wu], [m[:, :] for m in xTs]).then_inc(sem["up_made"], 1)
                    if e:
                        down0(e - 1)

                def down0(e):
                    pe.wait_ge(sem["glu_c"], up("glu_c", e + 1))
                    if e == 0:
                        pe.wait_ge(sem["y1_copied"], up("y1_copied", 0))
                    pe.matmul(ysum, wd[:, e, :], glc[:, e % 2, :], start=(e == 0), stop=(e == NE - 1),
                              skip_group_check=True).then_inc(sem["down0_added"], 1)

                def down1(e):
                    pe.wait_ge(sem["gelu_made"], up("gelu_made", e + 1))
                    pe.matmul(ysum, w2[:, e, :], act[:, e % 2, :], start=False, stop=False, skip_group_check=True)\
                        .then_inc(sem["down1_added"], 1)

                def out0(a, c):
                    pe.wait_ge(sem["oT_made"], up("oT_made", CH * a + c + 1))
                    pe.matmul(ysum, wo0[:, CH * a + c, :], oT[:, c % 2, :], start=False, stop=False,
                              skip_group_check=True).then_inc(sem["out0_added"], 1)

                for a in range(2):
                    if a:
                        values0(up, claim, a, range(NT))
                        queries(up, claim, a, range(HH))
                    o = claim(("rough_pm", a))
                    pe.wait_ge(sem["h_splits"], up("h_splits", 3))
                    for t in range(NT):
                        mm = pe.matmul(o[:, P * t:P * (t + 1)], hT16[:, P * t:P * (t + 1)],
                                       gpm16[:, P * a:P * (a + 1)], start=True, stop=True)
                    mm.then_inc(sem["rough_pm_made"], 1)
                    for t in range(NT):
                        o = claim(("rough", a, t))
                        pe.matmul(o.rearrange("p (h k) -> p h k", h=HH), identb[:, :],
                                  mask0[:, :].rearrange("p (o k) -> p o k", o=1).broadcast_to([P, HH, SEG]),
                                  start=True, stop=False, skip_group_check=True)
                        for h in range(HH):
                            if t == 0:
                                pe.wait_ge(sem["q16_made"], up("q16_made", HH * a + h + 1))
                            for w in range(2):
                                k = P * t + SEG * w
                                mm = pe.matmul(o[SEG * w:SEG * (w + 1), SEG * h:SEG * (h + 1)], q16[:, h, k:k + SEG],
                                               hT16[:, k:k + SEG], start=False, stop=(h == HH - 1), skip_group_check=True)
                        mm.then_inc(sem["rough_made"], 1)
                    expert0(4 * a)
                    turn(claim(("maxT", a)), lambda t: mp[:, t, :, :].rearrange("p c h -> p (c h)"),
                         lambda t: pe.wait_ge(sem["max0"], up("max0", 9 * (a + 1))) if t == 0 else None,
                         BF16, rows=2 * HH).then_inc(sem["maxT_made"], 1)
                    expert0(4 * a + 1)
                    o = claim(("pm_scores", a))
                    pe.wait_ge(sem["maxT_copied"], up("maxT_copied", a + 1))
                    pe.matmul(o, selpm[:, :], mT[:, :], start=True, stop=False, skip_group_check=True)
                    pe.matmul(o, gpm[:, P * a:P * (a + 1)], hT[:, :], start=False, stop=True, skip_group_check=True)\
                        .then_inc(sem["pm_scores"], 1)
                    pe.wait_ge(sem["max_rows"], up("max_rows", 16 * (a + 1)))
                    for t in range(NT):
                        o = claim(("scores", a, t))
                        for w in range(2):
                            k = P * t + SEG * w
                            pe.matmul(o[SEG * w:SEG * (w + 1), :].rearrange("p (h q) -> p h q", h=HH), neg[0:MROW + 2, :],
                                      QS8[0:MROW + 2, :, k:k + SEG], start=True, stop=False, skip_group_check=True)
                        for w in range(2):
                            k = P * t + SEG * w
                            mm = pe.matmul(o[SEG * w:SEG * (w + 1), :].rearrange("p (h q) -> p h q", h=HH), hT[:, k:k + SEG],
                                           q32[:, :, k:k + SEG], start=False, stop=True, skip_group_check=True)
                        mm.then_inc(sem["scores_made"], 1)
                    if a:
                        turn_h(up_next, claim)
                    expert0(4 * a + 2)
                    o = claim(("den", a))
                    pe.wait_ge(sem["pm_probs"], up("pm_probs", a + 1))
                    for j in range(4):
                        pe.matmul(o[32 * j:32 * j + 32, :], epm[:, j, :], ppm[:, :], start=True, stop=False,
                                  skip_group_check=True)
                    for t in range(NT):
                        pe.wait_ge(sem["probs_masked"], up("probs_masked", 8 * a + 2 * t + 2))
                        for h in range(HH):
                            j = h % 4
                            mm = pe.matmul(o[32 * j:32 * j + 32, P * t:P * (t + 1)], esel[:, h // 4, :], PT[:, t, h, :],
                                           start=False, stop=(h >= 4), skip_group_check=True)
                    mm.then_inc(sem["den_made"], 1)
                    expert0(4 * a + 3)
                    for c in range(CH):
                        o = claim(("spread", a, c))
                        if c == 0:
                            pe.wait_ge(sem["rden_made"], up("rden_made", 3 * (a + 1)))
                        pe.matmul(o, selr[:, c, :], rds[0][:, :], start=True, stop=False, skip_group_check=True)
                        pe.matmul(o, selr[:, c, :], rds[1][:, :], start=False, stop=True, skip_group_check=True)\
                            .then_inc(sem["spread_made"], 1)
                        o = claim(("pv", a, c))
                        if c == 0:
                            pe.wait_ge(sem["v_copied"], up("v_copied", NT * (a + 1)))
                        pe.matmul(o, pmv[:, CH * a + c, :], ppm[:, :], start=True, stop=False, skip_group_check=True)
                        for t in range(NT):
                            for r in range(2):
                                h = 2 * c + r
                                mm = pe.matmul(o[DH0 * r:DH0 * (r + 1), P * t:P * (t + 1)], v[:, t, DH0 * h:DH0 * (h + 1)],
                                               PT[:, t, h, :], start=False, stop=True, skip_group_check=True)
                        mm.then_inc(sem["pv_made"], 1)
                        if c:
                            out0(a, c - 1)
                    out0(a, CH - 1)
                down0(NE - 1)
                queries(up_next, claim, 0, range(Q_FIRST))
                turn(claim("y0"), lambda t: yT[:, P * t:P * (t + 1)],
                     lambda t: pe.wait_ge(sem["y0_copied"], up("y0_copied", 1)) if t == 0 else None).then_inc(sem["y0_turned"], 1)
                queries(up_next, claim, 0, range(Q_FIRST, HH))

                turn(claim("x1T"), lambda t: xn1[:, t, :], lambda t: pe.wait_ge(sem["xn1_ready"], up("xn1_ready", t + 1)))\
                    .then_inc(sem["x1T_made"], 1)
                o = claim("z1")
                pe.wait_ge(sem["x1T_copied"], up("x1T_copied", 1))
                for t in range(NT):
                    mm = pe.matmul(o[:, NE * t:NE * (t + 1)], xT[:, P * t:P * (t + 1)], wgate, start=True, stop=True)
                mm.then_inc(sem["z1_made"], 1)
                o = claim("v1")
                for t in range(NT):
                    mm = pe.matmul(o[:, P * t:P * (t + 1)], xT[:, P * t:P * (t + 1)], wv1, start=True, stop=True)
                mm.then_inc(sem["v1_made"], 1)
                turn(claim("pick"), lambda t: rt[:, 5, t, :],
                     lambda t: pe.wait_ge(sem["route1"], up("route1", 6)) if t == 0 else None, rows=NE).then_inc(sem["pick_turned"], 1)
                pe.wait_ge(sem["splits1"], up("splits1", 2))
                for j in range(4):
                    o = claim(("rope", j))
                    three(o, [w[:, j, :] for w in qk1], [m[:, :] for m in xTs]).then_inc(sem["rope_in"], 1)
                pe.wait_ge(sem["route1"], up("route1", 8))
                pe.wait_ge(sem["y0_copied"], up("y0_copied", 1))
                pe.matmul(ysum, b2[:, :], ohT, start=True, stop=False, skip_group_check=True)
                for e in range(NE):
                    o = claim(("hidden", e))
                    pe.matmul(o, selw[0:NE, e, :], gm, start=True, stop=False, skip_group_check=True)
                    three(o, [w[:, e, :] for w in w1], [m[:, :] for m in xTs], first=False).then_inc(sem["hidden_made"], 1)
                    if e:
                        down1(e - 1)
                down1(NE - 1)

                def rough_job(m):
                    g, (t, h0, k, w) = m // NMJ, MAX_JOBS[m % NMJ]
                    o = claim(("rough1", m))
                    if m % NMJ == 0:
                        parts = f"parts_loaded{g % LOADED}"
                        pe.wait_ge(sem[parts], up(parts, 192 * (g // LOADED + 1)))
                    if t == 0:
                        pe.matmul(o, identb[:, :], mask1[:, :], start=True, stop=False, skip_group_check=True)
                    else:
                        for j in range(k):
                            pe.matmul(o[:, w * j + w - P:w * (j + 1)], identb[:, :], mask1[:, 0:P], start=(j == 0),
                                      stop=False, skip_group_check=True)
                    for j in range(k):
                        mm = pe.matmul(o[:, w * j:w * (j + 1)], QS[0:MROW, g % LOADED, h0 + j, P * t:P * (t + 1)],
                                       KS[0:MROW, g % LOADED, h0 + j, 0:w], start=False, stop=(j == k - 1),
                                       skip_group_check=True)
                    mm.then_inc(sem["rough1_made"], 1)

                def scores_job(m):
                    g, (i, h0, k, w) = m // NEJ, EXP_JOBS[m % NEJ]
                    if m % NEJ == 0:
                        pe.wait_ge(sem[f"max1_rows{g % 2}"], up(f"max1_rows{g % 2}", 16 * (g // 2 + 1)))
                    o = claim(("scores1", m))
                    for j in range(k):
                        mm = pe.matmul(o[:, w * j:w * (j + 1)], KS[0:MROW + 2, g % LOADED, h0 + j, P * i:P * (i + 1)],
                                       QS[0:MROW + 2, g % LOADED, h0 + j, P * i:S], start=(j == 0), stop=(j == k - 1),
                                       skip_group_check=True)
                    mm.then_inc(sem["scores1_made"], 1)

                def values_job(m):
                    g, (i, h0, k, w) = m // NEJ, EXP_JOBS[m % NEJ]
                    if m % NEJ == 0:
                        claim(("pv1", g))
                    if m == 0:
                        pe.wait_ge(sem["v1_copied"], up("v1_copied", 1))
                    o = bank(("pv1", g))
                    pe.wait_ge(sem["probs1_masked"], up("probs1_masked", m + 1))
                    for j in range(k):
                        h = h0 + j
                        mm = pe.matmul(o[32 * h:32 * h + 32, P * i:S], v1[:, i, GH * g + h, :],
                                       ring[:, m % RING, w * j:w * (j + 1)], start=(i == 0), stop=(i == NT - 1),
                                       skip_group_check=True)
                    mm.then_inc(sem["values1_made"], 1)

                for slot in range(SLOTS):
                    if slot < N1:
                        rough_job(slot)
                    if 0 <= slot - S_LAG < N1:
                        scores_job(slot - S_LAG)
                    if 0 <= slot - V_LAG < N1:
                        values_job(slot - V_LAG)
                    if slot == TURN_X:
                        turn_x(up_next, claim)
                    if slot == TURN_Z:
                        route_product(up_next, claim)
                    for g in range(NG):
                        if slot == maxima_slot(g) + 2:
                            turn(claim(("maxT1", g)), lambda t: mp1[:, t, :, :].rearrange("p c h -> p (c h)"),
                                 lambda t: pe.wait_ge(sem["max1_parts"], up("max1_parts", 3 * (g + 1))) if t == 0 else None,
                                 BF16, rows=2 * GH).then_inc(sem["maxT1_made"], 1)
                        if slot == values_slot(g) + 1:
                            turn(claim(("o1", g)), lambda t: ov[:, g % 2, P * t:P * (t + 1)],
                                 lambda t: pe.wait_ge(sem["pv1_copied"], up("pv1_copied", g + 1)) if t == 0 else None)\
                                .then_inc(sem["o1_turned"], 1)
                values0(up_next, claim, 0, range(2))
                turn(claim("ocT"), lambda t: o1v[:, t, :, :].rearrange("p h d -> p (h d)"),
                     lambda t: pe.wait_ge(sem["o1_ready"], up("o1_ready", 2 * NG)) if t == 0 else None).then_inc(sem["ocT_made"], 1)
                values0(up_next, claim, 0, range(2, NT))
                pe.wait_ge(sem["ocT_copied"], up("ocT_copied", 1))
                pe.matmul(ysum, wo1, ocT, start=False, stop=True, skip_group_check=True).then_inc(sem["out1_added"], 1)
                turn_weights(up_next, claim)
                turn(claim("y1"), lambda t: yT[:, P * t:P * (t + 1)],
                     lambda t: pe.wait_ge(sem["y1_copied"], up("y1_copied", 1)) if t == 0 else None).then_inc(sem["y1_turned"], 1)

        @block.scalar
        def _(scalar):
            def copy(up, dst, src, made, n, done):
                scalar.wait_ge(sem[made], up(made, n))
                scalar.activation(dst, src, ACT.Copy).then_inc(sem[done], 1)

            def queries(up, a, heads):
                for h in heads:
                    copy(up, q32[:, h, :], bank(("q", a, h)), "q_made", HH * a + h + 1, "q_copied")

            def values0(up, a, tiles):
                for t in tiles:
                    copy(up, v[:, t, :], bank(("v", a, t)), "v_made", NT * a + t + 1, "v_copied")

            def route_tanh(up):
                scalar.wait_ge(sem["route0"], up("route0", 1))
                scalar.activation(rt[:, 1, :, :], rt[:, 0, :, :], ACT.Tanh, scale=0.5).then_inc(sem["route_tanh"], 1)

            def route_exp(up):
                scalar.wait_ge(sem["route0"], up("route0", 5))
                scalar.activation(rt[:, 5, :, :], rt[:, 4, :, :], ACT.Exp, scale=10.0).then_inc(sem["route_exp"], 1)
                scalar.activation(rt[:, 6, :, :], rt[:, 4, :, :], ACT.Exp, scale=1.0 / 0.3).then_inc(sem["route_exp"], 1)

            def up_first(name, n):
                return START.get(name, 0) + n

            copy(up_first, hT[:, :], bank("hT"), "hT_made", 1, "hT_copied")
            queries(up_first, 0, range(HH))
            copy(up_first, xT[:, :], bank("xT"), "xT_made", 1, "xT_copied")
            route_tanh(up_first)
            route_exp(up_first)
            values0(up_first, 0, range(NT))
            with scalar.Fori(0, BATCH) as b:
                def up(name, n):
                    return b * PER[name] + START.get(name, 0) + n

                def up_next(name, n):
                    return up(name, n + PER[name])

                def tanh0(e):
                    scalar.wait_ge(sem["gate_made"], up("gate_made", e + 1))
                    if e >= 2:
                        scalar.wait_ge(sem["glu_a"], up("glu_a", e - 1))
                    if e == 0:
                        scalar.wait_ge(sem["y1_turned"], up("y1_turned", 0))
                    scalar.activation(act[:, e % 2, :], bank(("gate", e)), ACT.Tanh, scale=0.5).then_inc(sem["tanh_made"], 1)

                for a in range(2):
                    if a:
                        scalar.wait_ge(sem["pv_made"], up("pv_made", CH))
                        values0(up, a, range(NT))
                        scalar.wait_ge(sem["scores_made"], up("scores_made", NT))
                        queries(up, a, range(HH))
                    tanh0(4 * a)
                    tanh0(4 * a + 1)
                    scalar.wait_ge(sem["pm_scores"], up("pm_scores", a + 1))
                    if a:
                        scalar.wait_ge(sem["pv_made"], up("pv_made", CH))
                    scalar.activation(ppm[:, :], bank(("pm_scores", a)), ACT.Exp).then_inc(sem["pm_probs"], 1)
                    scalar.wait_ge(sem["pt_zeroed"], up("pt_zeroed", 2))
                    for t in range(NT):
                        scalar.wait_ge(sem["scores_made"], up("scores_made", NT * a + t + 1))
                        for w in range(2):
                            rows = slice(SEG * w, SEG * (w + 1))
                            scalar.activation(PT[rows, t, :, SEG * w:SEG * (w + 1)],
                                              bank(("scores", a, t))[rows, :].rearrange("p (h q) -> p h q", h=HH),
                                              ACT.Exp).then_inc(sem["probs_made"], 1)
                    if a:
                        copy(up_next, hT[:, :], bank("hT"), "hT_made", 1, "hT_copied")
                    tanh0(4 * a + 2)
                    tanh0(4 * a + 3)
                    for c in range(CH):
                        n = CH * a + c
                        if n >= 2:
                            scalar.wait_ge(sem["oT_made"], up("oT_made", n - 1))
                        copy(up, spread[:, c % 2, :], bank(("spread", a, c)), "spread_made", n + 1, "spread_copied")
                copy(up, yT, ysum, "down0_added", NE, "y0_copied")
                queries(up_next, 0, range(HH))
                copy(up, xT[:, :], bank("x1T"), "x1T_made", 1, "x1T_copied")
                scalar.wait_ge(sem["v1_filled"], up("v1_filled", 2))
                copy(up, v1[:, :, :, 0:DH1].rearrange("p t h d -> p (t h) d"), bank("v1").rearrange("p (n d) -> p n d", d=DH1),
                     "v1_made", 1, "v1_copied")
                for e in range(NE):
                    scalar.wait_ge(sem["hidden_made"], up("hidden_made", e + 1))
                    if e >= 2:
                        scalar.wait_ge(sem["down1_added"], up("down1_added", e - 1))
                    scalar.activation(act[:, e % 2, :], bank(("hidden", e)), ACT.Gelu, bias=b1T[:, e:e + 1]).then_inc(sem["gelu_made"], 1)
                for slot in range(SLOTS):
                    if slot == TURN_X:
                        copy(up_next, xT[:, :], bank("xT"), "xT_made", 1, "xT_copied")
                    if slot == TURN_Z + 1:
                        route_tanh(up_next)
                    if slot == TURN_Z + 2:
                        route_exp(up_next)
                    m = slot - S_LAG
                    if 0 <= m < N1:
                        i, h0, k, w = EXP_JOBS[m % NEJ]
                        scalar.wait_ge(sem["scores1_made"], up("scores1_made", m + 1))
                        if m >= RING:
                            scalar.wait_ge(sem["values1_made"], up("values1_made", m - RING + 1))
                        scalar.activation(ring[:, m % RING, 0:w * k], bank(("scores1", m))[:, 0:w * k], ACT.Exp)\
                            .then_inc(sem["probs1_made"], 1)
                    for g in range(NG):
                        if slot == values_slot(g):
                            if g >= 2:
                                scalar.wait_ge(sem["o1_turned"], up("o1_turned", g - 1))
                            copy(up, ov[:, g % 2, :], bank(("pv1", g)), "values1_made", NEJ * (g + 1), "pv1_copied")
                values0(up_next, 0, range(2))
                copy(up, ocT, bank("ocT"), "ocT_made", 1, "ocT_copied")
                values0(up_next, 0, range(2, NT))
                copy(up, yT, ysum, "out1_added", 1, "y1_copied")

        @block.gpsimd
        def _(pool):
            pool.memset(QS[:, :, :, :], 0.0).then_inc(s_clear, 1)
            pool.memset(KS[:, :, :, :], 0.0).then_inc(s_clear, 1)
            pool.memset(neg[:, :], 0.0).then_inc(s_clear, 1)
            pool.memset(half[:, :], -0.5).then_inc(s_clear, 1)
            pool.wait_ge(s_clear, 4)
            pool.memset(KS[MROW:MROW + 2, :, :, :], -1.0).then_inc(s_clear, 1)
            pool.wait_ge(s_clear, 5)
            pool.memset(neg[MROW:MROW + 2, :], -1.0).then_inc(s_clear, 1)
            pool.wait_ge(s_clear, CLEARED)
            pool.wait_ge(s_set, SETUP_ALL)

            def scales(up, layer, rms):
                s, var = f"scales{layer}", mv[:, NT * layer:NT * (layer + 1), 1]
                pool.wait_ge(sem[f"moments{layer}"], up(f"moments{layer}", NT))
                pool.nop(nofuse=True)
                pool.tensor_scalar(sc[:, 0, :], var, 1e-5, None, ALU.add).then_inc(sem[s], 1)
                pool.wait_ge(sem[s], up(s, 1))
                pool.nop(nofuse=True)
                pool.tensor_tensor(sc[:, 1, :], sc[:, 0, :], half[:, :], ALU.pow).then_inc(sem[s], 1)
                if rms:
                    pool.wait_ge(sem[s], up(s, 2))
                    pool.nop(nofuse=True)
                    pool.tensor_tensor(sc[:, 2, :], sc[:, 1, :], sc[:, 1, :], ALU.mult).then_inc(sem[s], 1)
                    pool.wait_ge(sem[s], up(s, 3))
                    pool.nop(nofuse=True)
                    pool.tensor_tensor(sc[:, 3, :], sc[:, 2, :], var, ALU.mult).then_inc(sem[s], 1)
                    pool.wait_ge(sem[s], up(s, 4))
                    pool.nop(nofuse=True)
                    pool.tensor_scalar(sc[:, 4, :], sc[:, 3, :], 1e-6, None, ALU.add).then_inc(sem[s], 1)
                    pool.wait_ge(sem[s], up(s, 5))
                    pool.nop(nofuse=True)
                    pool.tensor_tensor(sc[:, 5, :], sc[:, 4, :], half[:, :], ALU.pow).then_inc(sem[s], 1)

            def zero_windows(up):
                for w in range(2):
                    if w:
                        pool.wait_ge(sem["pt_zeroed"], up("pt_zeroed", 1))
                        pool.nop(nofuse=True)
                    pool.memset(PT[SEG * w:SEG * (w + 1), :, :, SEG * (1 - w):SEG * (2 - w)].rearrange("p t h q -> p (t h) q"), 0.0)\
                        .then_inc(sem["pt_zeroed"], 1)
                pool.wait_ge(sem["pt_zeroed"], up("pt_zeroed", 2))
                pool.nop(nofuse=True)

            def up_first(name, n):
                return START.get(name, 0) + n

            scales(up_first, 0, True)
            zero_windows(up_first)
            with pool.Fori(0, BATCH) as b:
                def up(name, n):
                    return b * PER[name] + START.get(name, 0) + n

                def up_next(name, n):
                    return up(name, n + PER[name])

                for a in range(2):
                    for t in range(NT):
                        for w in range(2):
                            n = 2 * (NT * a + t) + w + 1
                            pool.wait_ge(sem["probs_made"], up("probs_made", n))
                            pool.nop(nofuse=True)
                            if n > 1:
                                pool.wait_ge(sem["probs_masked"], up("probs_masked", n - 1))
                                pool.nop(nofuse=True)
                            block_ = PT[SEG * w:SEG * (w + 1), t, :, SEG * w:SEG * (w + 1)]
                            pool.affine_select(out=block_, in_=block_, compare_op=ALU.is_ge, fill=0.0, base=0,
                                               pattern=[[0, HH], [1, SEG]], channel_multiplier=-1).then_inc(sem["probs_masked"], 1)
                    if a == 0:
                        pool.wait_ge(sem["probs_masked"], up("probs_masked", 8))
                        pool.nop(nofuse=True)
                        scales(up_next, 0, True)
                pool.wait_ge(sem["probs_masked"], up("probs_masked", 16))
                pool.nop(nofuse=True)
                pool.wait_ge(sem["pv_made"], up("pv_made", 2 * CH))
                pool.nop(nofuse=True)
                pool.memset(v1[:, :, :, :], 0.0).then_inc(sem["v1_filled"], 1)
                pool.wait_ge(sem["v1_filled"], up("v1_filled", 1))
                pool.nop(nofuse=True)
                pool.memset(v1[:, :, :, DH1:DH1 + 1], 1.0).then_inc(sem["v1_filled"], 1)
                scales(up, 1, False)
                for m in range(N1):
                    i, h0, k, w = EXP_JOBS[m % NEJ]
                    pool.wait_ge(sem["probs1_made"], up("probs1_made", m + 1))
                    pool.nop(nofuse=True)
                    block_ = ring[:, m % RING, 0:w * k].rearrange("p (h q) -> p h q", h=k)[:, :, 0:P]
                    pool.affine_select(out=block_, in_=block_, compare_op=ALU.is_ge, fill=0.0, base=0,
                                       pattern=[[0, k], [1, P]], channel_multiplier=-1).then_inc(sem["probs1_masked"], 1)
                pool.wait_ge(sem["values1_made"], up("values1_made", N1))
                pool.nop(nofuse=True)
                zero_windows(up_next)

        @block.vector
        def _(dve):
            done = [0]

            def prepare(ins_):
                done[0] += 1
                ins_.then_inc(s_set, 1)
                dve.wait_ge(s_set, done[0])

            dve.wait_ge(s_load, 16 * loads)
            gbc = place["gbc"]
            for c in range(H // 2):
                part = place["wkT"][:, P * c:P * (c + 1)]
                prepare(dve.tensor_tensor(part, part, gbc, ALU.mult))
            assert done[0] == SETUP_KEYS
            prepare(dve.tensor_scalar(gam8, gam, DH0 ** -0.5, None, ALU.mult))
            prepare(dve.reciprocal(rtemp, temp))
            prepare(dve.tensor_copy(identb[:, :], ident))
            prepare(dve.tensor_copy(mask0[:, :], place["mask0"]))
            prepare(dve.tensor_copy(mask1[:, :], place["mask1"]))
            prepare(dve.tensor_copy(selr[:, :, :], place["selr"].rearrange("p (a b) -> p a b", a=CH)))
            prepare(dve.tensor_copy(selw[:, :, :], place["selw"].rearrange("p (a b) -> p a b", a=NE)))
            prepare(dve.tensor_copy(selpm[:, :], place["selpm"]))
            prepare(dve.tensor_scalar(place["wv"], place["wv"], gam, None, ALU.mult))
            prepare(dve.tensor_scalar(place["qk1"][:, 0:2 * P], place["qk1"][:, 0:2 * P], DH1 ** -0.5, None, ALU.mult))
            for name, t in (("wv", wv), ("wg", wg), ("wu", wu), ("w1", w1), ("qk1", qk1)):
                full = tuple([slice(None)] * len(t[0].shape))
                src = place[name]
                if len(t[0].shape) == 3:
                    src = src.rearrange("p (a b) -> p a b", a=t[0].shape[1])
                prepare(dve.tensor_copy(t[0][full], src))
                prepare(dve.tensor_tensor(t[1][full], src, t[0][full].bitcast(F32), ALU.subtract))
            dve.wait_ge(s_setpe, 2)
            for n in range(4):
                src = banks[:, n, :].rearrange("p (a b) -> p a b", a=4)
                first = HH * (n % 2) + n // 2
                hi, lo = (t[:, first:HH * (n % 2 + 1):2, :] for t in aq)
                prepare(dve.tensor_scalar(hi, src, gam8, None, ALU.mult))
                prepare(dve.scalar_tensor_tensor(lo, src, gam8, hi.bitcast(F32), ALU.mult, ALU.subtract))
            for r in range(2):
                dst = gpm[:, :].rearrange("p (c r k) -> p c r k", c=H // 2, r=2)[:, :, r, :]
                prepare(dve.tensor_scalar(dst, banks[:, 4 + r, 0:P].rearrange("p (c k) -> p c k", k=PM), gam8, None, ALU.mult))
            prepare(dve.tensor_copy(gpm16[:, :], gpm[:, :]))
            assert done[0] == SETUP_ALL


            def moments(up, layer, src):
                s, m, k = f"stats{layer}", f"moments{layer}", NT * layer
                for t in range(NT):
                    dve.bn_stats(st[:, k + t, :], src[:, t, :]).then_inc(sem[s], 1)
                dve.wait_ge(sem[s], up(s, NT))
                dve.nop(nofuse=True)
                for t in range(NT):
                    dve.bn_aggr(mv[:, k + t, :], st[:, k + t, :]).then_inc(sem[m], 1)

            def norm(up, layer, src, dst, ready):
                k = NT * layer
                dve.wait_ge(sem[f"scales{layer}"], up(f"scales{layer}", 2))
                for t in range(NT):
                    dve.tensor_scalar(dst[:, t, :], src[:, t, :], mv[:, k + t, 0:1], sc[:, 1, t:t + 1],
                                      ALU.subtract, ALU.mult).then_inc(sem[ready], 1)

            def split(up, dst, src, s, n):
                dve.tensor_copy(dst[0][:, :], src[:, :]).then_inc(sem[s], 1)
                dve.wait_ge(sem[s], up(s, n))
                dve.tensor_tensor(dst[1][:, :], src[:, :], dst[0][:, :].bitcast(F32), ALU.subtract).then_inc(sem[s], 1)

            count = {}

            def step(up, name, ins_):
                count[name] += 1
                ins_.then_inc(sem[name], 1)
                dve.wait_ge(sem[name], up(name, count[name]))

            def moments0(up):
                dve.wait_ge(sem["x_loaded"], up("x_loaded", 16))
                moments(up, 0, xin)

            def norm0(up, stored):
                norm(up, 0, xin, xn, "xn_ready")
                dve.wait_ge(sem["scales0"], up("scales0", 6))
                if stored is not None:
                    dve.wait_ge(sem["stored"], stored)
                for t in range(NT):
                    dve.wait_ge(sem["xn_ready"], up("xn_ready", t + 1))
                    dve.tensor_scalar(hn[:, t, :], xn[:, t, :], sc[:, 5, t:t + 1], None, ALU.mult).then_inc(sem["h_ready"], 1)

            def split_h(up):
                dve.wait_ge(sem["hT_copied"], up("hT_copied", 1))
                split(up, hTs, hT, "h_splits", 1)
                dve.tensor_copy(hT16[:, :], hT[:, :]).then_inc(sem["h_splits"], 1)

            def queries16(up, a, heads):
                for h in heads:
                    dve.wait_ge(sem["q_copied"], up("q_copied", HH * a + h + 1))
                    dve.tensor_copy(q16[:, h, :], q32[:, h, :]).then_inc(sem["q16_made"], 1)

            def split_x(up):
                dve.wait_ge(sem["xT_copied"], up("xT_copied", 1))
                split(up, xTs, xT, "x_splits", 1)

            R = [rt[:, i, :, :] for i in range(16)]
            T = [rw[:, i, :] for i in range(12)]

            def wide(t):
                return t.rearrange("p (t o) -> p t o", o=1).broadcast_to([P, NT, NE])

            def route_zone(up):
                count["route0"] = 0
                dve.wait_ge(sem["z_made"], up("z_made", 1))
                step(up, "route0", dve.tensor_scalar(R[0], bank("z")[:, 0:NT * NE].rearrange("p (t e) -> p t e", t=NT), rtemp, None, ALU.mult))
                step(up, "route0", dve.tensor_scalar(R[2], R[0], LOGIT_LOWER, None, ALU.is_ge))
                step(up, "route0", dve.scalar_tensor_tensor(R[3], R[0], 0.0, R[2], ALU.is_le, ALU.mult))

            def route_distance(up):
                dve.wait_ge(sem["route_tanh"], up("route_tanh", 1))
                step(up, "route0", dve.tensor_scalar(R[7], R[1], 0.5, 0.5 - CENTER, ALU.mult, ALU.add))
                step(up, "route0", dve.scalar_tensor_tensor(R[4], R[7], -1.0, R[7], ALU.mult, ALU.min))

            def route_sum(up):
                dve.wait_ge(sem["route_exp"], up("route_exp", 2))
                step(up, "route0", dve.tensor_tensor(R[8], R[5], R[3], ALU.mult))
                step(up, "route0", dve.reduce_sum(T[0], R[8], AX))
                step(up, "route0", dve.tensor_scalar(T[1], T[0], 1e-8, None, ALU.is_lt))

            def route_nearest(up, k):
                key, pick = ((R[4], R[11]), (R[12], R[13]))[k]
                step(up, "route0", dve.reduce_max(T[2], key, AX))
                step(up, "route0", dve.tensor_tensor(R[9], key, wide(T[2]), ALU.is_equal))
                step(up, "route0", dve.tensor_tensor(R[10], R[9], rank[:, :, :], ALU.mult))
                step(up, "route0", dve.reduce_max(T[3], R[10], AX))
                step(up, "route0", dve.tensor_tensor(pick, R[10], wide(T[3]), ALU.is_equal))
                if k == 0:
                    step(up, "route0", dve.scalar_tensor_tensor(R[12], R[11], -4.0, R[4], ALU.mult, ALU.add))

            def route_fallback(up):
                step(up, "route0", dve.tensor_tensor(R[11], R[11], R[13], ALU.add))
                step(up, "route0", dve.tensor_tensor(R[12], R[6], R[11], ALU.mult))
                step(up, "route0", dve.reduce_sum(T[4], R[12], AX))
                step(up, "route0", dve.tensor_scalar(T[5], T[4], 1e-8, None, ALU.max))
                step(up, "route0", dve.reciprocal(T[6], T[5]))
                step(up, "route0", dve.tensor_tensor(R[13], R[12], wide(T[6]), ALU.mult))

            def route_choose(up):
                step(up, "route0", dve.tensor_tensor(R[14], R[13], R[8], ALU.subtract))
                step(up, "route0", dve.tensor_tensor(R[9], R[14], wide(T[1]), ALU.mult))
                step(up, "route0", dve.tensor_tensor(R[10], R[9], R[8], ALU.add))
                step(up, "route0", dve.reduce_sum(T[7], R[10], AX))
                step(up, "route0", dve.tensor_scalar(T[8], T[7], 1e-8, None, ALU.max))
                step(up, "route0", dve.reciprocal(T[9], T[8]))
                step(up, "route0", dve.tensor_tensor(R[11], R[10], wide(T[9]), ALU.mult))

            def route_parts(up):
                step(up, "route0", dve.tensor_scalar(R[12], R[11], 0.5, None, ALU.mult))
                step(up, "route0", dve.tensor_copy(wp[:, :, 0:NE], R[12]))
                step(up, "route0", dve.tensor_tensor(R[13], R[12], wp[:, :, 0:NE], ALU.subtract))
                step(up, "route0", dve.tensor_copy(wp[:, :, NE:2 * NE], R[13]))
                step(up, "route0", dve.tensor_tensor(wp[:, :, 2 * NE:3 * NE], R[13], wp[:, :, NE:2 * NE], ALU.subtract))
                assert count["route0"] == PER["route0"], count

            def copy_weights(up):
                dve.wait_ge(sem["wT_made"], up("wT_made", 1))
                dve.tensor_copy(wT[:, :], bank("wT").bitcast(BF16)[0:24, 0:S]).then_inc(sem["wT_copied"], 1)

            def up_first(name, n):
                return START.get(name, 0) + n

            moments0(up_first)
            norm0(up_first, None)
            split_h(up_first)
            queries16(up_first, 0, range(HH))
            split_x(up_first)
            route_zone(up_first)
            route_distance(up_first)
            route_sum(up_first)
            route_nearest(up_first, 0)
            route_nearest(up_first, 1)
            route_fallback(up_first)
            route_choose(up_first)
            route_parts(up_first)
            copy_weights(up_first)
            with dve.Fori(0, BATCH) as b:
                def up(name, n):
                    return b * PER[name] + START.get(name, 0) + n

                def up_next(name, n):
                    return up(name, n + PER[name])

                def glu_fn(e):
                    dve.wait_ge(sem["tanh_made"], up("tanh_made", e + 1))
                    if e:
                        dve.wait_ge(sem["glu_c"], up("glu_c", e))
                    dve.scalar_tensor_tensor(glu[:, :], act[:, e % 2, :], 1.0, bank(("gate", e)), ALU.add, ALU.mult).then_inc(sem["glu_a"], 1)
                    dve.wait_ge(sem["up_made"], up("up_made", e + 1))
                    dve.wait_ge(sem["glu_a"], up("glu_a", e + 1))
                    dve.tensor_tensor(glu[:, :], glu[:, :], bank(("up", e)), ALU.mult).then_inc(sem["glu_b"], 1)
                    dve.wait_ge(sem["glu_b"], up("glu_b", e + 1))
                    if e >= 2:
                        dve.wait_ge(sem["down0_added"], up("down0_added", e - 1))
                    dve.tensor_tensor(glc[:, e % 2, :], glu[:, :], bank(("wb", e)), ALU.mult).then_inc(sem["glu_c"], 1)

                for a in range(2):
                    if a:
                        dve.wait_ge(sem["rough_made"], up("rough_made", NT))
                        queries16(up, a, range(HH))
                    dve.wait_ge(sem["rough_pm_made"], up("rough_pm_made", a + 1))
                    count["max0"] = 9 * a
                    step(up, "max0", dve.reduce_max(mx[:, 0, :, :], bank(("rough_pm", a)).rearrange("p (t h k) -> p t h k", t=NT, h=HH), AX))
                    for t in range(NT):
                        dve.wait_ge(sem["rough_made"], up("rough_made", NT * a + t + 1))
                        count["max0"] += 1
                        dve.reduce_max(mx[:, 1, t, :], bank(("rough", a, t)).rearrange("p (h k) -> p h k", h=HH), AX).then_inc(sem["max0"], 1)
                    dve.wait_ge(sem["max0"], up("max0", count["max0"]))
                    step(up, "max0", dve.tensor_tensor(mx[:, 2, :, :], mx[:, 0, :, :], mx[:, 1, :, :], ALU.max))
                    step(up, "max0", dve.tensor_copy(mp[:, :, 0, :], mx[:, 2, :, :]))
                    step(up, "max0", dve.tensor_tensor(mx[:, 3, :, :], mx[:, 2, :, :], mp[:, :, 0, :], ALU.subtract))
                    step(up, "max0", dve.tensor_copy(mp[:, :, 1, :], mx[:, 3, :, :]))
                    assert count["max0"] == 9 * (a + 1)
                    if a:
                        norm0(up_next, up("stored", 0))
                    dve.wait_ge(sem["maxT_made"], up("maxT_made", a + 1))
                    if a:
                        dve.wait_ge(sem["max_stored"], up("max_stored", 16))
                        dve.wait_ge(sem["pm_scores"], up("pm_scores", 1))
                    dve.tensor_copy(mT[:, :], bank(("maxT", a)).bitcast(BF16)[0:2 * HH, 0:S]).then_inc(sem["maxT_copied"], 1)
                    for e in (4 * a, 4 * a + 1, 4 * a + 2):
                        glu_fn(e)
                    dve.wait_ge(sem["den_made"], up("den_made", a + 1))
                    if a:
                        dve.wait_ge(sem["spread_made"], up("spread_made", CH))
                    dve.wait_ge(sem["glu_c"], up("glu_c", 4 * a + 3))
                    count["rden_made"] = 3 * a
                    step(up, "rden_made", dve.reciprocal(rd[:, :], bank(("den", a))))
                    step(up, "rden_made", dve.tensor_copy(rds[0][:, :], rd[:, :]))
                    step(up, "rden_made", dve.tensor_tensor(rds[1][:, :], rd[:, :], rds[0][:, :].bitcast(F32), ALU.subtract))
                    if a:
                        split_h(up_next)
                    glu_fn(4 * a + 3)
                    for c in range(CH):
                        n = CH * a + c
                        dve.wait_ge(sem["pv_made"], up("pv_made", n + 1))
                        dve.wait_ge(sem["spread_copied"], up("spread_copied", n + 1))
                        if n >= 2:
                            dve.wait_ge(sem["out0_added"], up("out0_added", n - 1))
                        dve.tensor_tensor(oT[:, c % 2, :], bank(("pv", a, c)), spread[:, c % 2, :], ALU.mult).then_inc(sem["oT_made"], 1)
                    if a == 0:
                        moments0(up_next)

                dve.wait_ge(sem["y0_turned"], up("y0_turned", 1))
                dve.wait_ge(sem["residual_loaded"], up("residual_loaded", 16))
                dve.tensor_tensor(x1[:, :, :], x[:, :, :], bank("y0").rearrange("p (t d) -> p t d", t=NT), ALU.add)\
                    .then_inc(sem["x1_ready"], 1)
                dve.wait_ge(sem["x1_ready"], up("x1_ready", 1))
                moments(up, 1, x1)
                norm(up, 1, x1, xn1, "xn1_ready")
                dve.wait_ge(sem["x1T_copied"], up("x1T_copied", 1))
                split(up, xTs, xT, "splits1", 1)
                count["route1"] = 0
                dve.wait_ge(sem["z1_made"], up("z1_made", 1))
                bgw = bg.rearrange("p (o e) -> p o e", o=1).broadcast_to([P, NT, NE])
                step(up, "route1", dve.tensor_tensor(R[1], bank("z1")[:, 0:NT * NE].rearrange("p (t e) -> p t e", t=NT), bgw, ALU.add))
                step(up, "route1", dve.reduce_max(T[0], R[1], AX))
                step(up, "route1", dve.tensor_tensor(R[2], R[1], wide(T[0]), ALU.is_equal))
                step(up, "route1", dve.tensor_tensor(R[3], R[2], rank[:, :, :], ALU.mult))
                step(up, "route1", dve.reduce_max(T[1], R[3], AX))
                step(up, "route1", dve.tensor_tensor(R[5], R[3], wide(T[1]), ALU.is_equal))
                dve.wait_ge(sem["pick_turned"], up("pick_turned", 1))
                step(up, "route1", dve.tensor_copy(ohT, bank("pick")[0:NE, :]))
                step(up, "route1", dve.tensor_scalar(gm, ohT, 1.0, -MASKED, ALU.subtract, ALU.mult))
                for j in range(2):
                    count["rope"] = 7 * j
                    dve.wait_ge(sem["rope_in"], up("rope_in", 2 * j + 1))
                    step(up, "rope", dve.tensor_tensor(tmp[:, 0, :], bank(("rope", 2 * j)), cos[:, :], ALU.mult))
                    dve.wait_ge(sem["rope_in"], up("rope_in", 2 * j + 2))
                    step(up, "rope", dve.tensor_tensor(tmp[:, 1, :], bank(("rope", 2 * j + 1)), sin[:, :], ALU.mult))
                    step(up, "rope", dve.tensor_tensor(tmp[:, 2, :], tmp[:, 0, :], tmp[:, 1, :], ALU.add))
                    step(up, "rope", dve.tensor_copy(pq[:, j, 0, :], tmp[:, 2, :]))
                    step(up, "rope", dve.tensor_tensor(tmp[:, 3, :], tmp[:, 2, :], pq[:, j, 0, :], ALU.subtract))
                    step(up, "rope", dve.tensor_copy(pq[:, j, 1, :], tmp[:, 3, :]))
                    step(up, "rope", dve.tensor_tensor(pq[:, j, 2, :], tmp[:, 3, :], pq[:, j, 1, :], ALU.subtract))
                dve.wait_ge(sem["rough_made"], up("rough_made", 2 * NT))
                queries16(up_next, 0, range(HH))

                def normalize(g):
                    dve.wait_ge(sem["o1_turned"], up("o1_turned", g + 1))
                    o = bank(("o1", g)).rearrange("p (t h c) -> p t h c", t=NT, h=GH)
                    dve.reciprocal(rdn[:, :, :], o[:, :, :, DH1]).then_inc(sem["o1_ready"], 1)
                    dve.wait_ge(sem["o1_ready"], up("o1_ready", 2 * g + 1))
                    dve.tensor_tensor(o1v[:, :, GH * g:GH * (g + 1), :], o[:, :, :, 0:DH1],
                                      rdn[:, :, :].rearrange("p t (h o) -> p t h o", o=1).broadcast_to([P, NT, GH, DH1]), ALU.mult)\
                        .then_inc(sem["o1_ready"], 1)

                for slot in range(SLOTS):
                    if slot < N1:
                        t, h0, k, w = MAX_JOBS[slot % NMJ]
                        dve.wait_ge(sem["rough1_made"], up("rough1_made", slot + 1))
                        dve.reduce_max(mx1[:, 0, t, h0:h0 + k], bank(("rough1", slot))[:, 0:w * k].rearrange("p (h k) -> p h k", h=k), AX)\
                            .then_inc(sem["max1"], 1)
                    for g in range(NG):
                        if slot == maxima_slot(g):
                            dve.wait_ge(sem["max1"], up("max1", NMJ * (g + 1)))
                            count["max1_parts"] = 3 * g
                            step(up, "max1_parts", dve.tensor_copy(mp1[:, :, 0, :], mx1[:, 0, :, :]))
                            step(up, "max1_parts", dve.tensor_tensor(mx1[:, 1, :, :], mx1[:, 0, :, :], mp1[:, :, 0, :], ALU.subtract))
                            step(up, "max1_parts", dve.tensor_copy(mp1[:, :, 1, :], mx1[:, 1, :, :]))
                        if slot == maxima_slot(g) + 2:
                            dve.wait_ge(sem["maxT1_made"], up("maxT1_made", g + 1))
                            if g >= 2:
                                dve.wait_ge(sem[f"max1_stored{g % 2}"], up(f"max1_stored{g % 2}", 16 * (g // 2)))
                            dve.tensor_copy(mT1[:, g % 2, :], bank(("maxT1", g)).bitcast(BF16)[0:2 * GH, 0:S]).then_inc(sem["maxT1_copied"], 1)
                        if slot == values_slot(g) + 2:
                            normalize(g)
                    if slot == TURN_X + 2:
                        split_x(up_next)
                    if slot == TURN_Z + 1:
                        route_zone(up_next)
                    if slot == TURN_Z + 2:
                        route_distance(up_next)
                    if slot == TURN_Z + 4:
                        route_sum(up_next)
                    if slot == TURN_Z + 5:
                        route_nearest(up_next, 0)
                    if slot == TURN_Z + 6:
                        route_nearest(up_next, 1)
                    if slot == TURN_Z + 8:
                        route_fallback(up_next)
                    if slot == TURN_Z + 11:
                        route_choose(up_next)
                    if slot == TURN_Z + 12:
                        route_parts(up_next)
                copy_weights(up_next)
                dve.wait_ge(sem["y1_turned"], up("y1_turned", 1))
                dve.tensor_tensor(yout[:, :, :], x1[:, :, :], bank("y1").rearrange("p (t d) -> p t d", t=NT), ALU.add)\
                    .then_inc(sem["out_ready"], 1)


SETUP_KEYS = H // 2
SETUP_ALL = SETUP_KEYS + 10 + 2 * 5 + 8 + 3
CLEARED = 6


def kernel(**inputs):
    import numpy as _np
    import concourse.bacc as _bacc
    from concourse import mybir as _mybir
    from concourse.bass_utils import run_bass_kernel_spmd as _run

    arrays = layout(inputs)
    nc = _bacc.Bacc("TRN2", target_bir_lowering=False, num_devices=1)
    ins, feed = {}, {}
    for name, a in arrays.items():
        feed[f"in_{name}"] = a
        ins[name] = nc.dram_tensor(f"in_{name}", a.shape, _mybir.dt.from_np(a.dtype), kind="ExternalInput").ap()
    out = nc.dram_tensor("out", (BATCH, S, P), F32, kind="ExternalOutput").ap()
    build(nc, ins, out)
    r = _run(nc, [feed], core_ids=[0])
    return r.results[0]["out"]


def layout(inputs):
    g = {k: np.asarray(v) for k, v in inputs.items()}

    def rows(a):
        return np.ascontiguousarray(a.transpose(1, 0, 2).reshape(a.shape[1], -1))

    out = {"x": np.ascontiguousarray(np.concatenate([g["L0_attn_x"], g["L0_attn_x"][0:1]], 0))}
    wqkv = g["L0_attn_w_qkv"]
    inner = H * DH0
    out["wv"] = np.ascontiguousarray(wqkv[:, 2 * inner:])
    out["wqT"] = rows(np.ascontiguousarray(wqkv[:, 0:inner].T).reshape(H // 2, P, P))
    out["wkT"] = rows(np.ascontiguousarray(wqkv[:, inner:2 * inner].T).reshape(H // 2, P, P))
    out["gbc"] = np.ascontiguousarray(np.broadcast_to(g["L0_attn_gamma"][None, :], (P, P)))
    pmk = g["L0_attn_pm_k"].reshape(H * PM, DH0).T
    out["pmkT"] = np.ascontiguousarray(np.concatenate([pmk, pmk], 0))
    out["wo0"] = rows(g["L0_attn_w_out"].reshape(H // 2, P, P))
    pmv = np.zeros((H // 2, HH, PM, 2, DH0), np.float32)
    for h in range(H):
        pmv[h // 2, h % HH, :, h % 2, :] = g["L0_attn_pm_v"][h]
    out["pmv"] = rows(pmv.reshape(H // 2, P, P))
    for name, key in (("wg", "L0_ffn_Wg"), ("wu", "L0_ffn_Wu"), ("wd", "L0_ffn_Wd"), ("w1", "L1_ffn_W1"), ("w2", "L1_ffn_W2")):
        out[name] = rows(g[key])
    w = g["L1_attn_w_qkv"].reshape(P, 3, P // 2, 2)
    q, k = w[:, 0], w[:, 1]
    out["qk1"] = np.ascontiguousarray(np.concatenate([a.reshape(P, P) for a in (q, q[:, :, ::-1], k, k[:, :, ::-1])], 1))
    col = [g["L0_attn_gamma"][:, None], np.zeros((P, 1), np.float32),
           np.broadcast_to(g["L0_ffn_temperature"][None, :], (P, 1)), np.zeros((P, 1), np.float32)]
    out["small"] = np.ascontiguousarray(np.concatenate(
        [w[:, 2].reshape(P, P), g["L1_attn_w_out"], np.eye(P, dtype=np.float32), g["L0_ffn_Wr"], g["L1_ffn_Wg"],
         np.broadcast_to(g["L1_ffn_bg"][None, :], (P, NE)), g["L1_ffn_b1"].T] + col, 1))
    out["b2"] = np.ascontiguousarray(g["L1_ffn_b2"])
    out["rank"] = np.tile(np.arange(NE, 0, -1, dtype=np.float32), (P, NT))
    r = np.arange(P)
    out["mask0"] = np.tile(np.where(np.arange(SEG)[None, :] > r[:, None] % SEG, MASKED, 0.0), (1, 1)).astype(np.float32)
    out["mask1"] = np.tile(np.where(r[None, :] > r[:, None], MASKED, 0.0), (1, NT)).astype(np.float32)
    out["selpm"] = np.where(np.arange(2 * HH)[:, None] % HH == r[None, :] // PM, -1.0, 0.0).astype(np.float32)
    out["selw"] = np.repeat(np.tile(np.eye(NE, dtype=np.float32), (3, 1)), P, 1)
    m = np.arange(32)
    out["esel"] = np.tile(np.concatenate([(m % 2 == c) for c in range(2)]).astype(np.float32), (P, 1))
    h8 = r // PM
    out["epm"] = np.concatenate([((h8[:, None] % 4 == j) & (h8[:, None] // 4 == m[None, :] % 2)) for j in range(4)], 1).astype(np.float32)
    selr = np.zeros((P, CH, 2, DH0), np.float32)
    for h in range(HH):
        selr[32 * (h % 4) + h // 4, h // 2, h % 2, :] = 1.0
    out["selr"] = selr.reshape(P, CH * P)
    inv = np.float32(1.0) / np.float32(10000.0) ** (np.arange(0, DH1, 2, dtype=np.float32) / np.float32(DH1))
    freqs = np.outer(np.arange(S, dtype=np.float32), inv).astype(np.float32)
    pair = (r % DH1) // 2
    out["cos"] = np.ascontiguousarray(np.cos(freqs).T[pair]).astype(np.float32)
    out["sin"] = np.ascontiguousarray(np.sin(freqs).T[pair] * np.where(r % 2 == 0, -1.0, 1.0)[:, None]).astype(np.float32)
    return out
```

```python
from contextlib import ExitStack
import math

import numpy as np

import concourse.bass as bass
from concourse import mybir

F32 = mybir.dt.float32
F32R = mybir.dt.float32r
BF16 = mybir.dt.bfloat16
F16 = mybir.dt.float16
ALU = mybir.AluOpType
ACT = mybir.ActivationFunctionType
AX = mybir.AxisListType.X

P = 128
BATCH = 8
S = 512
NT = S // P
H = 16
DH0 = 64
DH1 = P // H
SEG = 64
PM = 16
HH = H // 2
CH = HH // 2
NE = 8
GH = 4
NG = H // GH
VW = 32
NB = 7
MASKED = -1e30
CENTER = 1.0 / math.e
LOWER = 0.5 - math.log(4.0 / 3.0)
LOGIT_LOWER = math.log(LOWER / (1.0 - LOWER))
MROW = 96
TERMS = 6
Q_TERMS = ((0, 0, 3), (1, 3, 2), (2, 5, 1))
K_TERMS = ((1, 5), (2, 3), (3, 0))


def key_widths():
    return [S - P * i for i in range(NT)]


def sized_jobs(widths, order):
    out = []
    for i in order:
        k = min(GH, 512 // widths[i]) if widths[i] <= 256 else 1
        out += [(i, h, k, widths[i]) for h in range(0, GH, k)]
    return out


MAX_JOBS = sized_jobs([P * (i + 1) for i in range(NT)], range(NT))
EXP_JOBS = sized_jobs(key_widths(), range(NT))
NMJ, NEJ = len(MAX_JOBS), len(EXP_JOBS)
TILE_ENDS = [max(n for n, job in enumerate(EXP_JOBS) if job[0] == i) for i in range(NT)]

PER = {
    "x_loaded": 16, "residual_loaded": 16, "stats0": 4, "moments0": 4, "scales0": 6, "xn_ready": 4, "h_ready": 4,
    "xT_made": 1, "hT_made": 1, "xT_copied": 1, "hT_copied": 1, "h_splits": 3, "x_splits": 2,
    "z_made": 1, "route0": 37, "route_tanh": 1, "route_exp": 2, "wT_made": 1, "wT_copied": 1,
    "v_made": 8, "v_copied": 8, "q_made": 16, "q_copied": 16, "q16_made": 16,
    "rough_made": 8, "rough_pm_made": 2, "max0": 18, "maxT_made": 2, "maxT_copied": 2, "max_stored": 32, "max_rows": 32,
    "pm_scores": 2, "pm_probs": 2, "pt_zeroed": 2, "scores_made": 8, "probs_made": 16, "probs_masked": 16,
    "den_made": 2, "rden_made": 6, "spread_made": 8, "spread_copied": 8, "pv_made": 8, "oT_made": 8,
    "out0_added": 8, "wb_made": 8, "gate_made": 8, "up_made": 8, "tanh_made": 8,
    "glu_a": 8, "glu_b": 8, "glu_c": 8, "down0_added": 8,
    "y0_copied": 1, "y0_turned": 1, "x1_ready": 1,
    "stats1": 4, "moments1": 4, "scales1": 2, "xn1_ready": 4, "x1T_made": 1, "x1T_copied": 1, "splits1": 2,
    "z1_made": 1, "route1": 8, "pick_turned": 1, "rope_in": 4, "rope": 14, "parts_stored": 6 * 16,
    "parts_loaded0": 64, "parts_loaded1": 32, "parts_loaded2": 32, "v1_filled": 2, "v1_made": 1, "v1_copied": 1,
    "rough1_made": NMJ * NG, "max1": NMJ * NG,
    "max1_parts": 3 * NG, "maxT1_made": NG, "maxT1_copied": NG, "max1_stored0": 8 * NG, "max1_stored1": 8 * NG,
    "max1_rows0": 8 * NG, "max1_rows1": 8 * NG,
    "scores1_made": NEJ * NG, "probs1_made": NEJ * NG, "probs1_masked": NEJ * NG,
    "values1_made": NT * NG, "pv1_copied": NG, "o1_turned": NG, "o1_ready": 2 * NG, "ocT_made": 1, "ocT_copied": 1,
    "out1_added": 1, "hidden_made": 8, "gelu_made": 8, "down1_added": 8, "y1_copied": 1, "y1_turned": 1,
    "out_ready": 1, "stored": 16,
}


N1 = NMJ * NG
S_LAG = 19
V_LAG = S_LAG + 3
SLOTS = N1 + V_LAG + 3
RING = 8
LOADED = 3
MAX_TURN = 1
EXPERT_AT = {2: 6, 8: 7}
LAST_DOWN = 14
TURN_X, TURN_Z = 44, 46
ROUTE_AT = 52
Q_FIRST = 2


def maxima_slot(g):
    return NMJ * g + NMJ - 1


def values_slot(g):
    return NMJ * g + NMJ - 1 + V_LAG


def bank_plan():
    jobs = []

    def expert(e):
        return [(("wb", e), "glu_c", e + 1), (("gate", e), "glu_a", e + 1), (("up", e), "glu_b", e + 1)]

    def q_jobs(a, heads, ahead):
        return [(("q", a, h), "q_copied", HH * a + h + 1 + ahead * PER["q_copied"]) for h in heads]

    def v_jobs(a, tiles, ahead):
        return [(("v", a, t), "v_copied", NT * a + t + 1 + ahead * PER["v_copied"]) for t in tiles]

    def rough_jobs(a, ahead):
        return [(("rough_pm", a), "max0", 9 * a + 1 + ahead * PER["max0"])] + \
               [(("rough", a, t), "max0", 9 * a + 2 + t + ahead * PER["max0"]) for t in range(NT)]

    def pv_jobs(a, c):
        return [(("pv", a, c), "oT_made", CH * a + c + 1), (("spread", a, c), "spread_copied", CH * a + c + 1)]

    for a in range(2):
        jobs += [(("pm_scores", a), "pm_probs", a + 1)]
        jobs += [(("scores", a, t), "probs_made", 8 * a + 2 * t + 2) for t in range(NT)]
        jobs += [("hT", "hT_copied", 1 + PER["hT_copied"])] if a else []
        jobs += expert(4 * a) + expert(4 * a + 1)
        jobs += [(("den", a), "rden_made", 3 * a + 1)]
        jobs += q_jobs(1, range(HH), 0) if a == 0 else []
        jobs += expert(4 * a + 2)
        jobs += pv_jobs(a, 0)
        jobs += rough_jobs(1, 0) if a == 0 else []
        jobs += pv_jobs(a, 1) + pv_jobs(a, 2)
        jobs += [(("maxT", 1), "maxT_copied", 2)] if a == 0 else []
        jobs += pv_jobs(a, 3)
        jobs += expert(4 * a + 3)
        jobs += v_jobs(1, range(NT), 0) if a == 0 else []
    jobs += q_jobs(0, range(Q_FIRST), 1)
    jobs += [("y0", "x1_ready", 1)]
    jobs += q_jobs(0, range(Q_FIRST, HH), 1)
    jobs += [("x1T", "x1T_copied", 1), ("z1", "route1", 1), ("v1", "v1_copied", 1), ("pick", "route1", 7)]
    jobs += [(("rope", j), "rope", (1, 2, 8, 9)[j]) for j in range(4)]
    jobs += [(("hidden", e), "gelu_made", e + 1) for e in range(NE) if e not in EXPERT_AT.values()]
    jobs += rough_jobs(0, 1)
    for slot in range(SLOTS):
        if slot < N1:
            jobs += [(("rough1", slot), "max1", slot + 1)]
        if 0 <= slot - S_LAG < N1:
            jobs += [(("scores1", slot - S_LAG), "probs1_made", slot - S_LAG + 1)]
        if 0 <= slot - V_LAG < N1 and (slot - V_LAG) % NEJ == TILE_ENDS[0]:
            jobs += [(("pv1", (slot - V_LAG) // NEJ), "pv1_copied", (slot - V_LAG) // NEJ + 1)]
        jobs += [(("hidden", EXPERT_AT[slot]), "gelu_made", EXPERT_AT[slot] + 1)] if slot in EXPERT_AT else []
        jobs += [("xT", "xT_copied", 1 + PER["xT_copied"])] if slot == TURN_X else []
        jobs += [("z", "route0", 1 + PER["route0"])] if slot == TURN_Z else []
        for g in range(NG):
            jobs += [(("maxT1", g), "maxT1_copied", g + 1)] if slot == maxima_slot(g) + MAX_TURN else []
            jobs += [(("o1", g), "o1_ready", 2 * g + 2)] if slot == values_slot(g) + 1 else []
    jobs += [(("maxT", 0), "maxT_copied", 1 + PER["maxT_copied"])]
    jobs += v_jobs(0, range(2), 1) + [("ocT", "ocT_copied", 1)] + v_jobs(0, range(2, NT), 1)
    jobs += [("wT", "wT_copied", 1 + PER["wT_copied"]), ("y1", "out_ready", 1)]
    plan, age, last, held = {}, list(range(NB)), {}, set()
    for job, sem, count in jobs:
        bank = next(k for k in age if k not in held)
        if job[0] == "pv1":
            held.add(bank)
        if job[0] == "o1":
            held.discard(plan["pv1", job[1]][0])
        age.remove(bank)
        age.append(bank)
        plan[job] = (bank, last.get(bank))
        last[bank] = (sem, count)
    for job, (bank, before) in plan.items():
        if before is None:
            plan[job] = (bank, (last[bank][0], last[bank][1] - PER[last[bank][0]]))
    return plan


PLAN = bank_plan()

START = {"x1_ready": 1, "stored": 1, "y1_turned": 1, "y1_copied": 1}
START.update({name: PER[name] for bank, (name, count) in PLAN.values() if count <= 0})


def build(nc, ins, out):
    plan = PLAN
    with ExitStack() as ctx:
        def sb(name, shape, dt):
            return ctx.enter_context(nc.sbuf_tensor(name, shape, dt))

        sem = {name: ctx.enter_context(nc.semaphore(name)) for name in PER}
        s_first = ctx.enter_context(nc.semaphore("first_weights_loaded"))
        s_second = ctx.enter_context(nc.semaphore("second_weights_loaded"))
        s_load = ctx.enter_context(nc.semaphore("other_weights_loaded"))
        s_set = ctx.enter_context(nc.semaphore("weights_prepared"))
        s_setpe = ctx.enter_context(nc.semaphore("folded_weights_made"))
        s_clear = ctx.enter_context(nc.semaphore("buffers_cleared"))

        banks = ctx.enter_context(nc.psum_tensor("banks", [P, 8, 512], F32))
        ysum = banks[:, NB, :]

        def bank(job):
            return banks[:, plan[job][0], :]

        aq = [sb(f"aq{i}", [P, H, P], F32R) for i in range(2)]
        wv = [sb(f"wv{i}", [P, H * DH0], F32R) for i in range(2)]
        wg = [sb(f"wg{i}", [P, NE, P], F32R) for i in range(2)]
        wu = [sb(f"wu{i}", [P, NE, P], F32R) for i in range(2)]
        w1 = [sb(f"w1{i}", [P, NE, P], F32R) for i in range(2)]
        qk1 = [sb(f"qk1{i}", [P, 4, P], F32R) for i in range(2)]
        wo0 = sb("wo0", [P, H // 2, P], F32)
        wd = sb("wd", [P, NE, P], F32)
        w2 = sb("w2", [P, NE, P], F32)
        gpm = sb("gpm", [P, H * PM], F32)
        gpm16 = sb("gpm16", [P, H * PM], F16)
        pmv = sb("pmv", [P, H // 2, P], F32)
        small = sb("small", [P, 3 * P + 8 + 8 + 8 + 8 + 5], F32)
        wv1, wo1, ident = small[:, 0:P], small[:, P:2 * P], small[:, 2 * P:3 * P]
        wr = small[:, 3 * P:3 * P + 8]
        wgate = small[:, 3 * P + 8:3 * P + 16]
        bg = small[:, 3 * P + 16:3 * P + 24]
        b1T = small[:, 3 * P + 24:3 * P + 32]
        gam, gam8, temp, rtemp, lower = (small[:, 3 * P + 32 + i:3 * P + 33 + i] for i in range(5))
        b2 = sb("b2", [NE, P], F32)
        rank = sb("rank", [P, NT, NE], F32)
        esel = sb("esel", [P, 2, 32], F32)
        epm = sb("epm", [P, 4, 32], F32)
        cos = sb("cos", [P, S], F32)
        sin = sb("sin", [P, S], F32)
        identb = sb("identb", [P, P], BF16)
        mask0 = sb("mask0", [P, SEG], BF16)
        mask1 = sb("mask1", [P, S], BF16)
        selr = sb("selr", [P, CH, P], F32R)
        selw = sb("selw", [24, NE, P], BF16)
        selpm = sb("selpm", [2 * HH, P], BF16)
        neg = sb("neg", [P, SEG], BF16)
        QS = sb("QS", [P, LOADED, GH, S], BF16)
        KS = sb("KS", [P, LOADED, GH, S], BF16)
        QS8 = QS[:, 0:2, :, :].rearrange("p a h t -> p (a h) t")

        big = sb("big", [P, 12288], F32)
        q32 = big[:, 0:4096].rearrange("p (h t) -> p h t", h=HH)
        q16 = big[:, 4096:6144].bitcast(F16).rearrange("p (h t) -> p h t", h=HH)
        v = big[:, 6144:8192].rearrange("p (t n) -> p t n", t=NT)
        PT = big[:, 8192:12288].rearrange("p (t h q) -> p t h q", t=NT, h=HH)
        v1 = big[:, 6144:8192].rearrange("p (t h c) -> p t h c", t=NT, h=H)
        ring = big[:, 8192:12288].rearrange("p (n q) -> p n q", n=RING)
        tmp = big[:, 8192:8192 + 4 * S].rearrange("p (a t) -> p a t", a=4)
        pq = big[:, 8192 + 4 * S:8192 + 7 * S].bitcast(BF16).rearrange("p (j a t) -> p j a t", j=2, a=3)

        xin = sb("xin", [P, NT, P], F32)
        x = sb("x", [P, NT, P], F32)
        x1 = sb("x1", [P, NT, P], F32)
        xn = sb("xn", [P, NT, P], F32)
        hn = sb("hn", [P, NT, P], F32)
        xT = sb("xT", [P, S], F32)
        hT = sb("hT", [P, S], F32)
        xTs = [sb(f"xTs{i}", [P, S], F32R) for i in range(2)]
        hTs = [sb(f"hTs{i}", [P, S], F32R) for i in range(2)]
        hT16 = sb("hT16", [P, S], F16)
        st = sb("st", [P, 2 * NT, 6], F32)
        mv = sb("mv", [P, 2 * NT, 2], F32)
        sc = sb("sc", [P, 6, NT], F32)
        half = sb("half", [P, NT], F32)
        rt = sb("rt", [P, 16, NT, NE], F32)
        rw = sb("rw", [P, 12, NT], F32)
        wp = sb("wp", [P, NT, 24], BF16)
        wT = sb("wT", [24, S], BF16)
        mx = sb("mx", [P, 4, NT, HH], F32)
        mp = sb("mp", [P, NT, 2, HH], BF16)
        mT = sb("mT", [2 * HH, S], BF16)
        ppm = sb("ppm", [P, S], F32)
        rds = [sb(f"rds{i}", [P, S], F32R) for i in range(2)]
        spread = sb("spread", [P, 2, S], F32)
        oT = sb("oT", [P, 2, S], F32)
        act = sb("act", [P, 2, S], F32)
        glu = sb("glu", [P, S], F32)
        rd = glu
        glc = sb("glc", [P, 2, S], F32)
        yT = act[:, 0, :]
        xn1 = yout = hn
        ocT = spread[:, 1, :]
        ohT = glu[0:NE, :]
        gm = ppm[0:NE, 0:S // 2].bitcast(BF16)
        mT1 = glc[0:2 * GH, 0, :].bitcast(BF16).rearrange("p (a t) -> p a t", a=2)
        o1v = spread[:, 0, :].rearrange("p (t h d) -> p t h d", t=NT, h=H)
        rdn = sb("rdn", [P, NT, GH], F32)
        mx1 = sb("mx1", [P, 2, NT, GH], F32)
        mp1 = sb("mp1", [P, NT, 2, GH], BF16)
        ov = oT
        scratch = nc.dram_tensor("scratch", [2, TERMS, P, S], BF16, kind="Internal").ap()

        mrows0 = nc.dram_tensor("mrows0", [2, 2, HH, S], BF16, kind="Internal").ap()
        mrows1 = nc.dram_tensor("mrows1", [NG, 2, GH, S], BF16, kind="Internal").ap()

        x_d, out_d = ins["x"], out
        staged_first = ["wkT", "gbc", "wqT", "pmkT", "mask0", "selpm"]
        staged_second = ["mask1", "selr", "wv", "selw", "wg"]
        staged = ["wu", "w1", "qk1"]
        direct = {"wo0": wo0, "wd": wd, "w2": w2, "pmv": pmv, "b2": b2,
                  "rank": rank, "esel": esel, "epm": epm, "cos": cos, "sin": sin}
        at, place = 0, {}
        for name in staged_first + staged_second + staged:
            if name == staged_second[0]:
                assert at <= 4096
                at = 12288 - sum(ins[rest].shape[1] for rest in staged_second + staged)
            rows, cols = ins[name].shape
            place[name] = big[0:rows, at:at + cols]
            at += cols
        assert at == 12288
        fold = [k for k in range(8) if k != plan["hT"][0]][:6]

        block = ctx.enter_context(nc.Block())

        @block.sync
        def _(sp):
            sp.dma_start(xin[:, :, :], x_d[0].rearrange("(t p) d -> p t d", p=P)).then_inc(sem["x_loaded"], 16)
            sp.dma_start(small[:, :], ins["small"]).then_inc(s_first, 16)
            for name in staged_first:
                sp.dma_start(place[name], ins[name]).then_inc(s_first, 16)
            for name in staged_second:
                sp.dma_start(place[name], ins[name]).then_inc(s_second, 16)
            for name in staged:
                sp.dma_start(place[name], ins[name]).then_inc(s_load, 16)
            for name, t in direct.items():
                dst = t[tuple([slice(None)] * len(t.shape))]
                src = ins[name]
                if len(dst.shape) == 3:
                    src = src.rearrange("p (a b) -> p a b", a=dst.shape[1])
                sp.dma_start(dst, src).then_inc(s_load, 16)
            for name, n in START.items():
                sp.sem_inc(sem[name], n)

            def rows0(up, a):
                sp.wait_ge(sem["maxT_copied"], up("maxT_copied", a + 1))
                sp.dma_start(mrows0[a].rearrange("j h t -> (j h) t"), mT[:, :]).then_inc(sem["max_stored"], 16)
                sp.wait_ge(sem["max_stored"], up("max_stored", 16 * (a + 1)))
                sp.dma_start(QS8[MROW:MROW + 2, :, :], mrows0[a]).then_inc(sem["max_rows"], 16)

            sp.wait_ge(s_clear, CLEARED)
            rows0(lambda name, n: START.get(name, 0) + n, 0)
            with sp.Fori(0, BATCH) as b:
                def up(name, n):
                    return b * PER[name] + START.get(name, 0) + n

                sp.wait_ge(sem["x1_ready"], up("x1_ready", 0))
                sp.dma_start(x[:, :, :], x_d[bass.ds(b, 1), :, :].rearrange("a (t p) d -> p (a t) d", p=P)).then_inc(sem["residual_loaded"], 16)
                sp.wait_ge(sem["xn_ready"], up("xn_ready", NT))
                sp.dma_start(xin[:, :, :], x_d[bass.ds(b + 1, 1), :, :].rearrange("a (t p) d -> p (a t) d", p=P)).then_inc(sem["x_loaded"], 16)
                sp.wait_ge(sem["scores_made"], up("scores_made", NT))
                sp.nop(nofuse=True)
                rows0(up, 1)
                for part, first, n in Q_TERMS:
                    sp.wait_ge(sem["rope"], up("rope", (4, 6, 7)[part]))
                    sp.dma_start(scratch[0, first:first + n].rearrange("m p t -> p m t"),
                                 pq[:, 0, part:part + 1, :].broadcast_to([P, n, S])).then_inc(sem["parts_stored"], 16)
                for parts, first in K_TERMS:
                    sp.wait_ge(sem["rope"], up("rope", 7 + (4, 6, 7)[parts - 1]))
                    sp.dma_start(scratch[1, first:first + parts].rearrange("m p t -> p m t"), pq[:, 1, 0:parts, :]).then_inc(sem["parts_stored"], 16)
                sp.wait_ge(sem["parts_stored"], up("parts_stored", PER["parts_stored"]))

                def load_group(g):
                    for j, dst in enumerate((QS, KS)):
                        sp.dma_start(dst[0:TERMS * DH1, g % LOADED, :, :],
                                     scratch[j].rearrange("m (d h) t -> (m d) h t", h=H)[:, GH * g:GH * (g + 1), :])\
                            .then_inc(sem[f"parts_loaded{g % LOADED}"], 16)

                def rows_group(g):
                    sp.wait_ge(sem["maxT1_copied"], up("maxT1_copied", g + 1))
                    sp.dma_start(mrows1[g].rearrange("j h t -> (j h) t"), mT1[:, g % 2, :]).then_inc(sem[f"max1_stored{g % 2}"], 16)
                    sp.wait_ge(sem[f"max1_stored{g % 2}"], up(f"max1_stored{g % 2}", 16 * (g // 2 + 1)))
                    sp.dma_start(QS[MROW:MROW + 2, g % LOADED, :, :], mrows1[g]).then_inc(sem[f"max1_rows{g % 2}"], 16)

                for g in range(LOADED):
                    load_group(g)
                for g in range(NG):
                    rows_group(g)
                    if g + 2 >= LOADED and g + 2 < NG:
                        sp.wait_ge(sem["scores1_made"], up("scores1_made", NEJ * (g + 3 - LOADED)))
                        load_group(g + 2)
                sp.wait_ge(sem["scores1_made"], up("scores1_made", N1))
                sp.nop(nofuse=True)
                rows0(lambda name, n: up(name, n + PER[name]), 0)
                sp.wait_ge(sem["out_ready"], up("out_ready", 1))
                sp.dma_start(out_d[bass.ds(b, 1), :, :].rearrange("a (t p) d -> p (a t) d", p=P), yout[:, :, :]).then_inc(sem["stored"], 16)
            sp.wait_ge(sem["stored"], BATCH * PER["stored"] + START["stored"])
            sp.wait_ge(sem["max_rows"], BATCH * PER["max_rows"] + START.get("max_rows", 0) + 16)


        @block.tensor
        def _(pe):
            pe.wait_ge(s_first, 16 * (1 + len(staged_first)))
            pe.wait_ge(s_set, SETUP_KEYS)
            for h in range(H):
                r, c = DH0 * (h % 2), h // 2
                rows = slice(r, r + DH0)
                mm = pe.matmul(banks[:, fold[2 * (h % 2) + c // 4], P * (c % 4):P * (c % 4) + P], place["wqT"][rows, P * c:P * c + P],
                               place["wkT"][rows, P * c:P * c + P], start=True, stop=True)
            mm.then_inc(s_setpe, 1)
            for h in range(H):
                r, c = DH0 * (h % 2), h // 2
                rows = slice(r, r + DH0)
                mm = pe.matmul(banks[:, fold[4 + h % 2], PM * c:PM * (c + 1)], place["wqT"][rows, P * c:P * c + P],
                               place["pmkT"][rows, PM * h:PM * (h + 1)], start=True, stop=True)
            mm.then_inc(s_setpe, 1)


            def three(o, w, m, first=True, last=True):
                pe.matmul(o, w[0], m[0], start=first, stop=False, skip_group_check=True)
                pe.matmul(o, w[1], m[0], start=False, stop=False, skip_group_check=True)
                return pe.matmul(o, w[0], m[1], start=False, stop=last, skip_group_check=True)

            def turn(o, src, wait, dt=F32, rows=P):
                o = o if dt == F32 else o.bitcast(BF16)
                for t in range(NT):
                    wait(t)
                    mm = pe.transpose(o[0:rows, P * t:P * (t + 1)], src(t), (ident if dt == F32 else identb[:, :]))
                return mm

            def turn_h(up, claim):
                turn(claim("hT"), lambda t: hn[:, t, :], lambda t: pe.wait_ge(sem["h_ready"], up("h_ready", t + 1)))\
                    .then_inc(sem["hT_made"], 1)

            def queries(up, claim, a, heads):
                pe.wait_ge(sem["h_splits"], up("h_splits", 2))
                for h in heads:
                    o = claim(("q", a, h))
                    three(o, [w[:, HH * a + h, :] for w in aq], [m[:, :] for m in hTs]).then_inc(sem["q_made"], 1)

            def values0(up, claim, a, tiles):
                for t in tiles:
                    o = claim(("v", a, t))
                    three(o, [m[:, P * t:P * (t + 1)] for m in hTs], [w[:, S * a:S * (a + 1)] for w in wv])\
                        .then_inc(sem["v_made"], 1)

            def rough0(up, claim, a):
                o = claim(("rough_pm", a))
                pe.wait_ge(sem["h_splits"], up("h_splits", 3))
                for t in range(NT):
                    mm = pe.matmul(o[:, P * t:P * (t + 1)], hT16[:, P * t:P * (t + 1)],
                                   gpm16[:, P * a:P * (a + 1)], start=True, stop=True)
                mm.then_inc(sem["rough_pm_made"], 1)
                for t in range(NT):
                    o = claim(("rough", a, t))
                    pe.matmul(o.rearrange("p (h k) -> p h k", h=HH), identb[:, :],
                              mask0[:, :].rearrange("p (o k) -> p o k", o=1).broadcast_to([P, HH, SEG]),
                              start=True, stop=False, skip_group_check=True)
                    for h in range(HH):
                        if t == 0:
                            pe.wait_ge(sem["q16_made"], up("q16_made", HH * a + h + 1))
                        for w in range(2):
                            k = P * t + SEG * w
                            mm = pe.matmul(o[SEG * w:SEG * (w + 1), SEG * h:SEG * (h + 1)], q16[:, h, k:k + SEG],
                                           hT16[:, k:k + SEG], start=False, stop=(h == HH - 1), skip_group_check=True)
                    mm.then_inc(sem["rough_made"], 1)

            def turn_maxima0(up, claim, a):
                turn(claim(("maxT", a)), lambda t: mp[:, t, :, :].rearrange("p c h -> p (c h)"),
                     lambda t: pe.wait_ge(sem["max0"], up("max0", 9 * (a + 1))) if t == 0 else None,
                     BF16, rows=2 * HH).then_inc(sem["maxT_made"], 1)

            def turn_x(up, claim):
                turn(claim("xT"), lambda t: xn[:, t, :], lambda t: pe.wait_ge(sem["xn_ready"], up("xn_ready", t + 1)))\
                    .then_inc(sem["xT_made"], 1)

            def route_product(up, claim):
                z = claim("z")
                pe.wait_ge(sem["xT_copied"], up("xT_copied", 1))
                for t in range(NT):
                    mm = pe.matmul(z[:, NE * t:NE * (t + 1)], xT[:, P * t:P * (t + 1)], wr, start=True, stop=True)
                mm.then_inc(sem["z_made"], 1)

            def turn_weights(up, claim):
                turn(claim("wT"), lambda t: wp[:, t, :], lambda t: pe.wait_ge(sem["route0"], up("route0", PER["route0"])) if t == 0 else None,
                     BF16, rows=24).then_inc(sem["wT_made"], 1)

            def up_first(name, n):
                return START.get(name, 0) + n

            freed = {}

            def claim_first(job):
                before = freed.get(plan[job][0])
                if before:
                    pe.wait_ge(sem[before[0]], up_first(*before))
                kind, last = (job, 0) if isinstance(job, str) else (job[0], job[-1])
                freed[plan[job][0]] = {
                    "hT": ("hT_copied", 1), "q": ("q_copied", last + 1), "rough_pm": ("max0", 1),
                    "rough": ("max0", last + 2), "maxT": ("maxT_copied", 1), "xT": ("xT_copied", 1),
                    "z": ("route0", 1), "v": ("v_copied", last + 1), "wT": ("wT_copied", 1)}[kind]
                return bank(job)

            turn_h(up_first, claim_first)
            pe.wait_ge(s_set, SETUP_FIRST)
            queries(up_first, claim_first, 0, range(HH))
            rough0(up_first, claim_first, 0)
            turn_maxima0(up_first, claim_first, 0)
            turn_x(up_first, claim_first)
            route_product(up_first, claim_first)
            pe.wait_ge(s_load, 16 * (len(staged) + len(direct)))
            pe.wait_ge(s_set, SETUP_ALL)
            pe.wait_ge(s_clear, CLEARED)
            values0(up_first, claim_first, 0, range(NT))
            turn_weights(up_first, claim_first)
            for name, n in (("q_copied", HH), ("v_copied", NT), ("maxT_copied", 1), ("xT_copied", 1), ("wT_copied", 1)):
                pe.wait_ge(sem[name], up_first(name, n))

            with pe.Fori(0, BATCH) as b:
                def up(name, n):
                    return b * PER[name] + START.get(name, 0) + n

                def up_next(name, n):
                    return up(name, n + PER[name])

                def claim(job):
                    before = plan[job][1]
                    pe.wait_ge(sem[before[0]], up(*before))
                    return bank(job)

                def expert0(e):
                    o = claim(("wb", e))
                    pe.wait_ge(sem["wT_copied"], up("wT_copied", 1))
                    pe.matmul(o, selw[:, e, :], wT[:, :], start=True, stop=True).then_inc(sem["wb_made"], 1)
                    o = claim(("gate", e))
                    pe.wait_ge(sem["x_splits"], up("x_splits", 2))
                    three(o, [w[:, e, :] for w in wg], [m[:, :] for m in xTs]).then_inc(sem["gate_made"], 1)
                    o = claim(("up", e))
                    three(o, [w[:, e, :] for w in wu], [m[:, :] for m in xTs]).then_inc(sem["up_made"], 1)

                def down0(e):
                    pe.wait_ge(sem["glu_c"], up("glu_c", e + 1))
                    if e == 0:
                        pe.wait_ge(sem["y1_copied"], up("y1_copied", 0))
                    pe.matmul(ysum, wd[:, e, :], glc[:, e % 2, :], start=(e == 0), stop=(e == NE - 1),
                              skip_group_check=True).then_inc(sem["down0_added"], 1)

                def down1(e):
                    pe.wait_ge(sem["gelu_made"], up("gelu_made", e + 1))
                    pe.matmul(ysum, w2[:, e, :], act[:, e % 2, :], start=False, stop=False, skip_group_check=True)\
                        .then_inc(sem["down1_added"], 1)

                def out0(a, c):
                    pe.wait_ge(sem["oT_made"], up("oT_made", CH * a + c + 1))
                    pe.matmul(ysum, wo0[:, CH * a + c, :], oT[:, c % 2, :], start=False, stop=False,
                              skip_group_check=True).then_inc(sem["out0_added"], 1)

                def weighted_values0(a, c):
                    o = claim(("pv", a, c))
                    if c == 0:
                        pe.wait_ge(sem["v_copied"], up("v_copied", NT * (a + 1)))
                    pe.matmul(o, pmv[:, CH * a + c, :], ppm[:, :], start=True, stop=False, skip_group_check=True)
                    for t in range(NT):
                        for r in range(2):
                            h = 2 * c + r
                            mm = pe.matmul(o[DH0 * r:DH0 * (r + 1), P * t:P * (t + 1)], v[:, t, DH0 * h:DH0 * (h + 1)],
                                           PT[:, t, h, :], start=False, stop=True, skip_group_check=True)
                    mm.then_inc(sem["pv_made"], 1)
                    o = claim(("spread", a, c))
                    if c == 0:
                        pe.wait_ge(sem["rden_made"], up("rden_made", 3 * (a + 1)))
                    pe.matmul(o, selr[:, c, :], rds[1][:, :], start=True, stop=True, skip_group_check=True)\
                        .then_inc(sem["spread_made"], 1)

                for a in range(2):
                    o = claim(("pm_scores", a))
                    pe.wait_ge(sem["maxT_copied"], up("maxT_copied", a + 1))
                    pe.matmul(o, selpm[:, :], mT[:, :], start=True, stop=False, skip_group_check=True)
                    pe.matmul(o, gpm[:, P * a:P * (a + 1)], hT[:, :], start=False, stop=True, skip_group_check=True)\
                        .then_inc(sem["pm_scores"], 1)
                    pe.wait_ge(sem["max_rows"], up("max_rows", 16 * (a + 1)))
                    for t in range(NT):
                        o = claim(("scores", a, t))
                        for w in range(2):
                            k = P * t + SEG * w
                            pe.matmul(o[SEG * w:SEG * (w + 1), :].rearrange("p (h q) -> p h q", h=HH), neg[0:MROW + 2, :],
                                      QS8[0:MROW + 2, :, k:k + SEG], start=True, stop=False, skip_group_check=True)
                        for w in range(2):
                            k = P * t + SEG * w
                            mm = pe.matmul(o[SEG * w:SEG * (w + 1), :].rearrange("p (h q) -> p h q", h=HH), hT[:, k:k + SEG],
                                           q32[:, :, k:k + SEG], start=False, stop=True, skip_group_check=True)
                        mm.then_inc(sem["scores_made"], 1)
                    if a:
                        turn_h(up_next, claim)
                    expert0(4 * a)
                    expert0(4 * a + 1)
                    o = claim(("den", a))
                    pe.wait_ge(sem["pm_probs"], up("pm_probs", a + 1))
                    for j in range(4):
                        pe.matmul(o[32 * j:32 * j + 32, :], epm[:, j, :], ppm[:, :], start=True, stop=False,
                                  skip_group_check=True)
                    for t in range(NT):
                        pe.wait_ge(sem["probs_masked"], up("probs_masked", 8 * a + 2 * t + 2))
                        for h in range(HH):
                            j = h % 4
                            mm = pe.matmul(o[32 * j:32 * j + 32, P * t:P * (t + 1)], esel[:, h // 4, :], PT[:, t, h, :],
                                           start=False, stop=(h >= 4), skip_group_check=True)
                    mm.then_inc(sem["den_made"], 1)
                    down0(4 * a)
                    if a == 0:
                        queries(up, claim, 1, range(HH))
                    expert0(4 * a + 2)
                    down0(4 * a + 1)
                    weighted_values0(a, 0)
                    if a == 0:
                        rough0(up, claim, 1)
                    weighted_values0(a, 1)
                    out0(a, 0)
                    weighted_values0(a, 2)
                    out0(a, 1)
                    if a == 0:
                        turn_maxima0(up, claim, 1)
                    down0(4 * a + 2)
                    weighted_values0(a, 3)
                    out0(a, 2)
                    expert0(4 * a + 3)
                    out0(a, 3)
                    if a == 0:
                        values0(up, claim, 1, range(NT))
                    if a:
                        queries(up_next, claim, 0, range(Q_FIRST))
                    down0(4 * a + 3)
                turn(claim("y0"), lambda t: yT[:, P * t:P * (t + 1)],
                     lambda t: pe.wait_ge(sem["y0_copied"], up("y0_copied", 1)) if t == 0 else None).then_inc(sem["y0_turned"], 1)
                queries(up_next, claim, 0, range(Q_FIRST, HH))

                turn(claim("x1T"), lambda t: xn1[:, t, :], lambda t: pe.wait_ge(sem["xn1_ready"], up("xn1_ready", t + 1)))\
                    .then_inc(sem["x1T_made"], 1)
                o = claim("z1")
                pe.wait_ge(sem["x1T_copied"], up("x1T_copied", 1))
                for t in range(NT):
                    mm = pe.matmul(o[:, NE * t:NE * (t + 1)], xT[:, P * t:P * (t + 1)], wgate, start=True, stop=True)
                mm.then_inc(sem["z1_made"], 1)
                o = claim("v1")
                for t in range(NT):
                    mm = pe.matmul(o[:, P * t:P * (t + 1)], xT[:, P * t:P * (t + 1)], wv1, start=True, stop=True)
                mm.then_inc(sem["v1_made"], 1)
                turn(claim("pick"), lambda t: rt[:, 5, t, :],
                     lambda t: pe.wait_ge(sem["route1"], up("route1", 6)) if t == 0 else None, rows=NE).then_inc(sem["pick_turned"], 1)
                pe.wait_ge(sem["splits1"], up("splits1", 2))
                for j in range(4):
                    o = claim(("rope", j))
                    three(o, [w[:, j, :] for w in qk1], [m[:, :] for m in xTs]).then_inc(sem["rope_in"], 1)
                pe.wait_ge(sem["route1"], up("route1", 8))
                pe.wait_ge(sem["y0_copied"], up("y0_copied", 1))
                pe.matmul(ysum, b2[:, :], ohT, start=True, stop=False, skip_group_check=True)

                def hidden(e):
                    o = claim(("hidden", e))
                    pe.matmul(o, selw[0:NE, e, :], gm, start=True, stop=False, skip_group_check=True)
                    three(o, [w[:, e, :] for w in w1], [m[:, :] for m in xTs], first=False).then_inc(sem["hidden_made"], 1)
                    if e:
                        down1(e - 1)

                for e in range(NE):
                    if e not in EXPERT_AT.values():
                        hidden(e)

                rough0(up_next, claim, 0)

                def rough_job(m):
                    g, (t, h0, k, w) = m // NMJ, MAX_JOBS[m % NMJ]
                    o = claim(("rough1", m))
                    if m % NMJ == 0:
                        parts = f"parts_loaded{g % LOADED}"
                        pe.wait_ge(sem[parts], up(parts, 32 * (g // LOADED + 1)))
                    if t == 0:
                        pe.matmul(o, identb[:, :], mask1[:, :], start=True, stop=False, skip_group_check=True)
                    else:
                        for j in range(k):
                            pe.matmul(o[:, w * j + w - P:w * (j + 1)], identb[:, :], mask1[:, 0:P], start=(j == 0),
                                      stop=False, skip_group_check=True)
                    for j in range(k):
                        mm = pe.matmul(o[:, w * j:w * (j + 1)], QS[0:MROW, g % LOADED, h0 + j, P * t:P * (t + 1)],
                                       KS[0:MROW, g % LOADED, h0 + j, 0:w], start=False, stop=(j == k - 1),
                                       skip_group_check=True)
                    mm.then_inc(sem["rough1_made"], 1)

                def scores_job(m):
                    g, (i, h0, k, w) = m // NEJ, EXP_JOBS[m % NEJ]
                    if m % NEJ == 0:
                        pe.wait_ge(sem[f"max1_rows{g % 2}"], up(f"max1_rows{g % 2}", 16 * (g // 2 + 1)))
                    o = claim(("scores1", m))
                    for j in range(k):
                        mm = pe.matmul(o[:, w * j:w * (j + 1)], KS[0:MROW + 2, g % LOADED, h0 + j, P * i:P * (i + 1)],
                                       QS[0:MROW + 2, g % LOADED, h0 + j, P * i:S], start=(j == 0), stop=(j == k - 1),
                                       skip_group_check=True)
                    mm.then_inc(sem["scores1_made"], 1)

                def values_job(g, i):
                    if i == 0:
                        claim(("pv1", g))
                    if g == 0 and i == 0:
                        pe.wait_ge(sem["v1_copied"], up("v1_copied", 1))
                    o = bank(("pv1", g))
                    pe.wait_ge(sem["probs1_masked"], up("probs1_masked", NEJ * g + TILE_ENDS[i] + 1))
                    for n, (tile, h0, k, w) in enumerate(EXP_JOBS):
                        if tile == i:
                            for h in range(h0, h0 + k):
                                mm = pe.matmul(o[32 * h:32 * h + 32, P * i:S], v1[:, i, GH * g + h, :],
                                               ring[:, (NEJ * g + n) % RING, w * (h - h0):w * (h - h0 + 1)],
                                               start=(i == 0), stop=(i == NT - 1), skip_group_check=True)
                    mm.then_inc(sem["values1_made"], 1)

                for slot in range(SLOTS):
                    if slot < N1:
                        rough_job(slot)
                    if 0 <= slot - S_LAG < N1:
                        scores_job(slot - S_LAG)
                    if 0 <= slot - V_LAG < N1 and (slot - V_LAG) % NEJ in TILE_ENDS:
                        values_job((slot - V_LAG) // NEJ, TILE_ENDS.index((slot - V_LAG) % NEJ))
                    if slot in EXPERT_AT:
                        hidden(EXPERT_AT[slot])
                    if slot == LAST_DOWN:
                        down1(NE - 1)
                    if slot == TURN_X:
                        turn_x(up_next, claim)
                    if slot == TURN_Z:
                        route_product(up_next, claim)
                    for g in range(NG):
                        if slot == maxima_slot(g) + MAX_TURN:
                            turn(claim(("maxT1", g)), lambda t: mp1[:, t, :, :].rearrange("p c h -> p (c h)"),
                                 lambda t: pe.wait_ge(sem["max1_parts"], up("max1_parts", 3 * (g + 1))) if t == 0 else None,
                                 BF16, rows=2 * GH).then_inc(sem["maxT1_made"], 1)
                        if slot == values_slot(g) + 1:
                            turn(claim(("o1", g)), lambda t: ov[:, g % 2, P * t:P * (t + 1)],
                                 lambda t: pe.wait_ge(sem["pv1_copied"], up("pv1_copied", g + 1)) if t == 0 else None)\
                                .then_inc(sem["o1_turned"], 1)
                turn_maxima0(up_next, claim, 0)
                values0(up_next, claim, 0, range(2))
                turn(claim("ocT"), lambda t: o1v[:, t, :, :].rearrange("p h d -> p (h d)"),
                     lambda t: pe.wait_ge(sem["o1_ready"], up("o1_ready", 2 * NG)) if t == 0 else None).then_inc(sem["ocT_made"], 1)
                values0(up_next, claim, 0, range(2, NT))
                pe.wait_ge(sem["ocT_copied"], up("ocT_copied", 1))
                pe.matmul(ysum, wo1, ocT, start=False, stop=True, skip_group_check=True).then_inc(sem["out1_added"], 1)
                turn_weights(up_next, claim)
                turn(claim("y1"), lambda t: yT[:, P * t:P * (t + 1)],
                     lambda t: pe.wait_ge(sem["y1_copied"], up("y1_copied", 1)) if t == 0 else None).then_inc(sem["y1_turned"], 1)

        @block.scalar
        def _(scalar):
            def copy(up, dst, src, made, n, done):
                scalar.wait_ge(sem[made], up(made, n))
                scalar.activation(dst, src, ACT.Copy).then_inc(sem[done], 1)

            def queries(up, a, heads):
                for h in heads:
                    copy(up, q32[:, h, :], bank(("q", a, h)), "q_made", HH * a + h + 1, "q_copied")

            def values0(up, a, tiles):
                for t in tiles:
                    copy(up, v[:, t, :], bank(("v", a, t)), "v_made", NT * a + t + 1, "v_copied")

            def route_tanh(up):
                scalar.wait_ge(sem["route0"], up("route0", 1))
                scalar.activation(rt[:, 1, :, :], rt[:, 0, :, :], ACT.Tanh, scale=0.5).then_inc(sem["route_tanh"], 1)

            def route_exp(up):
                scalar.wait_ge(sem["route0"], up("route0", 5))
                scalar.activation(rt[:, 5, :, :], rt[:, 4, :, :], ACT.Exp, scale=10.0).then_inc(sem["route_exp"], 1)
                scalar.activation(rt[:, 6, :, :], rt[:, 4, :, :], ACT.Exp, scale=1.0 / 0.3).then_inc(sem["route_exp"], 1)

            def up_first(name, n):
                return START.get(name, 0) + n

            copy(up_first, hT[:, :], bank("hT"), "hT_made", 1, "hT_copied")
            queries(up_first, 0, range(HH))
            copy(up_first, xT[:, :], bank("xT"), "xT_made", 1, "xT_copied")
            route_tanh(up_first)
            route_exp(up_first)
            values0(up_first, 0, range(NT))
            with scalar.Fori(0, BATCH) as b:
                def up(name, n):
                    return b * PER[name] + START.get(name, 0) + n

                def up_next(name, n):
                    return up(name, n + PER[name])

                def tanh0(e):
                    scalar.wait_ge(sem["gate_made"], up("gate_made", e + 1))
                    if e >= 2:
                        scalar.wait_ge(sem["glu_a"], up("glu_a", e - 1))
                    if e == 0:
                        scalar.wait_ge(sem["y1_turned"], up("y1_turned", 0))
                    scalar.activation(act[:, e % 2, :], bank(("gate", e)), ACT.Tanh, scale=0.5).then_inc(sem["tanh_made"], 1)

                def spread0(a, c):
                    n = CH * a + c
                    if n >= 2:
                        scalar.wait_ge(sem["oT_made"], up("oT_made", n - 1))
                    copy(up, spread[:, c % 2, :], bank(("spread", a, c)), "spread_made", n + 1, "spread_copied")

                for a in range(2):
                    scalar.wait_ge(sem["pm_scores"], up("pm_scores", a + 1))
                    scalar.activation(ppm[:, :], bank(("pm_scores", a)), ACT.Exp).then_inc(sem["pm_probs"], 1)
                    scalar.wait_ge(sem["pt_zeroed"], up("pt_zeroed", 2))
                    for t in range(NT):
                        scalar.wait_ge(sem["scores_made"], up("scores_made", NT * a + t + 1))
                        for w in range(2):
                            rows = slice(SEG * w, SEG * (w + 1))
                            scalar.activation(PT[rows, t, :, SEG * w:SEG * (w + 1)],
                                              bank(("scores", a, t))[rows, :].rearrange("p (h q) -> p h q", h=HH),
                                              ACT.Exp).then_inc(sem["probs_made"], 1)
                    if a:
                        copy(up_next, hT[:, :], bank("hT"), "hT_made", 1, "hT_copied")
                    tanh0(4 * a)
                    tanh0(4 * a + 1)
                    if a == 0:
                        queries(up, 1, range(HH))
                    tanh0(4 * a + 2)
                    for c in range(CH):
                        spread0(a, c)
                    tanh0(4 * a + 3)
                    if a == 0:
                        scalar.wait_ge(sem["pv_made"], up("pv_made", CH))
                        values0(up, 1, range(NT))
                copy(up, yT, ysum, "down0_added", NE, "y0_copied")
                queries(up_next, 0, range(HH))
                copy(up, xT[:, :], bank("x1T"), "x1T_made", 1, "x1T_copied")
                scalar.wait_ge(sem["v1_filled"], up("v1_filled", 2))
                copy(up, v1[:, :, :, 0:DH1].rearrange("p t h d -> p (t h) d"), bank("v1").rearrange("p (n d) -> p n d", d=DH1),
                     "v1_made", 1, "v1_copied")

                def gelu(e):
                    scalar.wait_ge(sem["hidden_made"], up("hidden_made", e + 1))
                    if e >= 2:
                        scalar.wait_ge(sem["down1_added"], up("down1_added", e - 1))
                    scalar.activation(act[:, e % 2, :], bank(("hidden", e)), ACT.Gelu, bias=b1T[:, e:e + 1]).then_inc(sem["gelu_made"], 1)

                for e in range(NE):
                    gelu(e)
                for slot in range(SLOTS):
                    if slot == TURN_X:
                        copy(up_next, xT[:, :], bank("xT"), "xT_made", 1, "xT_copied")
                    if slot == ROUTE_AT:
                        route_tanh(up_next)
                    if slot == ROUTE_AT + 1:
                        route_exp(up_next)
                    m = slot - S_LAG
                    if 0 <= m < N1:
                        i, h0, k, w = EXP_JOBS[m % NEJ]
                        scalar.wait_ge(sem["scores1_made"], up("scores1_made", m + 1))
                        if m >= RING:
                            g, n = (m - RING) // NEJ, (m - RING) % NEJ
                            scalar.wait_ge(sem["values1_made"], up("values1_made", NT * g + EXP_JOBS[n][0] + 1))
                        scalar.activation(ring[:, m % RING, 0:w * k], bank(("scores1", m))[:, 0:w * k], ACT.Exp)\
                            .then_inc(sem["probs1_made"], 1)
                    for g in range(NG):
                        if slot == values_slot(g):
                            if g >= 2:
                                scalar.wait_ge(sem["o1_turned"], up("o1_turned", g - 1))
                            copy(up, ov[:, g % 2, :], bank(("pv1", g)), "values1_made", NT * (g + 1), "pv1_copied")
                values0(up_next, 0, range(2))
                copy(up, ocT, bank("ocT"), "ocT_made", 1, "ocT_copied")
                values0(up_next, 0, range(2, NT))
                copy(up, yT, ysum, "out1_added", 1, "y1_copied")

        @block.gpsimd
        def _(pool):

            def scales(up, layer, rms):
                s, var = f"scales{layer}", mv[:, NT * layer:NT * (layer + 1), 1]
                pool.wait_ge(sem[f"moments{layer}"], up(f"moments{layer}", NT))
                pool.nop(nofuse=True)
                pool.tensor_scalar(sc[:, 0, :], var, 1e-5, None, ALU.add).then_inc(sem[s], 1)
                pool.wait_ge(sem[s], up(s, 1))
                pool.nop(nofuse=True)
                pool.tensor_tensor(sc[:, 1, :], sc[:, 0, :], half[:, :], ALU.pow).then_inc(sem[s], 1)
                if rms:
                    pool.wait_ge(sem[s], up(s, 2))
                    pool.nop(nofuse=True)
                    pool.tensor_tensor(sc[:, 2, :], sc[:, 1, :], sc[:, 1, :], ALU.mult).then_inc(sem[s], 1)
                    pool.wait_ge(sem[s], up(s, 3))
                    pool.nop(nofuse=True)
                    pool.tensor_tensor(sc[:, 3, :], sc[:, 2, :], var, ALU.mult).then_inc(sem[s], 1)
                    pool.wait_ge(sem[s], up(s, 4))
                    pool.nop(nofuse=True)
                    pool.tensor_scalar(sc[:, 4, :], sc[:, 3, :], 1e-6, None, ALU.add).then_inc(sem[s], 1)
                    pool.wait_ge(sem[s], up(s, 5))
                    pool.nop(nofuse=True)
                    pool.tensor_tensor(sc[:, 5, :], sc[:, 4, :], half[:, :], ALU.pow).then_inc(sem[s], 1)

            def zero_windows(up):
                for w in range(2):
                    if w:
                        pool.wait_ge(sem["pt_zeroed"], up("pt_zeroed", 1))
                        pool.nop(nofuse=True)
                    pool.memset(PT[SEG * w:SEG * (w + 1), :, :, SEG * (1 - w):SEG * (2 - w)].rearrange("p t h q -> p (t h) q"), 0.0)\
                        .then_inc(sem["pt_zeroed"], 1)
                pool.wait_ge(sem["pt_zeroed"], up("pt_zeroed", 2))
                pool.nop(nofuse=True)

            def up_first(name, n):
                return START.get(name, 0) + n

            pool.memset(half[:, :], -0.5).then_inc(s_clear, 1)
            pool.wait_ge(s_clear, 1)
            scales(up_first, 0, True)
            pool.memset(QS[:, :, :, :], 0.0).then_inc(s_clear, 1)
            pool.memset(KS[:, :, :, :], 0.0).then_inc(s_clear, 1)
            pool.memset(neg[:, :], 0.0).then_inc(s_clear, 1)
            pool.wait_ge(s_clear, 4)
            pool.memset(KS[MROW:MROW + 2, :, :, :], -1.0).then_inc(s_clear, 1)
            pool.wait_ge(s_clear, 5)
            pool.memset(neg[MROW:MROW + 2, :], -1.0).then_inc(s_clear, 1)
            pool.wait_ge(s_clear, CLEARED)
            pool.wait_ge(s_set, SETUP_ALL)
            zero_windows(up_first)
            with pool.Fori(0, BATCH) as b:
                def up(name, n):
                    return b * PER[name] + START.get(name, 0) + n

                def up_next(name, n):
                    return up(name, n + PER[name])

                for a in range(2):
                    for t in range(NT):
                        for w in range(2):
                            n = 2 * (NT * a + t) + w + 1
                            pool.wait_ge(sem["probs_made"], up("probs_made", n))
                            pool.nop(nofuse=True)
                            if n > 1:
                                pool.wait_ge(sem["probs_masked"], up("probs_masked", n - 1))
                                pool.nop(nofuse=True)
                            block_ = PT[SEG * w:SEG * (w + 1), t, :, SEG * w:SEG * (w + 1)]
                            pool.affine_select(out=block_, in_=block_, compare_op=ALU.is_ge, fill=0.0, base=0,
                                               pattern=[[0, HH], [1, SEG]], channel_multiplier=-1).then_inc(sem["probs_masked"], 1)
                    if a == 0:
                        pool.wait_ge(sem["probs_masked"], up("probs_masked", 8))
                        pool.nop(nofuse=True)
                        scales(up_next, 0, True)
                pool.wait_ge(sem["probs_masked"], up("probs_masked", 16))
                pool.nop(nofuse=True)
                pool.wait_ge(sem["pv_made"], up("pv_made", 2 * CH))
                pool.nop(nofuse=True)
                pool.memset(v1[:, :, :, :], 0.0).then_inc(sem["v1_filled"], 1)
                pool.wait_ge(sem["v1_filled"], up("v1_filled", 1))
                pool.nop(nofuse=True)
                pool.memset(v1[:, :, :, DH1:DH1 + 1], 1.0).then_inc(sem["v1_filled"], 1)
                scales(up, 1, False)
                for m in range(N1):
                    i, h0, k, w = EXP_JOBS[m % NEJ]
                    pool.wait_ge(sem["probs1_made"], up("probs1_made", m + 1))
                    pool.nop(nofuse=True)
                    block_ = ring[:, m % RING, 0:w * k].rearrange("p (h q) -> p h q", h=k)[:, :, 0:P]
                    pool.affine_select(out=block_, in_=block_, compare_op=ALU.is_ge, fill=0.0, base=0,
                                       pattern=[[0, k], [1, P]], channel_multiplier=-1).then_inc(sem["probs1_masked"], 1)
                pool.wait_ge(sem["values1_made"], up("values1_made", NT * NG))
                pool.nop(nofuse=True)
                zero_windows(up_next)

        @block.vector
        def _(dve):
            done = [0]

            def prepare(ins_):
                done[0] += 1
                ins_.then_inc(s_set, 1)
                dve.wait_ge(s_set, done[0])

            def moments(up, layer, src):
                s, m, k = f"stats{layer}", f"moments{layer}", NT * layer
                for t in range(NT):
                    dve.bn_stats(st[:, k + t, :], src[:, t, :]).then_inc(sem[s], 1)
                dve.wait_ge(sem[s], up(s, NT))
                dve.nop(nofuse=True)
                for t in range(NT):
                    dve.bn_aggr(mv[:, k + t, :], st[:, k + t, :]).then_inc(sem[m], 1)

            def norm(up, layer, src, dst, ready):
                k = NT * layer
                dve.wait_ge(sem[f"scales{layer}"], up(f"scales{layer}", 2))
                for t in range(NT):
                    dve.tensor_scalar(dst[:, t, :], src[:, t, :], mv[:, k + t, 0:1], sc[:, 1, t:t + 1],
                                      ALU.subtract, ALU.mult).then_inc(sem[ready], 1)

            def split(up, dst, src, s, n):
                dve.tensor_copy(dst[0][:, :], src[:, :]).then_inc(sem[s], 1)
                dve.wait_ge(sem[s], up(s, n))
                dve.tensor_tensor(dst[1][:, :], src[:, :], dst[0][:, :].bitcast(F32), ALU.subtract).then_inc(sem[s], 1)

            count = {}

            def step(up, name, ins_):
                count[name] += 1
                ins_.then_inc(sem[name], 1)
                dve.wait_ge(sem[name], up(name, count[name]))

            def moments0(up):
                dve.wait_ge(sem["x_loaded"], up("x_loaded", 16))
                moments(up, 0, xin)

            def norm0(up, stored):
                norm(up, 0, xin, xn, "xn_ready")
                dve.wait_ge(sem["scales0"], up("scales0", 6))
                if stored is not None:
                    dve.wait_ge(sem["stored"], stored)
                for t in range(NT):
                    dve.wait_ge(sem["xn_ready"], up("xn_ready", t + 1))
                    dve.tensor_scalar(hn[:, t, :], xn[:, t, :], sc[:, 5, t:t + 1], None, ALU.mult).then_inc(sem["h_ready"], 1)

            def split_h(up):
                dve.wait_ge(sem["hT_copied"], up("hT_copied", 1))
                split(up, hTs, hT, "h_splits", 1)
                dve.tensor_copy(hT16[:, :], hT[:, :]).then_inc(sem["h_splits"], 1)

            def queries16(up, a, heads):
                for h in heads:
                    dve.wait_ge(sem["q_copied"], up("q_copied", HH * a + h + 1))
                    dve.tensor_copy(q16[:, h, :], q32[:, h, :]).then_inc(sem["q16_made"], 1)

            def maxima0(up, a):
                dve.wait_ge(sem["rough_pm_made"], up("rough_pm_made", a + 1))
                count["max0"] = 9 * a
                step(up, "max0", dve.reduce_max(mx[:, 0, :, :], bank(("rough_pm", a)).rearrange("p (t h k) -> p t h k", t=NT, h=HH), AX))
                for t in range(NT):
                    dve.wait_ge(sem["rough_made"], up("rough_made", NT * a + t + 1))
                    count["max0"] += 1
                    dve.reduce_max(mx[:, 1, t, :], bank(("rough", a, t)).rearrange("p (h k) -> p h k", h=HH), AX).then_inc(sem["max0"], 1)
                dve.wait_ge(sem["max0"], up("max0", count["max0"]))
                step(up, "max0", dve.tensor_tensor(mx[:, 2, :, :], mx[:, 0, :, :], mx[:, 1, :, :], ALU.max))
                step(up, "max0", dve.tensor_copy(mp[:, :, 0, :], mx[:, 2, :, :]))
                step(up, "max0", dve.tensor_tensor(mx[:, 3, :, :], mx[:, 2, :, :], mp[:, :, 0, :], ALU.subtract))
                step(up, "max0", dve.tensor_copy(mp[:, :, 1, :], mx[:, 3, :, :]))
                assert count["max0"] == 9 * (a + 1)

            def turned_maxima0(up, a):
                dve.wait_ge(sem["maxT_made"], up("maxT_made", a + 1))
                dve.tensor_copy(mT[:, :], bank(("maxT", a)).bitcast(BF16)[0:2 * HH, 0:S]).then_inc(sem["maxT_copied"], 1)

            def split_x(up):
                dve.wait_ge(sem["xT_copied"], up("xT_copied", 1))
                split(up, xTs, xT, "x_splits", 1)

            R = [rt[:, i, :, :] for i in range(16)]
            T = [rw[:, i, :] for i in range(12)]

            def wide(t):
                return t.rearrange("p (t o) -> p t o", o=1).broadcast_to([P, NT, NE])

            def route_zone(up):
                count["route0"] = 0
                dve.wait_ge(sem["z_made"], up("z_made", 1))
                step(up, "route0", dve.tensor_scalar(R[0], bank("z")[:, 0:NT * NE].rearrange("p (t e) -> p t e", t=NT), rtemp, None, ALU.mult))
                step(up, "route0", dve.tensor_scalar(R[2], R[0], LOGIT_LOWER, None, ALU.is_ge))
                step(up, "route0", dve.scalar_tensor_tensor(R[3], R[0], 0.0, R[2], ALU.is_le, ALU.mult))

            def route_distance(up):
                dve.wait_ge(sem["route_tanh"], up("route_tanh", 1))
                step(up, "route0", dve.tensor_scalar(R[7], R[1], 0.5, 0.5 - CENTER, ALU.mult, ALU.add))
                step(up, "route0", dve.scalar_tensor_tensor(R[4], R[7], -1.0, R[7], ALU.mult, ALU.min))

            def route_sum(up):
                dve.wait_ge(sem["route_exp"], up("route_exp", 2))
                step(up, "route0", dve.tensor_tensor(R[8], R[5], R[3], ALU.mult))
                step(up, "route0", dve.reduce_sum(T[0], R[8], AX))
                step(up, "route0", dve.tensor_scalar(T[1], T[0], 1e-8, None, ALU.is_lt))

            def route_nearest(up, k):
                key, pick = ((R[4], R[11]), (R[12], R[13]))[k]
                step(up, "route0", dve.reduce_max(T[2], key, AX))
                step(up, "route0", dve.tensor_tensor(R[9], key, wide(T[2]), ALU.is_equal))
                step(up, "route0", dve.tensor_tensor(R[10], R[9], rank[:, :, :], ALU.mult))
                step(up, "route0", dve.reduce_max(T[3], R[10], AX))
                step(up, "route0", dve.tensor_tensor(pick, R[10], wide(T[3]), ALU.is_equal))
                if k == 0:
                    step(up, "route0", dve.scalar_tensor_tensor(R[12], R[11], -4.0, R[4], ALU.mult, ALU.add))

            def route_fallback(up):
                step(up, "route0", dve.tensor_tensor(R[11], R[11], R[13], ALU.add))
                step(up, "route0", dve.tensor_tensor(R[12], R[6], R[11], ALU.mult))
                step(up, "route0", dve.reduce_sum(T[4], R[12], AX))
                step(up, "route0", dve.tensor_scalar(T[5], T[4], 1e-8, None, ALU.max))
                step(up, "route0", dve.reciprocal(T[6], T[5]))
                step(up, "route0", dve.tensor_tensor(R[13], R[12], wide(T[6]), ALU.mult))

            def route_choose(up):
                step(up, "route0", dve.tensor_tensor(R[14], R[13], R[8], ALU.subtract))
                step(up, "route0", dve.tensor_tensor(R[9], R[14], wide(T[1]), ALU.mult))
                step(up, "route0", dve.tensor_tensor(R[10], R[9], R[8], ALU.add))
                step(up, "route0", dve.reduce_sum(T[7], R[10], AX))
                step(up, "route0", dve.tensor_scalar(T[8], T[7], 1e-8, None, ALU.max))
                step(up, "route0", dve.reciprocal(T[9], T[8]))
                step(up, "route0", dve.tensor_tensor(R[11], R[10], wide(T[9]), ALU.mult))

            def route_parts(up):
                step(up, "route0", dve.tensor_scalar(R[12], R[11], 0.5, None, ALU.mult))
                step(up, "route0", dve.tensor_copy(wp[:, :, 0:NE], R[12]))
                step(up, "route0", dve.tensor_tensor(R[13], R[12], wp[:, :, 0:NE], ALU.subtract))
                step(up, "route0", dve.tensor_copy(wp[:, :, NE:2 * NE], R[13]))
                step(up, "route0", dve.tensor_tensor(wp[:, :, 2 * NE:3 * NE], R[13], wp[:, :, NE:2 * NE], ALU.subtract))
                assert count["route0"] == PER["route0"], count

            def copy_weights(up):
                dve.wait_ge(sem["wT_made"], up("wT_made", 1))
                dve.tensor_copy(wT[:, :], bank("wT").bitcast(BF16)[0:24, 0:S]).then_inc(sem["wT_copied"], 1)

            def up_first(name, n):
                return START.get(name, 0) + n

            moments0(up_first)
            dve.wait_ge(s_first, 16 * (1 + len(staged_first)))
            keys = place["wkT"].rearrange("p (c d) -> p c d", d=P)
            prepare(dve.tensor_tensor(keys, keys, place["gbc"].rearrange("p (o d) -> p o d", o=1).broadcast_to([P, H // 2, P]), ALU.mult))
            assert done[0] == SETUP_KEYS
            norm0(up_first, None)
            prepare(dve.tensor_scalar(gam8, gam, DH0 ** -0.5, None, ALU.mult))
            prepare(dve.reciprocal(rtemp, temp))
            prepare(dve.tensor_copy(identb[:, :], ident))
            prepare(dve.tensor_copy(mask0[:, :], place["mask0"]))
            prepare(dve.tensor_copy(selpm[:, :], place["selpm"]))

            def split_weights(name, t):
                full = tuple([slice(None)] * len(t[0].shape))
                src = place[name]
                if len(t[0].shape) == 3:
                    src = src.rearrange("p (a b) -> p a b", a=t[0].shape[1])
                prepare(dve.tensor_copy(t[0][full], src))
                prepare(dve.tensor_tensor(t[1][full], src, t[0][full].bitcast(F32), ALU.subtract))

            dve.wait_ge(s_second, 16 * len(staged_second))
            prepare(dve.tensor_copy(mask1[:, :], place["mask1"]))
            prepare(dve.tensor_copy(selr[:, :, :], place["selr"].rearrange("p (a b) -> p a b", a=CH)))
            prepare(dve.tensor_scalar(place["wv"], place["wv"], gam, None, ALU.mult))
            prepare(dve.tensor_copy(selw[:, :, :], place["selw"].rearrange("p (a b) -> p a b", a=NE)))
            split_weights("wv", wv)
            split_weights("wg", wg)
            split_h(up_first)
            dve.wait_ge(s_setpe, 2)
            for n in range(4):
                src = banks[:, fold[n], :].rearrange("p (a b) -> p a b", a=4)
                first = HH * (n % 2) + n // 2
                hi, lo = (t[:, first:HH * (n % 2 + 1):2, :] for t in aq)
                prepare(dve.tensor_scalar(hi, src, gam8, None, ALU.mult))
                prepare(dve.scalar_tensor_tensor(lo, src, gam8, hi.bitcast(F32), ALU.mult, ALU.subtract))
            for r in range(2):
                dst = gpm[:, :].rearrange("p (c r k) -> p c r k", c=H // 2, r=2)[:, :, r, :]
                prepare(dve.tensor_scalar(dst, banks[:, fold[4 + r], 0:P].rearrange("p (c k) -> p c k", k=PM), gam8, None, ALU.mult))
            prepare(dve.tensor_copy(gpm16[:, :], gpm[:, :]))
            assert done[0] == SETUP_FIRST
            dve.wait_ge(s_load, 16 * (len(staged) + len(direct)))
            split_weights("wu", wu)
            queries16(up_first, 0, range(HH))
            maxima0(up_first, 0)
            turned_maxima0(up_first, 0)
            split_x(up_first)
            split_weights("w1", w1)
            prepare(dve.tensor_scalar(place["qk1"][:, 0:2 * P], place["qk1"][:, 0:2 * P], DH1 ** -0.5, None, ALU.mult))
            split_weights("qk1", qk1)
            assert done[0] == SETUP_ALL
            route_zone(up_first)
            route_distance(up_first)
            route_sum(up_first)
            route_nearest(up_first, 0)
            route_nearest(up_first, 1)
            route_fallback(up_first)
            route_choose(up_first)
            route_parts(up_first)
            copy_weights(up_first)
            with dve.Fori(0, BATCH) as b:
                def up(name, n):
                    return b * PER[name] + START.get(name, 0) + n

                def up_next(name, n):
                    return up(name, n + PER[name])

                def glu_fn(e):
                    dve.wait_ge(sem["tanh_made"], up("tanh_made", e + 1))
                    if e:
                        dve.wait_ge(sem["glu_c"], up("glu_c", e))
                    dve.scalar_tensor_tensor(glu[:, :], act[:, e % 2, :], 1.0, bank(("gate", e)), ALU.add, ALU.mult).then_inc(sem["glu_a"], 1)
                    dve.wait_ge(sem["up_made"], up("up_made", e + 1))
                    dve.wait_ge(sem["glu_a"], up("glu_a", e + 1))
                    dve.tensor_tensor(glu[:, :], glu[:, :], bank(("up", e)), ALU.mult).then_inc(sem["glu_b"], 1)
                    dve.wait_ge(sem["glu_b"], up("glu_b", e + 1))
                    if e >= 2:
                        dve.wait_ge(sem["down0_added"], up("down0_added", e - 1))
                    dve.tensor_tensor(glc[:, e % 2, :], glu[:, :], bank(("wb", e)), ALU.mult).then_inc(sem["glu_c"], 1)

                def normalize0(a, c):
                    n = CH * a + c
                    dve.wait_ge(sem["pv_made"], up("pv_made", n + 1))
                    dve.wait_ge(sem["spread_copied"], up("spread_copied", n + 1))
                    if n >= 2:
                        dve.wait_ge(sem["out0_added"], up("out0_added", n - 1))
                    dve.tensor_tensor(oT[:, c % 2, :], bank(("pv", a, c)), spread[:, c % 2, :], ALU.mult).then_inc(sem["oT_made"], 1)

                moments0(up_next)
                for a in range(2):
                    glu_fn(4 * a)
                    glu_fn(4 * a + 1)
                    dve.wait_ge(sem["den_made"], up("den_made", a + 1))
                    if a:
                        dve.wait_ge(sem["spread_made"], up("spread_made", CH))
                    dve.wait_ge(sem["glu_c"], up("glu_c", 4 * a + 2))
                    count["rden_made"] = 3 * a
                    step(up, "rden_made", dve.reciprocal(rd[:, :], bank(("den", a))))
                    step(up, "rden_made", dve.tensor_copy(rds[0][:, :], rd[:, :]))
                    step(up, "rden_made", dve.scalar_tensor_tensor(rds[1][:, :], rds[0][:, :].bitcast(F32), lower, rd[:, :], ALU.mult, ALU.add))
                    if a == 0:
                        queries16(up, 1, range(HH))
                    glu_fn(4 * a + 2)
                    normalize0(a, 0)
                    if a == 0:
                        maxima0(up, 1)
                    normalize0(a, 1)
                    normalize0(a, 2)
                    if a == 0:
                        dve.wait_ge(sem["max_stored"], up("max_stored", 16))
                        dve.wait_ge(sem["pm_scores"], up("pm_scores", 1))
                        turned_maxima0(up, 1)
                    normalize0(a, 3)
                    if a == 0:
                        norm0(up_next, up("stored", 0))
                    else:
                        split_h(up_next)
                    glu_fn(4 * a + 3)

                dve.wait_ge(sem["y0_turned"], up("y0_turned", 1))
                dve.wait_ge(sem["residual_loaded"], up("residual_loaded", 16))
                dve.tensor_tensor(x1[:, :, :], x[:, :, :], bank("y0").rearrange("p (t d) -> p t d", t=NT), ALU.add)\
                    .then_inc(sem["x1_ready"], 1)
                dve.wait_ge(sem["x1_ready"], up("x1_ready", 1))
                moments(up, 1, x1)
                norm(up, 1, x1, xn1, "xn1_ready")
                dve.wait_ge(sem["x1T_copied"], up("x1T_copied", 1))
                split(up, xTs, xT, "splits1", 1)
                count["route1"] = 0
                dve.wait_ge(sem["z1_made"], up("z1_made", 1))
                bgw = bg.rearrange("p (o e) -> p o e", o=1).broadcast_to([P, NT, NE])
                step(up, "route1", dve.tensor_tensor(R[1], bank("z1")[:, 0:NT * NE].rearrange("p (t e) -> p t e", t=NT), bgw, ALU.add))
                step(up, "route1", dve.reduce_max(T[0], R[1], AX))
                step(up, "route1", dve.tensor_tensor(R[2], R[1], wide(T[0]), ALU.is_equal))
                step(up, "route1", dve.tensor_tensor(R[3], R[2], rank[:, :, :], ALU.mult))
                step(up, "route1", dve.reduce_max(T[1], R[3], AX))
                step(up, "route1", dve.tensor_tensor(R[5], R[3], wide(T[1]), ALU.is_equal))
                dve.wait_ge(sem["pick_turned"], up("pick_turned", 1))
                step(up, "route1", dve.tensor_copy(ohT, bank("pick")[0:NE, :]))
                step(up, "route1", dve.tensor_scalar(gm, ohT, 1.0, -MASKED, ALU.subtract, ALU.mult))
                for j in range(2):
                    count["rope"] = 7 * j
                    dve.wait_ge(sem["rope_in"], up("rope_in", 2 * j + 1))
                    step(up, "rope", dve.tensor_tensor(tmp[:, 0, :], bank(("rope", 2 * j)), cos[:, :], ALU.mult))
                    dve.wait_ge(sem["rope_in"], up("rope_in", 2 * j + 2))
                    step(up, "rope", dve.tensor_tensor(tmp[:, 1, :], bank(("rope", 2 * j + 1)), sin[:, :], ALU.mult))
                    step(up, "rope", dve.tensor_tensor(tmp[:, 2, :], tmp[:, 0, :], tmp[:, 1, :], ALU.add))
                    step(up, "rope", dve.tensor_copy(pq[:, j, 0, :], tmp[:, 2, :]))
                    step(up, "rope", dve.tensor_tensor(tmp[:, 3, :], tmp[:, 2, :], pq[:, j, 0, :], ALU.subtract))
                    step(up, "rope", dve.tensor_copy(pq[:, j, 1, :], tmp[:, 3, :]))
                    step(up, "rope", dve.tensor_tensor(pq[:, j, 2, :], tmp[:, 3, :], pq[:, j, 1, :], ALU.subtract))
                dve.wait_ge(sem["rough_made"], up("rough_made", 2 * NT))
                queries16(up_next, 0, range(HH))
                maxima0(up_next, 0)

                def normalize(g):
                    dve.wait_ge(sem["o1_turned"], up("o1_turned", g + 1))
                    o = bank(("o1", g)).rearrange("p (t h c) -> p t h c", t=NT, h=GH)
                    dve.reciprocal(rdn[:, :, :], o[:, :, :, DH1]).then_inc(sem["o1_ready"], 1)
                    dve.wait_ge(sem["o1_ready"], up("o1_ready", 2 * g + 1))
                    dve.tensor_tensor(o1v[:, :, GH * g:GH * (g + 1), :], o[:, :, :, 0:DH1],
                                      rdn[:, :, :].rearrange("p t (h o) -> p t h o", o=1).broadcast_to([P, NT, GH, DH1]), ALU.mult)\
                        .then_inc(sem["o1_ready"], 1)

                for slot in range(SLOTS):
                    if slot < N1:
                        t, h0, k, w = MAX_JOBS[slot % NMJ]
                        dve.wait_ge(sem["rough1_made"], up("rough1_made", slot + 1))
                        dve.reduce_max(mx1[:, 0, t, h0:h0 + k], bank(("rough1", slot))[:, 0:w * k].rearrange("p (h k) -> p h k", h=k), AX)\
                            .then_inc(sem["max1"], 1)
                    for g in range(NG):
                        if slot == maxima_slot(g):
                            dve.wait_ge(sem["max1"], up("max1", NMJ * (g + 1)))
                            count["max1_parts"] = 3 * g
                            step(up, "max1_parts", dve.tensor_copy(mp1[:, :, 0, :], mx1[:, 0, :, :]))
                            step(up, "max1_parts", dve.tensor_tensor(mx1[:, 1, :, :], mx1[:, 0, :, :], mp1[:, :, 0, :], ALU.subtract))
                            step(up, "max1_parts", dve.tensor_copy(mp1[:, :, 1, :], mx1[:, 1, :, :]))
                        if slot == maxima_slot(g) + MAX_TURN:
                            dve.wait_ge(sem["maxT1_made"], up("maxT1_made", g + 1))
                            if g >= 2:
                                dve.wait_ge(sem[f"max1_stored{g % 2}"], up(f"max1_stored{g % 2}", 16 * (g // 2)))
                            dve.tensor_copy(mT1[:, g % 2, :], bank(("maxT1", g)).bitcast(BF16)[0:2 * GH, 0:S]).then_inc(sem["maxT1_copied"], 1)
                        if slot == values_slot(g) + 2:
                            normalize(g)
                    if slot == ROUTE_AT - 1:
                        split_x(up_next)
                    if slot == TURN_Z + 1:
                        route_zone(up_next)
                    if slot == ROUTE_AT + 0:
                        route_distance(up_next)
                    if slot == ROUTE_AT + 2:
                        route_sum(up_next)
                    if slot == ROUTE_AT + 3:
                        route_nearest(up_next, 0)
                    if slot == ROUTE_AT + 4:
                        route_nearest(up_next, 1)
                    if slot == ROUTE_AT + 5:
                        route_fallback(up_next)
                    if slot == ROUTE_AT + 6:
                        route_choose(up_next)
                    if slot == ROUTE_AT + 7:
                        route_parts(up_next)
                turned_maxima0(up_next, 0)
                copy_weights(up_next)
                dve.wait_ge(sem["y1_turned"], up("y1_turned", 1))
                dve.tensor_tensor(yout[:, :, :], x1[:, :, :], bank("y1").rearrange("p (t d) -> p t d", t=NT), ALU.add)\
                    .then_inc(sem["out_ready"], 1)


SETUP_KEYS = 1
SETUP_FIRST = SETUP_KEYS + 5 + 8 + 11
SETUP_ALL = SETUP_FIRST + 7
CLEARED = 6


def kernel(**inputs):
    import numpy as _np
    import concourse.bacc as _bacc
    from concourse import mybir as _mybir
    from concourse.bass_utils import run_bass_kernel_spmd as _run

    arrays = layout(inputs)
    nc = _bacc.Bacc("TRN2", target_bir_lowering=False, num_devices=1)
    ins, feed = {}, {}
    for name, a in arrays.items():
        feed[f"in_{name}"] = a
        ins[name] = nc.dram_tensor(f"in_{name}", a.shape, _mybir.dt.from_np(a.dtype), kind="ExternalInput").ap()
    out = nc.dram_tensor("out", (BATCH, S, P), F32, kind="ExternalOutput").ap()
    build(nc, ins, out)
    r = _run(nc, [feed], core_ids=[0])
    return r.results[0]["out"]


def layout(inputs):
    g = {k: np.asarray(v) for k, v in inputs.items()}

    def rows(a):
        return np.ascontiguousarray(a.transpose(1, 0, 2).reshape(a.shape[1], -1))

    out = {"x": np.ascontiguousarray(np.concatenate([g["L0_attn_x"], g["L0_attn_x"][0:1]], 0))}
    wqkv = g["L0_attn_w_qkv"]
    inner = H * DH0
    out["wv"] = np.ascontiguousarray(wqkv[:, 2 * inner:])
    out["wqT"] = rows(np.ascontiguousarray(wqkv[:, 0:inner].T).reshape(H // 2, P, P))
    out["wkT"] = rows(np.ascontiguousarray(wqkv[:, inner:2 * inner].T).reshape(H // 2, P, P))
    out["gbc"] = np.ascontiguousarray(np.broadcast_to(g["L0_attn_gamma"][None, :], (P, P)))
    pmk = g["L0_attn_pm_k"].reshape(H * PM, DH0).T
    out["pmkT"] = np.ascontiguousarray(np.concatenate([pmk, pmk], 0))
    out["wo0"] = rows(g["L0_attn_w_out"].reshape(H // 2, P, P))
    pmv = np.zeros((H // 2, HH, PM, 2, DH0), np.float32)
    for h in range(H):
        pmv[h // 2, h % HH, :, h % 2, :] = g["L0_attn_pm_v"][h]
    out["pmv"] = rows(pmv.reshape(H // 2, P, P))
    for name, key in (("wg", "L0_ffn_Wg"), ("wu", "L0_ffn_Wu"), ("wd", "L0_ffn_Wd"), ("w1", "L1_ffn_W1"), ("w2", "L1_ffn_W2")):
        out[name] = rows(g[key])
    w = g["L1_attn_w_qkv"].reshape(P, 3, P // 2, 2)
    q, k = w[:, 0], w[:, 1]
    out["qk1"] = np.ascontiguousarray(np.concatenate([a.reshape(P, H, DH1).transpose(0, 2, 1).reshape(P, P)
                                                      for a in (q, q[:, :, ::-1], k, k[:, :, ::-1])], 1))
    col = [g["L0_attn_gamma"][:, None], np.zeros((P, 1), np.float32),
           np.broadcast_to(g["L0_ffn_temperature"][None, :], (P, 1)), np.zeros((P, 1), np.float32),
           np.where(np.arange(P)[:, None] % 4 < 2, 0.0, -1.0).astype(np.float32)]
    out["small"] = np.ascontiguousarray(np.concatenate(
        [w[:, 2].reshape(P, P), g["L1_attn_w_out"], np.eye(P, dtype=np.float32), g["L0_ffn_Wr"], g["L1_ffn_Wg"],
         np.broadcast_to(g["L1_ffn_bg"][None, :], (P, NE)), g["L1_ffn_b1"].T] + col, 1))
    out["b2"] = np.ascontiguousarray(g["L1_ffn_b2"])
    out["rank"] = np.tile(np.arange(NE, 0, -1, dtype=np.float32), (P, NT))
    r = np.arange(P)
    out["mask0"] = np.tile(np.where(np.arange(SEG)[None, :] > r[:, None] % SEG, MASKED, 0.0), (1, 1)).astype(np.float32)
    out["mask1"] = np.tile(np.where(r[None, :] > r[:, None], MASKED, 0.0), (1, NT)).astype(np.float32)
    out["selpm"] = np.where(np.arange(2 * HH)[:, None] % HH == r[None, :] // PM, -1.0, 0.0).astype(np.float32)
    out["selw"] = np.repeat(np.tile(np.eye(NE, dtype=np.float32), (3, 1)), P, 1)
    m = np.arange(32)
    out["esel"] = np.tile(np.concatenate([(m % 2 == c) for c in range(2)]).astype(np.float32), (P, 1))
    h8 = r // PM
    out["epm"] = np.concatenate([((h8[:, None] % 4 == j) & (h8[:, None] // 4 == m[None, :] % 2)) for j in range(4)], 1).astype(np.float32)
    selr = np.zeros((P, CH, 2, DH0), np.float32)
    for h in range(HH):
        for part in range(2):
            selr[32 * (h % 4) + h // 4 + 2 * part, h // 2, h % 2, :] = 1.0
    out["selr"] = selr.reshape(P, CH * P)
    inv = np.float32(1.0) / np.float32(10000.0) ** (np.arange(0, DH1, 2, dtype=np.float32) / np.float32(DH1))
    freqs = np.outer(np.arange(S, dtype=np.float32), inv).astype(np.float32)
    pair = (r // H) // 2
    out["cos"] = np.ascontiguousarray(np.cos(freqs).T[pair]).astype(np.float32)
    out["sin"] = np.ascontiguousarray(np.sin(freqs).T[pair] * np.where(r // H % 2 == 0, -1.0, 1.0)[:, None]).astype(np.float32)
    return out
```
